# Optimizing a Trainium2 kernel written in Bass

```python
import numpy as np
import jax
import jax.numpy as jnp

def _softmax(x, axis=-1):
    return jax.nn.softmax(x, axis=axis)

def _gelu(x):
    return jax.nn.gelu(x, approximate=True)

def _silu(x):
    return jax.nn.silu(x)

def _sigmoid(x):
    return jax.nn.sigmoid(x)

def _layernorm(x, axis=-1, eps=1e-05):
    m = jnp.mean(x, axis=axis, keepdims=True)
    v = jnp.var(x, axis=axis, keepdims=True)
    return (x - m) / jnp.sqrt(v + eps)

def _scatter_add(tgt, idx, src, axis=0):
    return tgt.at[idx].add(src)

def _segment_sum(src, seg, n):
    return jax.ops.segment_sum(src, seg, n)
kernel_name = 'mk_lm_tower_d1_tok_ids512_r4_ea201c'

def setup_inputs(seed: int=0):
    np.random.seed(seed)
    _w = jnp.asarray

    def _rec_inputs():
        import jax
        import jax.numpy as jnp
        _rk = jax.random.key(seed)
        x = jax.random.randint(jax.random.fold_in(_rk, 1), (8, 512), 0, 33, jnp.int32)
        return x
    x = _rec_inputs()

    def _L0_tok_setup():
        import jax, jax.numpy as jnp
        import numpy as np
        B, S, H, L, V, PAD = (32, 256, 128, 8, 33, 1)

        def layer_norm(x, g, b, eps):
            mu = jnp.mean(x, axis=-1, keepdims=True)
            var = jnp.mean(jnp.square(x - mu), axis=-1, keepdims=True)
            return (x - mu) * jax.lax.rsqrt(var + eps) * g + b

        def conv1d_same(x, w):
            return jax.lax.conv_general_dilated(x, w, window_strides=(1,), padding=[(1, 1)], dimension_numbers=('NWC', 'WIO', 'NWC'))
        key = jax.random.key(seed)
        ks = jax.random.split(key, 4)
        tokens = jax.random.randint(ks[0], (B, S), 0, V)
        emb = jax.random.normal(ks[1], (V, H), dtype=jnp.float32) * 0.02
        W1 = jax.random.normal(ks[2], (L, 3, H, H), dtype=jnp.float32) * (2.0 / (3 * H)) ** 0.5
        W2 = jax.random.normal(ks[3], (L, 3, H, H), dtype=jnp.float32) * (2.0 / (3 * H)) ** 0.5
        return {'tokens': tokens, 'emb': emb, 'ln0_g': jnp.ones((H,), jnp.float32), 'ln0_b': jnp.zeros((H,), jnp.float32), 'W1': W1, 'g1': jnp.ones((L, H), jnp.float32), 'b1': jnp.zeros((L, H), jnp.float32), 'W2': W2, 'g2': jnp.ones((L, H), jnp.float32), 'b2': jnp.zeros((L, H), jnp.float32)}
    _L0_tok_all = _L0_tok_setup()
    _L0_tok_in = {k: v for k, v in _L0_tok_all.items() if k in ('emb', 'ln0_g', 'ln0_b', 'W1', 'g1', 'b1', 'W2', 'g2', 'b2')}
    del _L0_tok_all

    def _L0_attn_setup():
        import jax, jax.numpy as jnp
        import numpy as np
        B, S, D = (2, 512, 128)
        H = 8
        G = 4
        LAMBDA_INIT = 0.2
        EPS = 1e-05
        key = jax.random.key(seed)
        ks = jax.random.split(key, 16)
        n = jax.random.normal
        return {'x': n(ks[0], (B, S, D), jnp.float32), 'K1_w': n(ks[1], (D, D), jnp.float32) * 0.02, 'K1_b': n(ks[2], (D,), jnp.float32) * 0.02, 'Q1_w': n(ks[3], (D, D), jnp.float32) * 0.02, 'K2_w': n(ks[4], (D, D), jnp.float32) * 0.02, 'K2_b': n(ks[5], (D,), jnp.float32) * 0.02, 'Q2_w': n(ks[6], (D, D), jnp.float32) * 0.02, 'V_w': n(ks[7], (D, D), jnp.float32) * 0.02, 'lambda_q1': n(ks[8], (H, 1), jnp.float32), 'lambda_k1': n(ks[9], (H, 1), jnp.float32), 'lambda_q2': n(ks[10], (H, 1), jnp.float32), 'lambda_k2': n(ks[11], (H, 1), jnp.float32), 'gn_w': jnp.ones((D,), jnp.float32), 'gn_b': jnp.zeros((D,), jnp.float32), 'out_w': n(ks[12], (D, D), jnp.float32) * 0.02, 'out_b': n(ks[13], (D,), jnp.float32) * 0.02}
    _L0_attn_all = _L0_attn_setup()
    _L0_attn_in = {k: v for k, v in _L0_attn_all.items() if k in ('K1_w', 'K1_b', 'Q1_w', 'K2_w', 'K2_b', 'Q2_w', 'V_w', 'lambda_q1', 'lambda_k1', 'lambda_q2', 'lambda_k2', 'gn_w', 'gn_b', 'out_w', 'out_b')}
    del _L0_attn_all

    def _L0_ffn_setup():
        import jax, jax.numpy as jnp
        import numpy as np
        TOP_K = 6
        CAP_FACTOR = 2.0
        key = jax.random.key(seed)
        ks = jax.random.split(key, 9)
        B, S, D, F, E, SH = (4, 512, 128, 64, 64, 2)
        return {'x': jax.random.normal(ks[0], (B, S, D), jnp.float32), 'router_w': jax.random.normal(ks[1], (E, D), jnp.float32) * 0.02, 'bias': jnp.zeros((E,), jnp.float32), 'shared_w_gate': jax.random.normal(ks[2], (SH, F, D), jnp.float32) * 0.02, 'shared_w_up': jax.random.normal(ks[3], (SH, F, D), jnp.float32) * 0.02, 'shared_w_down': jax.random.normal(ks[4], (SH, D, F), jnp.float32) * 0.02, 'w_gate': jax.random.normal(ks[5], (E, F, D), jnp.float32) * 0.02, 'w_up': jax.random.normal(ks[6], (E, F, D), jnp.float32) * 0.02, 'w_down': jax.random.normal(ks[7], (E, D, F), jnp.float32) * 0.02}
    _L0_ffn_all = _L0_ffn_setup()
    _L0_ffn_in = {k: v for k, v in _L0_ffn_all.items() if k in ('router_w', 'bias', 'shared_w_gate', 'shared_w_up', 'shared_w_down', 'w_gate', 'w_up', 'w_down')}
    del _L0_ffn_all
    return {'x': x, 'L0_tok_emb': _L0_tok_in['emb'], 'L0_tok_ln0_g': _L0_tok_in['ln0_g'], 'L0_tok_ln0_b': _L0_tok_in['ln0_b'], 'L0_tok_W1': _L0_tok_in['W1'], 'L0_tok_g1': _L0_tok_in['g1'], 'L0_tok_b1': _L0_tok_in['b1'], 'L0_tok_W2': _L0_tok_in['W2'], 'L0_tok_g2': _L0_tok_in['g2'], 'L0_tok_b2': _L0_tok_in['b2'], 'L0_attn_K1_w': _L0_attn_in['K1_w'], 'L0_attn_K1_b': _L0_attn_in['K1_b'], 'L0_attn_Q1_w': _L0_attn_in['Q1_w'], 'L0_attn_K2_w': _L0_attn_in['K2_w'], 'L0_attn_K2_b': _L0_attn_in['K2_b'], 'L0_attn_Q2_w': _L0_attn_in['Q2_w'], 'L0_attn_V_w': _L0_attn_in['V_w'], 'L0_attn_lambda_q1': _L0_attn_in['lambda_q1'], 'L0_attn_lambda_k1': _L0_attn_in['lambda_k1'], 'L0_attn_lambda_q2': _L0_attn_in['lambda_q2'], 'L0_attn_lambda_k2': _L0_attn_in['lambda_k2'], 'L0_attn_gn_w': _L0_attn_in['gn_w'], 'L0_attn_gn_b': _L0_attn_in['gn_b'], 'L0_attn_out_w': _L0_attn_in['out_w'], 'L0_attn_out_b': _L0_attn_in['out_b'], 'L0_ffn_router_w': _L0_ffn_in['router_w'], 'L0_ffn_bias': _L0_ffn_in['bias'], 'L0_ffn_shared_w_gate': _L0_ffn_in['shared_w_gate'], 'L0_ffn_shared_w_up': _L0_ffn_in['shared_w_up'], 'L0_ffn_shared_w_down': _L0_ffn_in['shared_w_down'], 'L0_ffn_w_gate': _L0_ffn_in['w_gate'], 'L0_ffn_w_up': _L0_ffn_in['w_up'], 'L0_ffn_w_down': _L0_ffn_in['w_down']}

def reference(x, L0_tok_emb, L0_tok_ln0_g, L0_tok_ln0_b, L0_tok_W1, L0_tok_g1, L0_tok_b1, L0_tok_W2, L0_tok_g2, L0_tok_b2, L0_attn_K1_w, L0_attn_K1_b, L0_attn_Q1_w, L0_attn_K2_w, L0_attn_K2_b, L0_attn_Q2_w, L0_attn_V_w, L0_attn_lambda_q1, L0_attn_lambda_k1, L0_attn_lambda_q2, L0_attn_lambda_k2, L0_attn_gn_w, L0_attn_gn_b, L0_attn_out_w, L0_attn_out_b, L0_ffn_router_w, L0_ffn_bias, L0_ffn_shared_w_gate, L0_ffn_shared_w_up, L0_ffn_shared_w_down, L0_ffn_w_gate, L0_ffn_w_up, L0_ffn_w_down):
    import jax
    import jax.numpy as jnp

    def _L0_tok_ref(tokens, emb, ln0_g, ln0_b, W1, g1, b1, W2, g2, b2):
        import jax, jax.numpy as jnp
        import numpy as np
        B, S, H, L, V, PAD = (32, 256, 128, 8, 33, 1)

        def layer_norm(x, g, b, eps):
            mu = jnp.mean(x, axis=-1, keepdims=True)
            var = jnp.mean(jnp.square(x - mu), axis=-1, keepdims=True)
            return (x - mu) * jax.lax.rsqrt(var + eps) * g + b

        def conv1d_same(x, w):
            return jax.lax.conv_general_dilated(x, w, window_strides=(1,), padding=[(1, 1)], dimension_numbers=('NWC', 'WIO', 'NWC'))
        dt = emb.dtype
        pad = tokens == PAD
        x = emb[tokens]
        s = x.shape[1]
        pos = jnp.arange(s - 1, -1, -1, dtype=dt)
        inv_freq = 1.0 / 10000.0 ** (jnp.arange(0.0, H, 2.0, dtype=dt) / H)
        sin_in = pos[:, None] * inv_freq[None, :]
        pe = jnp.concatenate([jnp.sin(sin_in), jnp.cos(sin_in)], axis=-1)
        x = x + pe[None]
        x = layer_norm(x, ln0_g, ln0_b, 1e-12)
        x = x * (1.0 - pad[..., None].astype(dt))
        for i in range(W1.shape[0]):
            r = x
            h = conv1d_same(x, W1[i])
            h = layer_norm(h, g1[i], b1[i], 1e-05)
            h = jax.nn.relu(h)
            h = conv1d_same(h, W2[i])
            h = layer_norm(h, g2[i], b2[i], 1e-05)
            x = h + r
        return x

    def _L0_attn_ref(x, K1_w, K1_b, Q1_w, K2_w, K2_b, Q2_w, V_w, lambda_q1, lambda_k1, lambda_q2, lambda_k2, gn_w, gn_b, out_w, out_b):
        import jax, jax.numpy as jnp
        import numpy as np
        B, S, D = (2, 512, 128)
        H = 8
        G = 4
        LAMBDA_INIT = 0.2
        EPS = 1e-05
        b, s, d = x.shape
        hd = d // H

        def heads(t):
            return t.reshape(b, s, H, hd).transpose(0, 2, 1, 3)
        q1 = heads(x @ Q1_w.T)
        k1 = heads(x @ K1_w.T + K1_b)
        q2 = heads(x @ Q2_w.T)
        k2 = heads(x @ K2_w.T + K2_b)
        v = heads(x @ V_w.T)
        scale = hd ** 0.5
        a1 = jax.nn.softmax(jnp.einsum('bhqd,bhkd->bhqk', q1, k1) / scale, axis=-1)
        a2 = jax.nn.softmax(jnp.einsum('bhqd,bhkd->bhqk', q2, k2) / scale, axis=-1)
        lam = jnp.exp(lambda_q1 * lambda_k1) - jnp.exp(lambda_q2 * lambda_k2) + LAMBDA_INIT
        attn = a1 - lam.reshape(1, H, 1, 1) * a2
        o = jnp.einsum('bhqk,bhkd->bhqd', attn, v)
        o = o.transpose(0, 2, 1, 3).reshape(b, s, d)
        xc = o.transpose(0, 2, 1).reshape(b, G, d // G, s)
        mu = xc.mean(axis=(2, 3), keepdims=True)
        var = xc.var(axis=(2, 3), keepdims=True)
        xn = ((xc - mu) * jax.lax.rsqrt(var + EPS)).reshape(b, d, s)
        xn = xn * gn_w[None, :, None] + gn_b[None, :, None]
        y = xn.transpose(0, 2, 1) @ out_w.T + out_b
        return y

    def _L0_ffn_ref(x, router_w, bias, shared_w_gate, shared_w_up, shared_w_down, w_gate, w_up, w_down):
        import jax, jax.numpy as jnp
        import numpy as np
        TOP_K = 6
        CAP_FACTOR = 2.0
        B, S, D = x.shape
        E = router_w.shape[0]
        K = TOP_K
        N = B * S
        C = max(1, int(N * K * CAP_FACTOR / E))
        router_logits = jnp.einsum('bsd,ed->bse', x, router_w) + bias
        hg = jnp.einsum('bsd,efd->bsef', x, shared_w_gate)
        hu = jnp.einsum('bsd,efd->bsef', x, shared_w_up)
        shared_out = jnp.einsum('bsef,edf->bsd', jax.nn.silu(hg) * hu, shared_w_down)
        shared_out = shared_out / shared_w_gate.shape[0]
        router_probs = jax.nn.softmax(router_logits, axis=-1)
        topk_p, topk_i = jax.lax.top_k(router_probs, K)
        topk_p = topk_p / (jnp.sum(topk_p, axis=-1, keepdims=True) + 1e-09)
        x_flat = x.reshape(N, D)
        flat_e = topk_i.reshape(-1)
        flat_g = topk_p.reshape(-1)
        token_ids = jnp.repeat(jnp.arange(N), K)
        order = jnp.argsort(flat_e)
        se = flat_e[order]
        st = token_ids[order]
        sg = flat_g[order]
        M = se.shape[0]
        pos = jnp.arange(M)
        is_first = jnp.concatenate([jnp.ones((1,), bool), se[1:] != se[:-1]])
        group_starts = jax.lax.cummax(pos * is_first.astype(pos.dtype))
        slot = pos - group_starts
        valid = slot < C
        safe_slot = jnp.where(valid, slot, C)
        expert_in = jnp.zeros((E, C + 1, D), x.dtype).at[se, safe_slot].set(x_flat[st])
        expert_gate = jnp.zeros((E, C + 1), x.dtype).at[se, safe_slot].set(sg)
        expert_tok = jnp.full((E, C + 1), N, jnp.int32).at[se, safe_slot].set(st.astype(jnp.int32))
        expert_mask = jnp.zeros((E, C + 1), bool).at[se, safe_slot].set(valid)
        expert_in = expert_in[:, :C]
        expert_gate = expert_gate[:, :C]
        expert_tok = expert_tok[:, :C]
        expert_mask = expert_mask[:, :C]
        hg = jnp.einsum('ecd,efd->ecf', expert_in, w_gate)
        hu = jnp.einsum('ecd,efd->ecf', expert_in, w_up)
        expert_out = jnp.einsum('ecf,edf->ecd', jax.nn.silu(hg) * hu, w_down)
        fm = expert_mask.reshape(-1)
        dst = jnp.where(fm, expert_tok.reshape(-1), N)
        fg = jnp.where(fm, expert_gate.reshape(-1), jnp.zeros((), x.dtype))
        sparse = jax.ops.segment_sum(fg[:, None] * expert_out.reshape(-1, D), dst, num_segments=N + 1)[:N]
        return shared_out + sparse.reshape(B, S, D)
    h = _L0_tok_ref(x, L0_tok_emb, L0_tok_ln0_g, L0_tok_ln0_b, L0_tok_W1, L0_tok_g1, L0_tok_b1, L0_tok_W2, L0_tok_g2, L0_tok_b2)
    h = h + _L0_attn_ref(_layernorm(h, axis=-1), L0_attn_K1_w, L0_attn_K1_b, L0_attn_Q1_w, L0_attn_K2_w, L0_attn_K2_b, L0_attn_Q2_w, L0_attn_V_w, L0_attn_lambda_q1, L0_attn_lambda_k1, L0_attn_lambda_q2, L0_attn_lambda_k2, L0_attn_gn_w, L0_attn_gn_b, L0_attn_out_w, L0_attn_out_b)
    h = h + _L0_ffn_ref(_layernorm(h, axis=-1), L0_ffn_router_w, L0_ffn_bias, L0_ffn_shared_w_gate, L0_ffn_shared_w_up, L0_ffn_shared_w_down, L0_ffn_w_gate, L0_ffn_w_up, L0_ffn_w_down)
    return h

_drawn_inputs = setup_inputs


def setup_inputs(seed=0):
    import zlib

    import numpy as np

    out = dict(_drawn_inputs(seed))
    spreads = {'L0_tok_ln0_g': (1.0, 0.2),
     'L0_tok_ln0_b': (0.0, 0.1),
     'L0_tok_g1': (1.0, 0.2),
     'L0_tok_b1': (0.0, 0.1),
     'L0_tok_g2': (1.0, 0.2),
     'L0_tok_b2': (0.0, 0.1),
     'L0_attn_gn_w': (1.0, 0.6),
     'L0_attn_gn_b': (0.0, 0.8),
     'L0_ffn_bias': (0.0, 0.8)}
    factors = {'L0_attn_K1_w': 8.0,
     'L0_attn_K1_b': 8.0,
     'L0_attn_Q1_w': 8.0,
     'L0_attn_K2_w': 8.0,
     'L0_attn_K2_b': 8.0,
     'L0_attn_Q2_w': 8.0,
     'L0_attn_lambda_q2': 6.182,
     'L0_attn_out_b': 8.0,
     'L0_ffn_router_w': 8.0,
     'L0_ffn_shared_w_gate': 8.0,
     'L0_ffn_shared_w_up': 8.0,
     'L0_ffn_shared_w_down': 8.0,
     'L0_ffn_w_gate': 8.0,
     'L0_ffn_w_up': 8.0,
     'L0_ffn_w_down': 8.0}
    for name, (base, spread) in spreads.items():
        noise = np.random.default_rng([zlib.crc32(name.encode()), seed]).standard_normal(out[name].shape)
        drawn = base * np.exp(spread * noise) if base else spread * noise
        out[name] = jnp.asarray(drawn.astype(out[name].dtype))
    for name, factor in factors.items():
        out[name] = (out[name] * factor).astype(out[name].dtype)
    return out
```

```python
from contextlib import ExitStack

import numpy as np

import concourse.bass as bass
from concourse import mybir

F32 = mybir.dt.float32
BF16 = mybir.dt.bfloat16
I32 = mybir.dt.int32
ALU = mybir.AluOpType
ACT = mybir.ActivationFunctionType
AX = mybir.AxisListType

P = 128
B, S, D = 8, 512, 128
QT = S // P
LAYERS, TAPS, VOCAB, PAD = 8, 3, 33, 1
CONVS = 2 * B
E, TOPK, CAP = 64, 6, 768
ROW = D + E
ZROWS = 8
LAG = 3
RING = 4


def tower(nc, io, X, rows_x):
    with ExitStack() as ctx:
        def sb(name, shape, dt=F32):
            return ctx.enter_context(nc.sbuf_tensor(name, shape, dt))

        def sem(name):
            return ctx.enter_context(nc.semaphore(name))

        H = sb("hidden", [P, B, S + 2])
        W = sb("conv_w", [P, LAYERS, 2, TAPS, D])
        wmean = sb("wmean", [P, 2 * TAPS])
        gb = sb("gb", [P, 4, LAYERS])
        gb0 = sb("gb0", [P, 2])
        eps = sb("eps_tower", [P, 2])
        tok = sb("tok", [P, B, S], I32)
        onehot = sb("onehot", [P, 2, S])
        mask = sb("mask", [P, 2, S])
        emb = sb("emb", [P, D])
        pe = sb("pe", [P, QT, D])
        zrow = sb("zrow", [P, ZROWS * ROW])
        ident = sb("ident_t", [P, P])
        iota = sb("iota_t", [P, 1])
        sq = sb("sq", [P, 2, S])
        z = sb("z_tower", [P, RING, QT, D])
        sumsq = sb("sumsq", [P, RING, QT])
        std = sb("std", [P, RING, QT])
        rstd = sb("rstd", [P, RING, QT])
        stats = sb("stats", [P, QT, 6])
        mv = sb("mv", [P, 2, QT, 2])
        ps_y = [ctx.enter_context(nc.psum_tensor(f"y{n}", [P, QT, D], F32)) for n in range(RING)]
        ps_t = [ctx.enter_context(nc.psum_tensor(f"t{n}", [P, S], F32)) for n in range(RING)]

        zeros_ready = sem("zeros_ready")
        zeros_written = sem("zeros_written")
        consts_in = sem("consts_in")
        tokens_in = sem("tokens_in")
        weights_in = [sem(f"weights_in{n}") for n in range(LAYERS)]
        emb_zero = sem("emb_zero")
        emb_in = sem("emb_in")
        edges_zero = sem("edges_zero")
        onehot_ready = sem("onehot_ready")
        embedded = sem("embedded")
        stats_ready = sem("stats_ready")
        var_ready = sem("var_ready")
        std0_ready = sem("std0_ready")
        rstd0_ready = sem("rstd0_ready")
        z0_ready = sem("z0_ready")
        turned0 = sem("turned0")
        scaled0 = sem("scaled0")
        mask_ready = sem("mask_ready")
        wsum_ready = sem("wsum_ready")
        w_ready = sem("w_ready")
        conv_done = sem("conv_done")
        sq_ready = sem("sq_ready")
        sumsq_ready = sem("sumsq_ready")
        std_ready = sem("std_ready")
        rstd_ready = sem("rstd_ready")
        z_ready = sem("z_ready")
        turned = sem("turned")
        hidden_ready = sem("hidden_ready")
        x_ready = sem("x_ready")
        bias_added = sem("bias_added")

        sp_passed, pool_passed, act_passed = sem("sp_passed1"), sem("pool_passed1"), sem("act_passed1")
        block = ctx.enter_context(nc.Block())

        @block.sync
        def _(sp):
            sp.dma_start(tok[:], io["x"].unsqueeze(0).to_broadcast([P, B, S])).then_inc(tokens_in, 16)
            sp.dma_start(iota[:], io["iota"]).then_inc(consts_in, 16)
            sp.dma_start(ident[:], io["ident"]).then_inc(consts_in, 16)
            sp.dma_start(pe[:], io["pe"].rearrange("(q p) d -> p q d", p=P)).then_inc(consts_in, 16)
            sp.dma_start(gb0[:, 0:1], io["L0_tok_ln0_g"].unsqueeze(1)).then_inc(consts_in, 16)
            sp.dma_start(gb0[:, 1:2], io["L0_tok_ln0_b"].unsqueeze(1)).then_inc(consts_in, 16)
            for n, name in enumerate(("g1", "b1", "g2", "b2")):
                sp.dma_start(gb[:, n, :], io["L0_tok_" + name]).then_inc(consts_in, 16)
            sp.wait_ge(emb_zero, 1).then_inc(sp_passed, 1)
            sp.dma_start(emb[0:VOCAB, :], io["L0_tok_emb"]).then_inc(emb_in, 16)
            for layer in range(LAYERS):
                for c, name in enumerate(("W1", "W2")):
                    sp.dma_start(W[:, layer, c], io["L0_tok_" + name][layer].rearrange("t i o -> i t o")
                                 ).then_inc(weights_in[layer], 16)
            sp.wait_ge(zeros_ready, 1).then_inc(sp_passed, 1)
            filled = rows_x.rearrange("(a p r) c -> a p (r c)", p=P, r=ZROWS)
            with sp.Fori(0, E * CAP // (P * ZROWS)) as i:
                sp.dma_start(filled[i], zrow[:]).then_inc(zeros_written, 16)
            sp.wait_ge(zeros_written, 16 * (E * CAP // (P * ZROWS))).then_inc(sp_passed, 1)

        @block.gpsimd
        def _(pool):
            pool.memset(zrow[:], 0.0).then_inc(zeros_ready, 1)
            pool.memset(emb[:], 0.0).then_inc(emb_zero, 1)
            for buf in (X, H):
                for col in (0, S + 1):
                    pool.memset(buf[:, :, col:col + 1], 0.0).then_inc(edges_zero, 1)
            pool.memset(eps[:, 0:1], 1e-12).then_inc(edges_zero, 1)
            pool.memset(eps[:, 1:2], 1e-5).then_inc(edges_zero, 1)
            pool.wait_ge(consts_in, 16 * 9).then_inc(pool_passed, 1)
            with pool.Fori(0, LAYERS) as layer:
                for s in range(B):
                    pool.wait_ge(conv_done, layer * CONVS + s + 1).then_inc(pool_passed, 1)
                    pool.tensor_tensor(X[:, s, 1:S + 1], X[:, s, 1:S + 1],
                                       gb[:, 3, bass.ds(layer, 1)].to_broadcast([P, S]), ALU.add
                                       ).then_inc(bias_added, 1)

        @block.tensor
        def _(pe_):
            def transposes(s, src, dst, inc):
                for q in range(QT):
                    last = pe_.transpose(dst[:, q * P:(q + 1) * P], src[:, q, :], ident[:])
                last.then_inc(inc, 1)

            pe_.wait_ge(consts_in, 16 * 9)
            pe_.wait_ge(emb_in, 16)
            for s in range(B + 2):
                if s < B:
                    pe_.wait_ge(onehot_ready, s + 1)
                    if s >= RING:
                        pe_.wait_ge(z0_ready, s - RING + 1)
                    for q in range(QT):
                        pe_.matmul(ps_y[s % RING][:, q, :], onehot[:, s % 2, q * P:(q + 1) * P], emb[:],
                                   start=True, stop=False)
                        last = pe_.matmul(ps_y[s % RING][:, q, :], ident[:], pe[:, q, :],
                                          start=False, stop=True)
                    last.then_inc(embedded, 1)
                if s >= 2:
                    pe_.wait_ge(z0_ready, s - 1)
                    if s - 2 >= RING:
                        pe_.wait_ge(scaled0, s - 2 - RING + 1)
                    transposes(s - 2, z[:, (s - 2) % RING], ps_t[(s - 2) % RING], turned0)

            def conv(layer, c):
                n, s = c // B, c % B
                at = layer * CONVS + c
                src = H if n else X
                if n:
                    pe_.wait_ge(hidden_ready, layer * B + s + 1)
                else:
                    pe_.wait_ge(x_ready, layer * B + s + 1)
                    if s == 0:
                        pe_.wait_ge(w_ready, layer + 1)
                if isinstance(at, int) and at < RING:
                    pe_.wait_ge(z0_ready, B)
                else:
                    pe_.wait_ge(z_ready, at - RING + 1)
                for q in range(QT):
                    for t in range(TAPS):
                        last = pe_.matmul(ps_y[c % RING][:, q, :], src[:, s, q * P + t:q * P + t + P],
                                          W[:, layer, n, t, :], start=(t == 0), stop=(t == TAPS - 1))
                last.then_inc(conv_done, 1)

            def turn(layer, k, first=False):
                pe_.wait_ge(z_ready, layer * CONVS + k + 1)
                j = k - RING
                if j >= B:
                    pe_.wait_ge(x_ready, B + layer * B + j - B + 1)
                elif j >= 0:
                    pe_.wait_ge(hidden_ready, layer * B + j + 1)
                else:
                    pe_.wait_ge(x_ready, layer * B + B + j + 1)
                transposes(k % B, z[:, k % RING], ps_t[k % RING], turned)

            for c in range(LAG):
                conv(0, c)

            def body(layer, last):
                for k in range(CONVS):
                    turn(layer, k)
                    c = k + LAG
                    if c < CONVS:
                        conv(layer, c)
                    elif not last:
                        conv(layer + 1, c - CONVS)

            body(0, False)
            with pe_.Fori(1, LAYERS - 1) as layer:
                body(layer, False)
            body(LAYERS - 1, True)

        @block.scalar
        def _(act):
            act.wait_ge(consts_in, 16 * 9)
            act.wait_ge(edges_zero, 6)
            for s in range(B + 2):
                if s < B:
                    act.wait_ge(var_ready, s + 1)
                    act.activation(std[:, s % RING, :], mv[:, s % 2, :, 1], ACT.Sqrt, bias=eps[:, 0:1]
                                   ).then_inc(std0_ready, 1)
                if s >= 2:
                    act.wait_ge(turned0, s - 1)
                    act.activation(X[:, s - 2, 1:S + 1], ps_t[(s - 2) % RING][:], ACT.Identity,
                                   scale=gb0[:, 0:1], bias=gb0[:, 1:2]).then_inc(scaled0, 1)

            def square(layer, c):
                at = layer * CONVS + c
                act.wait_ge(conv_done, at + 1)
                if not (isinstance(at, int) and at < 2):
                    act.wait_ge(sumsq_ready, at - 1)
                act.activation(sq[:, c % 2, :], ps_y[c % RING][:].rearrange("p q d -> p (q d)"), ACT.Square
                               ).then_inc(sq_ready, 1)

            def root(layer, c):
                act.wait_ge(sumsq_ready, layer * CONVS + c + 1)
                act.activation(std[:, c % RING, :], sumsq[:, c % RING, :], ACT.Sqrt, scale=1.0 / D,
                               bias=eps[:, 1:2]).then_inc(std_ready, 1)

            square(0, 0)
            root(0, 0)
            square(0, 1)
            root(0, 1)
            square(0, 2)

            def body(layer, last):
                for k in range(CONVS):
                    c = k + LAG - 1
                    if c < CONVS:
                        root(layer, c)
                    elif not last:
                        root(layer + 1, c - CONVS)
                    if k < B:
                        act.wait_ge(turned, layer * CONVS + k + 1).then_inc(act_passed, 1)
                        act.activation(H[:, k, 1:S + 1], ps_t[k % RING][:], ACT.Relu,
                                       scale=gb[:, 0, bass.ds(layer, 1)], bias=gb[:, 1, bass.ds(layer, 1)]
                                       ).then_inc(hidden_ready, 1)
                    c = k + LAG
                    if c < CONVS:
                        square(layer, c)
                    elif not last:
                        square(layer + 1, c - CONVS)

            body(0, False)
            with act.Fori(1, LAYERS - 1) as layer:
                body(layer, False)
            body(LAYERS - 1, True)

        @block.vector
        def _(dve):
            dve.wait_ge(tokens_in, 16)
            dve.wait_ge(consts_in, 16 * 9)

            def masked(s):
                dve.wait_ge(scaled0, s + 1)
                dve.tensor_tensor(X[:, s, 1:S + 1], X[:, s, 1:S + 1], mask[:, s % 2, :], ALU.mult
                                  ).then_inc(x_ready, 1)

            for s in range(B + 3):
                if s < B:
                    if s >= 2:
                        dve.wait_ge(embedded, s - 1)
                    dve.tensor_scalar(onehot[:, s % 2, :], tok[:, s, :], iota[:, 0:1], None, ALU.is_equal
                                      ).then_inc(onehot_ready, 1)
                if 1 <= s <= B:
                    q_s = s - 1
                    dve.wait_ge(embedded, q_s + 1)
                    for q in range(QT):
                        dve.bn_stats(stats[:, q, :], ps_y[q_s % RING][:, q, :]).then_inc(stats_ready, 1)
                    dve.wait_ge(stats_ready, QT * (q_s + 1))
                    for q in range(QT):
                        last = dve.bn_aggr(mv[:, q_s % 2, q, :], stats[:, q, :])
                    last.then_inc(var_ready, 1)
                    dve.wait_ge(std0_ready, q_s + 1)
                    dve.reciprocal(rstd[:, q_s % RING, :], std[:, q_s % RING, :]).then_inc(rstd0_ready, 1)
                    dve.wait_ge(rstd0_ready, q_s + 1)
                    if q_s >= RING:
                        dve.wait_ge(turned0, q_s - RING + 1)
                    for q in range(QT):
                        last = dve.tensor_scalar(z[:, q_s % RING, q, :], ps_y[q_s % RING][:, q, :],
                                                 mv[:, q_s % 2, q, 0:1], rstd[:, q_s % RING, q:q + 1],
                                                 ALU.subtract, ALU.mult)
                    last.then_inc(z0_ready, 1)
                if s >= 3:
                    m = s - 3
                    dve.tensor_scalar(mask[:, m % 2, :], tok[:, m, :], float(PAD), None, ALU.not_equal
                                      ).then_inc(mask_ready, 1)
                    dve.wait_ge(mask_ready, m + 1)
                    masked(m)

            def centre(layer):
                w = W[:, layer].rearrange("p c t o -> p (c t) o")
                dve.tensor_reduce(wmean[:], w, AX.X, ALU.add).then_inc(wsum_ready, 1)
                dve.wait_ge(wsum_ready, layer * 2 + 1)
                dve.tensor_scalar(wmean[:], wmean[:], -1.0 / D, None, ALU.mult).then_inc(wsum_ready, 1)
                dve.wait_ge(wsum_ready, layer * 2 + 2)
                dve.tensor_tensor(w, w, wmean[:].unsqueeze(2).to_broadcast([P, 2 * TAPS, D]), ALU.add
                                  ).then_inc(w_ready, 1)

            def sums(layer, c):
                dve.wait_ge(sq_ready, layer * CONVS + c + 1)
                dve.tensor_reduce(sumsq[:, c % RING, :], sq[:, c % 2, :].rearrange("p (q d) -> p q d", q=QT),
                                  AX.X, ALU.add).then_inc(sumsq_ready, 1)

            def normalise(layer, c):
                at = layer * CONVS + c
                dve.wait_ge(std_ready, at + 1)
                dve.reciprocal(rstd[:, c % RING, :], std[:, c % RING, :]).then_inc(rstd_ready, 1)
                dve.wait_ge(rstd_ready, at + 1)
                if isinstance(at, int) and at < RING:
                    dve.wait_ge(turned0, B)
                else:
                    dve.wait_ge(turned, at - RING + 1)
                dve.tensor_tensor(z[:, c % RING], ps_y[c % RING][:],
                                  rstd[:, c % RING, :].unsqueeze(2).to_broadcast([P, QT, D]), ALU.mult
                                  ).then_inc(z_ready, 1)

            dve.wait_ge(weights_in[0], 32)
            centre(0)
            for n in range(1, LAYERS):
                dve.wait_ge(weights_in[n], 32)
            sums(0, 0)
            normalise(0, 0)
            sums(0, 1)
            normalise(0, 1)
            sums(0, 2)

            def body(layer, last):
                for k in range(CONVS):
                    c = k + LAG - 1
                    if c < CONVS:
                        normalise(layer, c)
                    elif not last:
                        normalise(layer + 1, c - CONVS)
                    if k >= B:
                        s = k - B
                        dve.wait_ge(turned, layer * CONVS + k + 1)
                        dve.wait_ge(bias_added, layer * B + s + 1)
                        dve.scalar_tensor_tensor(out=X[:, s, 1:S + 1], in0=ps_t[k % RING][:],
                                                 scalar=gb[:, 2, bass.ds(layer, 1)], in1=X[:, s, 1:S + 1],
                                                 op0=ALU.mult, op1=ALU.add).then_inc(x_ready, 1)
                    c = k + LAG
                    if c < CONVS:
                        sums(layer, c)
                    elif not last:
                        sums(layer + 1, c - CONVS)
                    if k == 4 and not last:
                        centre(layer + 1)

            body(0, False)
            with dve.Fori(1, LAYERS - 1) as layer:
                body(layer, False)
            body(LAYERS - 1, True)
HEADS, HD = 8, 16
MAPS = 2
GROUPS = 4
UNITS = 16
TERMS = 6
Q_PART = (0, 0, 1, 1, 0, 2)
K_PART = (0, 1, 0, 1, 2, 0)
KT = TERMS * HD
KM = KT + 3
NR = 14
FAR = float(1 << 17)


def attention(nc, io, X, H2, Z2, slots, dram):
    with ExitStack() as ctx:
        def sb(name, shape, dt=F32):
            return ctx.enter_context(nc.sbuf_tensor(name, shape, dt))

        def sem(name):
            return ctx.enter_context(nc.semaphore(name))

        def bank(name, shape=(P, S)):
            return ctx.enter_context(nc.psum_tensor(name, list(shape), F32))

        ident = sb("ident", [P, P])
        wproj = sb("wproj", [P, 4, D])
        kbias = sb("kbias", [P, 4])
        wv = sb("wv", [P, D])
        wout = sb("wout", [P, D])
        outb = sb("outb", [P, D])
        gnw = sb("gnw", [P, 2])
        grp = sb("grp", [P, P])
        wrout = sb("wrout", [P, E])
        rbias = sb("rbias", [P, E])
        base1 = sb("base1", [P, E])
        tri_f = sb("tri_f", [P, P])
        tri = sb("tri", [P, P], BF16)
        ones = sb("ones", [P, P], BF16)
        lam = sb("lam", [P, 4, HEADS])
        neglam = sb("neglam", [P, HEADS])
        half = sb("half", [P, QT])
        hc = sb("hc", [P, S])
        htok = sb("htok", [P, QT, D])
        ztok = sb("ztok", [P, QT, D])
        zT = sb("zT", [P, S])
        fstats = sb("fstats", [P, QT, 6])
        fmv = sb("fmv", [P, QT, 2])
        fve = sb("fve", [P, QT])
        frstd = sb("frstd", [P, QT])
        q32 = sb("q32", [P, S])
        rest = sb("rest", [P, S])
        parts = sb("parts", [P, 2, 3, S], BF16)
        stack = [[sb(f"stack{p}{j}", [P, HEADS, S], BF16) for j in range(4)] for p in range(2)]
        Vx = [sb(f"Vx{p}", [P, QT, HEADS, 32]) for p in range(2)]
        nm = sb("nm", [P, 2, UNITS])
        mp = sb("mp", [UNITS, 3, P], BF16)
        mrest = sb("mrest", [UNITS, P])
        ex = sb("ex", [P, 8, S])
        OT = sb("OT", [P, S])
        rsum = sb("rsum", [P, QT, 4])
        on = sb("on", [P, QT, 4, HD])
        otok = sb("otok", [P, QT, HEADS, HD])
        gst = sb("gst", [P, 6])
        gmv = sb("gmv", [P, 2])
        gm = sb("gm", [P, 1])
        gd = sb("gd", [P, 1])
        gv = sb("gv", [P, 1])
        gvar = sb("gvar", [P, 1])
        gve = sb("gve", [P, 1])
        grs = sb("grs", [P, 1])
        gsc = sb("gsc", [P, 1])
        gbi = sb("gbi", [P, 1])
        xn = sb("xn", [P, S])
        h2c = sb("h2c", [P, QT, D])
        tstats = sb("tstats", [P, QT, 6])
        tmv = sb("tmv", [P, QT, 2])
        tve = sb("tve", [P, QT])
        trstd = sb("trstd", [P, QT])
        R = sb("R", [P, QT, ROW])
        z2c = sb("z2c", [P, S])
        logit = sb("logit", [P, QT, E])
        lmax = sb("lmax", [P, QT])
        lsum = sb("lsum", [P, QT])
        lrec = sb("lrec", [P, QT])
        prob = sb("prob", [P, QT, E + 2])
        top = sb("top", [P, QT, 8])
        repl = sb("repl", [P, QT, E + 2])
        M = sb("M", [P, QT, E], BF16)
        Macc = sb("Macc", [P, E], BF16)
        mnew = sb("mnew", [P, E])
        gsum = sb("gsum", [P, QT])
        grec = sb("grec", [P, QT])
        Mv = sb("Mv", [P, QT, E])
        gate = sb("gate", [P, QT, E])
        slot1 = sb("slot1", [P, QT, E])
        v8 = sb("v8", [P, QT, 8])
        none = sb("none", [P, QT, 8])
        freed = sb("freed", [P, 1])
        sidx = sb("sidx", [P, QT, 8], I32)

        ps_m = [bank(f"ps_m{i}") for i in range(2)]
        ps_e = [bank(f"ps_e{i}") for i in range(2)]
        ps_o = bank("ps_o")
        psA, psB, psC = bank("psA"), bank("psB"), bank("psC")

        names = """consts_in lam_ready consts_ready ones_rows vones hc_ready f_turned htok_ready f_stats
            f_var f_eps f_rstd resid_ready ztok_ready z_turned zT_ready proj_done hi_ready rest_ready
            mid_ready parts_ready v_done v_ready mxmm_done max_ready nm_turned mp_chain rows_ready
            rows_stored rows_loaded smm_done exp_done pv_done o_copied o_turned o_chain o_norm
            t_turned gn_chain gn_mean_done gn_var_done gn_var_out gn_eps gn_rstd gn_ready xn_ready y_done
            h2_ready h2_kept t_chain t_var t_eps t_rstd z2_ready z2_turned z2c_ready logit_done
            shifted_ready prob_exp r_chain mask_ready rank_done rows_out slots_ready scattered macc_ready t_chain2 rows_free""".split()
        (consts_in, lam_ready, consts_ready, ones_rows, vones, hc_ready, f_turned, htok_ready, f_stats,
         f_var, f_eps, f_rstd, resid_ready, ztok_ready, z_turned, zT_ready, proj_done, hi_ready, rest_ready,
         mid_ready, parts_ready, v_done, v_ready, mxmm_done, max_ready, nm_turned, mp_chain, rows_ready,
         rows_stored, rows_loaded, smm_done, exp_done, pv_done, o_copied, o_turned, o_chain, o_norm,
         t_turned, gn_chain, gn_mean_done, gn_var_done, gn_var_out, gn_eps, gn_rstd, gn_ready, xn_ready, y_done,
         h2_ready, h2_kept, t_chain, t_var, t_eps, t_rstd, z2_ready, z2_turned, z2c_ready, logit_done,
         shifted_ready, prob_exp, r_chain, mask_ready, rank_done, rows_out, slots_ready, scattered,
         macc_ready, t_chain2, rows_free) = [sem(n) for n in names]
        stored = [sem(f"stored{j}") for j in range(4)]
        loaded = [sem(f"loaded{j}") for j in range(4)]

        sp_passed, pool_passed, act_passed, dve_passed = [sem(n + "_passed2") for n in (
            "sp", "pool", "act", "dve")]
        block = ctx.enter_context(nc.Block())

        consts = [(ident, io["ident"]), (wv, io["L0_attn_V_w"]), (wout, io["L0_attn_out_w"]),
                  (grp, io["grp"]), (tri_f, io["tri"]), (wrout, io["L0_ffn_router_w"]),
                  (outb, io["L0_attn_out_b"].unsqueeze(0).to_broadcast([P, D])),
                  (rbias, io["L0_ffn_bias"].unsqueeze(0).to_broadcast([P, E])),
                  (base1, io["base1"].unsqueeze(0).to_broadcast([P, E]))]
        small = [(gnw[:, 0:1], io["L0_attn_gn_w"].unsqueeze(1)), (gnw[:, 1:2], io["L0_attn_gn_b"].unsqueeze(1)),
                 (kbias[:, 1:2], io["L0_attn_K1_b"].unsqueeze(1)), (kbias[:, 3:4], io["L0_attn_K2_b"].unsqueeze(1))]
        for j, name in enumerate(("Q1", "K1", "Q2", "K2")):
            small.append((wproj[:, j, :], io[f"L0_attn_{name}_w"]))
        for j, name in enumerate(("q1", "k1", "q2", "k2")):
            small.append((lam[:, j, :], io["L0_attn_lambda_" + name].rearrange("h o -> o h").to_broadcast([P, HEADS])))
        NCONST = 16 * (len(consts) + len(small))

        def has(t, g, stage):
            if not isinstance(t, int):
                return True
            n = 4 * t + g
            return {"F": t + 1 < B, "M": t < B, "Mprev": 0 <= n - 1 < 4 * B, "X": 0 <= n - 2 < 4 * B,
                    "Xprev": 0 <= n - 3 < 4 * B, "T": 0 <= t - 1 < B, "R": 0 <= t - 2 < B}[stage]

        def run(eng, step, first):
            first()

            def seq(t, par):
                for g in range(GROUPS):
                    step(t, g, par)
            seq(0, 0)
            seq(1, 1)
            with eng.Fori(1, 3) as i:
                seq(i * 2, 0)
                seq(i * 2 + 1, 1)
            for t in range(6, B + 2):
                seq(t, t % 2)

        def at(t, g, back):
            return 4 * t + g - back, t + (g - back) // 4, (g - back) % 4, ((g - back) // 4) % 2

        @block.sync
        def _(sp):
            for dst, src in consts:
                sp.dma_start(dst[:], src).then_inc(consts_in, 16)
            for dst, src in small:
                sp.dma_start(dst, src).then_inc(consts_in, 16)

            def keep_parts(b, j):
                sp.wait_ge(parts_ready, 4 * b + j + 1).then_inc(sp_passed, 1)
                if not (isinstance(b, int) and b == 0):
                    sp.wait_ge(loaded[j], 16 * TERMS * b).then_inc(sp_passed, 1)
                sp.dma_start(dram["parts"][j].rearrange("a p t -> p a t"), parts[:, j % 2]).then_inc(stored[j], 16)

            def load_stack(b, j, par):
                sp.wait_ge(stored[j], 16 * b + 16).then_inc(sp_passed, 1)
                if isinstance(b, int) and b < 2:
                    pass
                else:
                    sp.wait_ge(smm_done, 4 * UNITS * (b - 1)).then_inc(sp_passed, 1)
                for k in range(TERMS):
                    part = (Q_PART, K_PART)[j % 2][k]
                    sp.dma_start(stack[par][j][k * HD:(k + 1) * HD],
                                 dram["parts"][j, part].rearrange("(d h) t -> d h t", h=HEADS)
                                 ).then_inc(loaded[j], 16)

            def first():
                for j in range(4):
                    keep_parts(0, j)
                    load_stack(0, j, 0)

            def step(t, g, par):
                if has(t, g, "Mprev"):
                    n, b, gg, flip = at(t, g, 1)
                    p = par ^ flip
                    sp.wait_ge(rows_ready, n + 1).then_inc(sp_passed, 1)
                    if not (isinstance(n, int) and n == 0):
                        sp.wait_ge(rows_loaded, 32 * n).then_inc(sp_passed, 1)
                    sp.dma_start(dram["rows"].rearrange("a u t -> u a t"), mp[:]).then_inc(rows_stored, 16)
                    sp.wait_ge(rows_stored, 16 * n + 16).then_inc(sp_passed, 1)
                    for m in range(MAPS):
                        sp.dma_start(stack[p][2 * m][KT:KM, 2 * gg:2 * gg + 2, :],
                                     dram["rows"][:, 8 * m:8 * m + 8, :].rearrange("a (h q) t -> a h (q t)", h=2)
                                     ).then_inc(rows_loaded, 16)
                if has(t, g, "F"):
                    if g == 1:
                        keep_parts(t + 1, 0)
                        keep_parts(t + 1, 1)
                    if g == 2:
                        keep_parts(t + 1, 2)
                        load_stack(t + 1, 0, 1 - par)
                        load_stack(t + 1, 1, 1 - par)
                        keep_parts(t + 1, 3)
                    if g == 3:
                        load_stack(t + 1, 2, 1 - par)
                        load_stack(t + 1, 3, 1 - par)

            run(sp, step, first)

        @block.tensor
        def _(pe):
            def turn(dst, src, inc):
                for q in range(QT):
                    last = pe.transpose(dst[:, q * P:(q + 1) * P], src[:, q], ident[:])
                last.then_inc(inc, 1)

            def tokens(b):
                pe.wait_ge(hc_ready, b + 1)
                if not (isinstance(b, int) and b == 0):
                    pe.wait_ge(v_ready, b)
                turn(psA, hc[:].rearrange("p (q t) -> p q t", q=QT), f_turned)

            def features(b):
                pe.wait_ge(ztok_ready, b + 1)
                turn(psA, ztok, z_turned)

            def project(b, j):
                if j == 0:
                    pe.wait_ge(zT_ready, b + 1)
                else:
                    pe.wait_ge(hi_ready, 4 * b + j)
                pe.matmul(psA[:], wproj[:, j, :], zT[:], start=True, stop=True).then_inc(proj_done, 1)

            def values(b):
                pe.wait_ge(hi_ready, 4 * b + 4)
                for q in range(QT):
                    last = pe.matmul(psA[:, q * P:(q + 1) * P], zT[:, q * P:(q + 1) * P], wv[:],
                                     start=True, stop=True)
                last.then_inc(v_done, 1)

            pe.wait_ge(consts_in, NCONST)
            pe.wait_ge(consts_ready, 5)
            pe.wait_ge(vones, 4)
            pe.wait_ge(ones_rows, 4)

            def first():
                tokens(0)
                features(0)
                for j in range(4):
                    project(0, j)
                values(0)

            def step(t, g, par):
                xn_, xb, xg, xf = at(t, g, 2)
                pn, pb, pg, pf = at(t, g, 3)
                mn, mb, mg, mf = at(t, g, 1)

                def pv(n, b, gg, p, c):
                    pe.wait_ge(exp_done, UNITS * n + 4 * c + 4)
                    if c == 0:
                        if not (isinstance(n, int) and n == 0):
                            pe.wait_ge(o_copied, n)
                        if gg == 0:
                            pe.wait_ge(v_ready, b + 1)
                    for j in range(4):
                        last = pe.matmul(ps_o[32 * j:32 * j + 32, :], Vx[p][:, c, 2 * gg + j % 2, :],
                                         ex[:, 4 * (c % 2) + j, :], start=(c == 0), stop=(c == QT - 1))
                    last.then_inc(pv_done, 1)

                for u in range(UNITS):
                    if has(t, g, "M"):
                        if g == 0 and u == 0:
                            for j in range(4):
                                pe.wait_ge(loaded[j], 16 * TERMS * (t + 1))
                        m = 4 * UNITS * t + UNITS * g + u
                        if not (isinstance(m, int) and m < 2):
                            pe.wait_ge(max_ready, m - 1)
                        mp_, h, q = u // 8, 2 * g + (u // 4) % 2, u % 4
                        pe.matmul(ps_m[u % 2][:], stack[par][2 * mp_][0:KT, h, q * P:(q + 1) * P],
                                  stack[par][2 * mp_ + 1][0:KT, h, :], start=True, stop=True
                                  ).then_inc(mxmm_done, 1)
                    if has(t, g, "X"):
                        p = par ^ xf
                        if u == 0:
                            pe.wait_ge(rows_loaded, 32 * xn_ + 32)
                        e = UNITS * xn_ + u
                        if not (isinstance(e, int) and e < 2):
                            pe.wait_ge(exp_done, e - 1)
                        c, j = u // 4, u % 4
                        m_, h = j // 2, 2 * xg + j % 2
                        pe.matmul(ps_e[u % 2][:], stack[p][2 * m_ + 1][0:KM, h, c * P:(c + 1) * P],
                                  stack[p][2 * m_][0:KM, h, :], start=True, stop=True).then_inc(smm_done, 1)
                        if u in (6, 10, 14):
                            pv(xn_, xb, xg, p, (u - 6) // 4)
                    if u == 2 and has(t, g, "Xprev"):
                        pv(pn, pb, pg, par ^ pf, 3)
                    if u == 3 and has(t, g, "Mprev"):
                        pe.wait_ge(max_ready, UNITS * (mn + 1))
                        if not (isinstance(t, int) and 4 * t + g < 4):
                            pe.wait_ge(o_norm, pn)
                        if g == 3 and has(t, g, "T"):
                            pe.wait_ge(gn_chain, 4 * (t - 1) + 3)
                        pe.transpose(psB[0:UNITS, 0:P], nm[:, (g - 1) % 2, :], ident[:]).then_inc(nm_turned, 1)
                    if u == 8 and has(t, g, "Xprev"):
                        pe.wait_ge(o_copied, pn + 1)
                        if has(t, g, "Mprev"):
                            pe.wait_ge(rows_ready, mn + 1)
                        else:
                            pe.wait_ge(o_norm, pn)
                        if g == 3 and has(t, g, "T"):
                            pe.wait_ge(gn_var_out, t)
                        turn(psB, OT[:].rearrange("p (q t) -> p q t", q=QT), o_turned)
                    b = t + 1
                    if has(t, g, "F"):
                        if (g, u) == (0, 1):
                            tokens(b)
                        if (g, u) == (0, 13):
                            features(b)
                        if (g, u) == (1, 1):
                            project(b, 0)
                        if (g, u) == (1, 7):
                            project(b, 1)
                        if (g, u) == (1, 13):
                            project(b, 2)
                        if (g, u) == (2, 4):
                            project(b, 3)
                        if (g, u) == (3, 2):
                            values(b)
                    b = t - 1
                    if has(t, g, "T"):
                        if (g, u) == (2, 14):
                            pe.wait_ge(o_norm, 4 * b + 4)
                            if not (isinstance(b, int) and b == 0):
                                pe.wait_ge(rows_out, b)
                            turn(psC, otok[:].rearrange("p q h d -> p q (h d)"), t_turned)
                        if (g, u) == (3, 1):
                            pe.wait_ge(gn_chain, 4 * b + 2)
                            pe.matmul(psB[:, 0:1], grp[:], gmv[:, 0:1], start=True, stop=True
                                      ).then_inc(gn_mean_done, 1)
                        if (g, u) == (3, 6):
                            pe.wait_ge(gn_chain, 4 * b + 4)
                            if has(t, g, "Mprev"):
                                pe.wait_ge(rows_ready, mn + 1)
                            pe.matmul(psB[:, 0:1], grp[:], gv[:], start=True, stop=True
                                      ).then_inc(gn_var_done, 1)
                        if (g, u) == (3, 13):
                            pe.wait_ge(xn_ready, b + 1)
                            for q in range(QT):
                                last = pe.matmul(psC[:, q * P:(q + 1) * P], xn[:, q * P:(q + 1) * P], wout[:],
                                                 start=True, stop=True)
                            last.then_inc(y_done, 1)
                    b = t - 2
                    if has(t, g, "R"):
                        if (g, u) == (0, 5):
                            pe.wait_ge(z2_ready, b + 1)
                            turn(psC, R[:, :, 0:D], z2_turned)
                        if (g, u) == (0, 12):
                            pe.wait_ge(z2c_ready, b + 1)
                            for q in range(QT):
                                last = pe.matmul(psC[:, q * E:(q + 1) * E], z2c[:, q * P:(q + 1) * P], wrout[:],
                                                 start=True, stop=True)
                            last.then_inc(logit_done, 1)
                        if (g, u) == (1, 14):
                            pe.wait_ge(mask_ready, b + 1)
                            pe.wait_ge(macc_ready, b + 1)
                            for q in range(QT):
                                out = psC[:, q * E:(q + 1) * E]
                                pe.matmul(out, ones[:], Macc[:], start=True, stop=False)
                                for q2 in range(q):
                                    pe.matmul(out, ones[:], M[:, q2, :], start=False, stop=False)
                                last = pe.matmul(out, tri[:], M[:, q, :], start=False, stop=True)
                            last.then_inc(rank_done, 1)

            run(pe, step, first)

        @block.scalar
        def _(act):
            act.wait_ge(consts_in, NCONST)
            act.wait_ge(lam_ready, 1)
            act.activation(lam[:, 0, :], lam[:, 1, :], ACT.Exp).then_inc(lam_ready, 1)
            act.activation(lam[:, 2, :], lam[:, 3, :], ACT.Exp).then_inc(lam_ready, 1)

            def take(b):
                if not (isinstance(b, int) and b == 0):
                    act.wait_ge(f_turned, b).then_inc(act_passed, 1)
                act.activation(hc[:], X[:, b, 1:S + 1], ACT.Copy).then_inc(hc_ready, 1)

            def tokens(b):
                act.wait_ge(f_turned, b + 1)
                if not (isinstance(b, int) and b == 0):
                    act.wait_ge(resid_ready, b)
                    act.wait_ge(ztok_ready, b)
                act.activation(htok[:].rearrange("p q d -> p (q d)"), psA[:], ACT.Copy).then_inc(htok_ready, 1)

            def features(b):
                act.wait_ge(z_turned, b + 1)
                act.activation(zT[:], psA[:], ACT.Copy).then_inc(zT_ready, 1)

            def split(b, j):
                n = 4 * b + j
                act.wait_ge(proj_done, n + 1)
                if not (isinstance(n, int) and n == 0):
                    act.wait_ge(rest_ready, n)
                if not (isinstance(n, int) and n < 2):
                    act.wait_ge(stored[j ^ 2], (16 * b if j < 2 else 16 * b + 16))
                bias = {"bias": kbias[:, j:j + 1]} if j % 2 else {}
                f = ACT.Identity if j % 2 else ACT.Copy
                act.activation(q32[:], psA[:], f, **bias)
                act.activation(parts[:, j % 2, 0, :], psA[:], f, **bias).then_inc(hi_ready, 1)

            def middle(b, j):
                n = 4 * b + j
                act.wait_ge(rest_ready, n + 1)
                act.activation(parts[:, j % 2, 1, :], rest[:], ACT.Copy).then_inc(mid_ready, 1)

            def values(b, par):
                act.wait_ge(v_done, b + 1)
                if not (isinstance(b, int) and b < 2):
                    act.wait_ge(pv_done, 4 * QT * (b - 1))
                act.activation(Vx[par][:, :, :, 0:HD], psA[:].rearrange("p (q h d) -> p q h d", q=QT, h=HEADS),
                               ACT.Copy).then_inc(v_ready, 1)

            act.wait_ge(vones, 4)

            def first():
                take(0)
                tokens(0)
                features(0)
                for j in range(4):
                    split(0, j)
                    middle(0, j)
                values(0, 0)

            def step(t, g, par):
                xn_, xb, xg, xf = at(t, g, 2)
                pn, pb, pg, pf = at(t, g, 3)
                for u in range(UNITS):
                    if has(t, g, "X"):
                        e = UNITS * xn_ + u
                        c = u // 4
                        act.wait_ge(smm_done, e + 1)
                        if u % 4 == 0:
                            k = 4 * xn_ + c
                            if not (isinstance(k, int) and k < 2):
                                act.wait_ge(pv_done, k - 1)
                        act.activation(ex[:, 4 * (c % 2) + u % 4, :], ps_e[u % 2][:], ACT.Exp,
                                       scale=float(HD) ** -0.5).then_inc(exp_done, 1)
                    if u == 4 and has(t, g, "Xprev"):
                        act.wait_ge(pv_done, 4 * pn + 4)
                        if not (isinstance(pn, int) and pn == 0):
                            act.wait_ge(o_turned, pn)
                        act.activation(OT[:], ps_o[:], ACT.Copy).then_inc(o_copied, 1)
                    b = t + 1
                    if has(t, g, "F"):
                        if (g, u) == (0, 0):
                            take(b)
                        if (g, u) == (0, 3):
                            tokens(b)
                        if (g, u) == (0, 14):
                            features(b)
                        for j, when in enumerate(((1, 2), (1, 8), (1, 14), (2, 5))):
                            if (g, u) == when:
                                split(b, j)
                        for j, when in enumerate(((1, 5), (1, 11), (2, 1), (2, 8))):
                            if (g, u) == when:
                                middle(b, j)
                        if (g, u) == (3, 3):
                            values(b, 1 - par)
                    b = t - 1
                    if has(t, g, "T"):
                        if (g, u) == (3, 11):
                            act.wait_ge(gn_ready, b + 1)
                            act.activation(xn[:], psC[:], ACT.Identity, scale=gsc[:], bias=gbi[:]
                                           ).then_inc(xn_ready, 1)
                        if (g, u) == (3, 15):
                            act.wait_ge(h2_ready, b + 1).then_inc(act_passed, 1)
                            act.activation(H2[:, b].rearrange("p q d -> p (q d)"), h2c[:].rearrange("p q d -> p (q d)"),
                                           ACT.Copy).then_inc(h2_kept, 1)
                    b = t - 2
                    if has(t, g, "R"):
                        if (g, u) == (0, 7):
                            act.wait_ge(z2_turned, b + 1)
                            act.activation(z2c[:], psC[:], ACT.Copy)
                            act.activation(Z2[:, b], psC[:], ACT.Copy).then_inc(z2c_ready, 1)
                        if (g, u) == (1, 3):
                            act.wait_ge(shifted_ready, b + 1)
                            act.activation(prob[:, :, 0:E], logit[:], ACT.Exp).then_inc(prob_exp, 1)

            run(act, step, first)

        @block.gpsimd
        def _(pool):
            for p in range(2):
                pool.memset(Vx[p][:, :, :, HD:32], 0.0).then_inc(vones, 1)
            for p in range(2):
                pool.wait_ge(vones, 2).then_inc(pool_passed, 1)
                pool.memset(Vx[p][:, :, :, HD:HD + 1], 1.0).then_inc(vones, 1)
            pool.memset(half[:], -0.5).then_inc(consts_ready, 1)
            pool.memset(ones[:], 1.0).then_inc(consts_ready, 1)
            pool.memset(Macc[:], 0.0).then_inc(consts_ready, 1)
            pool.memset(prob[:, :, E:E + 2], -1.0).then_inc(consts_ready, 1)
            pool.wait_ge(consts_in, NCONST).then_inc(pool_passed, 1)
            pool.tensor_copy(tri[:], tri_f[:]).then_inc(consts_ready, 1)
            pool.wait_ge(consts_ready, 5).then_inc(pool_passed, 1)

            def rstd_of(src, tmp, out, wait, n, count, eps_sem, done, width):
                pool.wait_ge(wait, count).then_inc(pool_passed, 1)
                pool.tensor_scalar(tmp, src, 1e-5, None, ALU.add).then_inc(eps_sem, 1)
                pool.wait_ge(eps_sem, n + 1).then_inc(pool_passed, 1)
                pool.tensor_tensor(out, tmp, half[:, 0:width], ALU.pow).then_inc(done, 1)

            def norm(b):
                rstd_of(fmv[:, :, 1], fve[:], frstd[:], f_var, b, b + 1, f_eps, f_rstd, QT)
                pool.tensor_tensor(H2[:, b], htok[:], outb[:].unsqueeze(1).to_broadcast([P, QT, D]), ALU.add
                                   ).then_inc(resid_ready, 1)

            def low(b, j):
                pool.wait_ge(mid_ready, 4 * b + j + 1).then_inc(pool_passed, 1)
                pool.tensor_tensor(parts[:, j % 2, 2, :], rest[:], parts[:, j % 2, 1, :], ALU.subtract
                                   ).then_inc(parts_ready, 1)

            def first():
                norm(0)
                for j in range(4):
                    low(0, j)

            def scatter(b, lo, hi):
                if lo == 0:
                    pool.wait_ge(slots_ready, b + 1).then_inc(pool_passed, 1)
                for i in range(lo, hi):
                    q, k = i // TOPK, i % TOPK
                    pool.indirect_dma_start(dram["rows_x"], bass.IndirectOffsetOnAxis(ap=sidx[:, q, k:k + 1], axis=0),
                                            R[:, q, :], None, bounds_check=E * CAP - 1, oob_is_err=False
                                            ).then_inc(scattered, 16)

            def step(t, g, par):
                b = t + 1
                if has(t, g, "F"):
                    if g == 0:
                        norm(b)
                    if g == 1:
                        low(b, 0)
                        low(b, 1)
                    if g == 2:
                        low(b, 2)
                        low(b, 3)
                if has(t, g, "T") and g == 3:
                    b = t - 1
                    rstd_of(gvar[:], gve[:], grs[:], gn_var_out, b, b + 1, gn_eps, gn_rstd, 1)
                    rstd_of(tmv[:, :, 1], tve[:], trstd[:], t_var, b, b + 1, t_eps, t_rstd, QT)
                if has(t, g, "R") and g == 2:
                    scatter(t - 2, 0, QT * TOPK)
                if has(t, g, "R") and g == 3:
                    pool.wait_ge(scattered, 16 * QT * TOPK * (t - 1)).then_inc(pool_passed, 1)
                    pool.memset(freed[:], 0.0).then_inc(rows_free, 1)

            run(pool, step, first)

        @block.vector
        def _(dve):
            for p in range(2):
                for j in (1, 3):
                    dve.memset(stack[p][j][KT:KM], 1.0).then_inc(ones_rows, 1)
            dve.wait_ge(consts_in, NCONST)
            dve.tensor_tensor(lam[:, 1, :], lam[:, 0, :], lam[:, 1, :], ALU.mult)
            dve.tensor_tensor(lam[:, 3, :], lam[:, 2, :], lam[:, 3, :], ALU.mult).then_inc(lam_ready, 1)
            dve.wait_ge(lam_ready, 3)
            dve.tensor_tensor(neglam[:], lam[:, 2, :], lam[:, 0, :], ALU.subtract).then_inc(lam_ready, 1)
            dve.wait_ge(lam_ready, 4)
            dve.tensor_scalar(neglam[:], neglam[:], -0.2, None, ALU.add).then_inc(lam_ready, 1)
            dve.wait_ge(lam_ready, 5)
            dve.wait_ge(consts_ready, 5)
            dve.memset(M[:], 0.0).then_inc(rows_free, 1)

            def stats(b):
                dve.wait_ge(htok_ready, b + 1)
                for q in range(QT):
                    last = dve.bn_stats(fstats[:, q, :], htok[:, q, :])
                last.then_inc(f_stats, 1)
                dve.wait_ge(f_stats, b + 1).then_inc(dve_passed, 1)
                for q in range(QT):
                    last = dve.bn_aggr(fmv[:, q, :], fstats[:, q, :])
                last.then_inc(f_var, 1)

            def norm(b):
                dve.wait_ge(f_rstd, b + 1)
                if not (isinstance(b, int) and b == 0):
                    dve.wait_ge(z_turned, b)
                for q in range(QT):
                    last = dve.tensor_scalar(ztok[:, q, :], htok[:, q, :], fmv[:, q, 0:1], frstd[:, q:q + 1],
                                             ALU.subtract, ALU.mult)
                last.then_inc(ztok_ready, 1)

            def take_rest(b, j):
                n = 4 * b + j
                dve.wait_ge(hi_ready, n + 1)
                if not (isinstance(n, int) and n == 0):
                    dve.wait_ge(parts_ready, n)
                dve.tensor_tensor(rest[:], q32[:], parts[:, j % 2, 0, :], ALU.subtract).then_inc(rest_ready, 1)

            def first():
                stats(0)
                norm(0)
                for j in range(4):
                    take_rest(0, j)

            def split_rows(n):
                dve.wait_ge(nm_turned, n + 1)
                if not (isinstance(n, int) and n == 0):
                    dve.wait_ge(rows_stored, 16 * n)
                src = psB[0:UNITS, 0:P]
                dve.tensor_copy(mp[:, 0, :], src).then_inc(mp_chain, 1)
                dve.wait_ge(mp_chain, 3 * n + 1)
                dve.tensor_tensor(mrest[:], src, mp[:, 0, :], ALU.subtract).then_inc(mp_chain, 1)
                dve.wait_ge(mp_chain, 3 * n + 2)
                dve.tensor_copy(mp[:, 1, :], mrest[:]).then_inc(mp_chain, 1)
                dve.wait_ge(mp_chain, 3 * n + 3)
                dve.tensor_tensor(mp[:, 2, :], mrest[:], mp[:, 1, :], ALU.subtract).then_inc(rows_ready, 1)

            def output(n, gg):
                dve.wait_ge(o_turned, n + 1)
                o = psB[:].rearrange("p (q j c) -> p q j c", q=QT, j=4)
                dve.reciprocal(rsum[:], o[:, :, :, HD]).then_inc(o_chain, 1)
                dve.wait_ge(o_chain, 3 * n + 1)
                dve.tensor_tensor(rsum[:, :, 2:4], rsum[:, :, 2:4],
                                  neglam[:, 2 * gg:2 * gg + 2].unsqueeze(1).to_broadcast([P, QT, 2]), ALU.mult
                                  ).then_inc(o_chain, 1)
                dve.wait_ge(o_chain, 3 * n + 2)
                dve.tensor_tensor(on[:], o[:, :, :, 0:HD], rsum[:].unsqueeze(3).to_broadcast([P, QT, 4, HD]),
                                  ALU.mult).then_inc(o_chain, 1)
                dve.wait_ge(o_chain, 3 * n + 3)
                dve.tensor_tensor(otok[:, :, 2 * gg:2 * gg + 2, :], on[:, :, 0:2, :], on[:, :, 2:4, :], ALU.add
                                  ).then_inc(o_norm, 1)

            def step(t, g, par):
                pn, pb, pg, pf = at(t, g, 3)
                mn, mb, mg, mf = at(t, g, 1)
                for u in range(UNITS):
                    if has(t, g, "M"):
                        m = 4 * UNITS * t + UNITS * g + u
                        dve.wait_ge(mxmm_done, m + 1)
                        if u == 0 and not (isinstance(t, int) and 4 * t + g < 2):
                            dve.wait_ge(nm_turned, mn)
                        dve.tensor_reduce(nm[:, g % 2, u:u + 1], ps_m[u % 2][:], AX.X, ALU.max, negate=True
                                          ).then_inc(max_ready, 1)
                    if u == 4 and has(t, g, "Mprev"):
                        split_rows(mn)
                    if u == 10 and has(t, g, "Xprev"):
                        if pg == 0 and not (isinstance(t, int) and pb == 0):
                            dve.wait_ge(t_turned, pb)
                        output(pn, pg)
                    b = t + 1
                    if has(t, g, "F"):
                        if (g, u) == (0, 5):
                            stats(b)
                        if (g, u) == (0, 9):
                            norm(b)
                        for j, when in enumerate(((1, 4), (1, 9), (1, 15), (2, 7))):
                            if (g, u) == when:
                                take_rest(b, j)
                    b = t - 1
                    if has(t, g, "T"):
                        if (g, u) == (2, 15):
                            dve.wait_ge(t_turned, b + 1)
                            dve.bn_stats(gst[:], psC[:]).then_inc(gn_chain, 1)
                            dve.wait_ge(gn_chain, 4 * b + 1).then_inc(dve_passed, 1)
                            dve.bn_aggr(gmv[:], gst[:]).then_inc(gn_chain, 1)
                        if (g, u) == (3, 2):
                            dve.wait_ge(gn_mean_done, b + 1)
                            dve.tensor_copy(gm[:], psB[:, 0:1])
                            dve.tensor_tensor(gd[:], gmv[:, 0:1], psB[:, 0:1], ALU.subtract).then_inc(gn_chain, 1)
                            dve.wait_ge(gn_chain, 4 * b + 3)
                            dve.scalar_tensor_tensor(out=gv[:], in0=gd[:], scalar=gd[:], in1=gmv[:, 1:2],
                                                     op0=ALU.mult, op1=ALU.add).then_inc(gn_chain, 1)
                        if (g, u) == (3, 7):
                            dve.wait_ge(gn_var_done, b + 1)
                            dve.tensor_copy(gvar[:], psB[:, 0:1]).then_inc(gn_var_out, 1)
                        if (g, u) == (3, 9):
                            dve.wait_ge(gn_rstd, b + 1)
                            dve.tensor_tensor(gsc[:], grs[:], gnw[:, 0:1], ALU.mult).then_inc(t_chain, 1)
                            dve.wait_ge(t_chain, 3 * b + 1)
                            dve.tensor_tensor(gbi[:], gm[:], gsc[:], ALU.mult).then_inc(t_chain, 1)
                            dve.wait_ge(t_chain, 3 * b + 2)
                            dve.tensor_tensor(gbi[:], gnw[:, 1:2], gbi[:], ALU.subtract).then_inc(gn_ready, 1)
                        if (g, u) == (3, 14):
                            dve.wait_ge(y_done, b + 1)
                            dve.wait_ge(resid_ready, b + 1)
                            if not (isinstance(b, int) and b == 0):
                                dve.wait_ge(h2_kept, b)
                            dve.tensor_tensor(h2c[:], psC[:].rearrange("p (q d) -> p q d", q=QT), H2[:, b], ALU.add
                                              ).then_inc(h2_ready, 1)
                            dve.wait_ge(h2_ready, b + 1)
                            for q in range(QT):
                                last = dve.bn_stats(tstats[:, q, :], h2c[:, q, :])
                            last.then_inc(t_chain, 1)
                            dve.wait_ge(t_chain, 3 * b + 3).then_inc(dve_passed, 1)
                            for q in range(QT):
                                last = dve.bn_aggr(tmv[:, q, :], tstats[:, q, :])
                            last.then_inc(t_var, 1)
                    b = t - 2
                    if has(t, g, "R"):
                        if (g, u) == (0, 2):
                            dve.wait_ge(t_rstd, b + 1)
                            dve.wait_ge(rows_free, b + 1)
                            for q in range(QT):
                                last = dve.tensor_scalar(R[:, q, 0:D], h2c[:, q, :], tmv[:, q, 0:1],
                                                         trstd[:, q:q + 1], ALU.subtract, ALU.mult)
                            last.then_inc(z2_ready, 1)
                            dve.tensor_reduce(mnew[:], M[:].rearrange("p q e -> p e q"), AX.X, ALU.add
                                              ).then_inc(t_chain2, 1)
                            dve.wait_ge(t_chain2, b + 1)
                            dve.tensor_tensor(Macc[:], Macc[:], mnew[:], ALU.add).then_inc(macc_ready, 1)
                        if (g, u) == (0, 14):
                            dve.wait_ge(logit_done, b + 1)
                            dve.tensor_tensor(logit[:], psC[:, 0:QT * E].rearrange("p (q e) -> p q e", q=QT),
                                              rbias[:].unsqueeze(1).to_broadcast([P, QT, E]), ALU.add
                                              ).then_inc(r_chain, 1)
                            dve.wait_ge(r_chain, NR * b + 1)
                            dve.tensor_reduce(lmax[:], logit[:], AX.X, ALU.max).then_inc(r_chain, 1)
                            dve.wait_ge(r_chain, NR * b + 2)
                            dve.tensor_tensor(logit[:], logit[:], lmax[:].unsqueeze(2).to_broadcast([P, QT, E]),
                                              ALU.subtract).then_inc(shifted_ready, 1)
                        if (g, u) == (1, 6):
                            dve.wait_ge(prob_exp, b + 1)
                            pr = prob[:, :, 0:E]
                            dve.tensor_reduce(lsum[:], pr, AX.X, ALU.add).then_inc(r_chain, 1)
                            dve.wait_ge(r_chain, NR * b + 3)
                            dve.reciprocal(lrec[:], lsum[:]).then_inc(r_chain, 1)
                            dve.wait_ge(r_chain, NR * b + 4)
                            dve.tensor_tensor(pr, pr, lrec[:].unsqueeze(2).to_broadcast([P, QT, E]), ALU.mult
                                              ).then_inc(r_chain, 1)
                            dve.wait_ge(r_chain, NR * b + 5).then_inc(dve_passed, 1)
                            for q in range(QT):
                                last = dve.max(top[:, q, :], prob[:, q, 0:E])
                            last.then_inc(r_chain, 1)
                            dve.wait_ge(r_chain, NR * b + 6)
                            dve.tensor_reduce(gsum[:], top[:, :, 0:TOPK], AX.X, ALU.add)
                            dve.memset(top[:, :, TOPK:8], -1.0).then_inc(r_chain, 1)
                            dve.wait_ge(r_chain, NR * b + 7).then_inc(dve_passed, 1)
                            for q in range(QT):
                                last = dve.match_replace(repl[:, q, :], top[:, q, :], prob[:, q, :], -2.0)
                            last.then_inc(r_chain, 1)
                            dve.wait_ge(r_chain, NR * b + 8)
                            dve.tensor_tensor(M[:], repl[:, :, 0:E], pr, ALU.not_equal).then_inc(mask_ready, 1)
                        if (g, u) == (1, 11):
                            dve.tensor_scalar(gsum[:], gsum[:], 1e-9, None, ALU.add).then_inc(r_chain, 1)
                            dve.wait_ge(r_chain, NR * b + 9)
                            dve.reciprocal(grec[:], gsum[:]).then_inc(r_chain, 1)
                            dve.wait_ge(r_chain, NR * b + 10)
                            dve.tensor_tensor(gate[:], prob[:, :, 0:E],
                                              grec[:].unsqueeze(2).to_broadcast([P, QT, E]), ALU.mult
                                              ).then_inc(r_chain, 1)
                            dve.wait_ge(r_chain, NR * b + 11)
                        if (g, u) == (1, 15):
                            dve.wait_ge(rank_done, b + 1)
                            rank = psC[:, 0:QT * E].rearrange("p (q e) -> p q e", q=QT)
                            dve.scalar_tensor_tensor(out=Mv[:], in0=rank, scalar=float(CAP), in1=M[:],
                                                     op0=ALU.is_lt, op1=ALU.mult)
                            dve.tensor_tensor(slot1[:], rank, base1[:].unsqueeze(1).to_broadcast([P, QT, E]),
                                              ALU.add).then_inc(rows_out, 1)
                            dve.wait_ge(rows_out, b + 1)
                            dve.tensor_tensor(slot1[:], slot1[:], Mv[:], ALU.mult).then_inc(r_chain, 1)
                            dve.wait_ge(r_chain, NR * b + 12)
                            dve.tensor_tensor(R[:, :, D:ROW], gate[:], Mv[:], ALU.mult)
                            for q in range(QT):
                                last = dve.max(v8[:, q, :], slot1[:, q, :])
                            last.then_inc(r_chain, 1)
                            dve.wait_ge(r_chain, NR * b + 13)
                            dve.tensor_copy(slots[:, b], v8[:])
                            dve.tensor_scalar(none[:], v8[:], 0.0, FAR, ALU.is_equal, ALU.mult).then_inc(r_chain, 1)
                            dve.wait_ge(r_chain, NR * b + 14)
                            dve.scalar_tensor_tensor(out=sidx[:], in0=v8[:], scalar=-1.0, in1=none[:],
                                                     op0=ALU.add, op1=ALU.add).then_inc(slots_ready, 1)

            run(dve, step, first)
PAIRS = E // 2
TILES = CAP // P
HALF = TILES // 2
COLS = HALF * P
FF = 64


def experts(nc, io, H2, Z2, slots, dram, out):
    with ExitStack() as ctx:
        def sb(name, shape, dt=F32):
            return ctx.enter_context(nc.sbuf_tensor(name, shape, dt))

        def sem(name):
            return ctx.enter_context(nc.semaphore(name))

        ident = sb("ident3", [P, P])
        shw = sb("shw", [P, 2, 2 * FF])
        shd = sb("shd", [P, D])
        rows = [sb(f"rows{i}", [P, 2, TILES, ROW]) for i in range(2)]
        wgu = [sb(f"wgu{i}", [P, 2, 2, FF]) for i in range(2)]
        wdn = [sb(f"wdn{i}", [P, D]) for i in range(2)]
        xT = sb("xT3", [P, 2, 2, COLS])
        act_g = sb("act_g", [P, 2, S])
        hid = sb("hid", [P, 2, S])
        yt = [sb(f"yt{i}", [P, 2, TILES, D]) for i in range(2)]
        zero = sb("zero3", [1, D])
        NG = 4
        got = [sb(f"got{i}", [P, TOPK, D]) for i in range(NG)]
        idx = [sb(f"idx{i}", [P, 8], I32) for i in range(NG)]
        total = [sb(f"total{i}", [P, D]) for i in range(NG)]
        res = [sb(f"res{i}", [P, D]) for i in range(NG)]

        ps_x = [ctx.enter_context(nc.psum_tensor(f"px{i}", [P, S], F32)) for i in range(2)]
        ps_g = [ctx.enter_context(nc.psum_tensor(f"pg{i}", [P, S], F32)) for i in range(2)]
        ps_u = [ctx.enter_context(nc.psum_tensor(f"pu{i}", [P, S], F32)) for i in range(2)]
        ps_y = [ctx.enter_context(nc.psum_tensor(f"py{i}", [P, S], F32)) for i in range(2)]

        (consts3, zero3_ready, zero3_written, sh_mm, sh_gated, sh_hid, sh_down, sh_added, x_turned, x_out,
         gu_done, gated, hid_ready, down_done, y_ready) = [sem(n) for n in (
             "consts3", "zero3_ready", "zero3_written", "sh_mm", "sh_gated", "sh_hid", "sh_down", "sh_added",
             "x_turned", "x_out", "gu_done", "gated", "hid_ready", "down_done", "y_ready")]
        rows_in = [sem(f"rows_in{i}") for i in range(2)]
        y_written = [sem(f"y_written{i}") for i in range(2)]
        idx_ready = sem("idx_ready")
        gathered = [sem(f"gathered{i}") for i in range(NG)]
        summed = sem("summed")
        res_ready = sem("res_ready")
        stored = [sem(f"res_stored{i}") for i in range(NG)]

        LOADS = 16 * 3
        sp_passed, pool_passed = sem("sp_passed3"), sem("pool_passed3")
        block = ctx.enter_context(nc.Block())

        @block.sync
        def _(sp):
            sp.dma_start(ident[:], io["ident"]).then_inc(consts3, 16)
            sp.dma_start(shw[:], io["shared_gu"]).then_inc(consts3, 16)
            sp.dma_start(shd[:], io["shared_down"]).then_inc(consts3, 16)

            def load(p, par):
                sp.dma_start(rows[par][:], dram["rows_x"].rearrange("(e p n) c -> p e n c", e=E, n=TILES)[
                    :, bass.ds(p * 2, 2)]).then_inc(rows_in[par], 16)
                sp.dma_start(wgu[par][:].rearrange("p a b f -> p (a b f)"), io["experts_gu"][p]).then_inc(rows_in[par], 16)
                sp.dma_start(wdn[par][:], io["experts_down"][p]).then_inc(rows_in[par], 16)

            load(0, 0)
            load(1, 1)

            def following(p, par):
                sp.wait_ge(y_ready, 4 * p + 4).then_inc(sp_passed, 1)
                load(p + 2, par)

            with sp.Fori(0, PAIRS // 2 - 1) as i:
                following(i * 2, 0)
                following(i * 2 + 1, 1)

        @block.tensor
        def _(pe):
            pe.wait_ge(consts3, 48)

            def shared_up(b):
                if not (isinstance(b, int) and b == 0):
                    pe.wait_ge(sh_hid, b)
                for ps, w in ((ps_g, 0), (ps_u, 1)):
                    last = pe.matmul(ps[0][:], shw[:, w, :], Z2[:, b, :], start=True, stop=True)
                last.then_inc(sh_mm, 1)

            def shared_down(b):
                pe.wait_ge(sh_hid, b + 1)
                if not (isinstance(b, int) and b == 0):
                    pe.wait_ge(sh_added, b)
                for q in range(QT):
                    last = pe.matmul(ps_y[0][:, q * P:(q + 1) * P], hid[:, 0, q * P:(q + 1) * P], shd[:],
                                     start=True, stop=True)
                last.then_inc(sh_down, 1)

            shared_up(0)
            with pe.Fori(1, B) as b:
                shared_down(b - 1)
                shared_up(b)
            shared_down(B - 1)

            def up(v, half, par):
                pe.wait_ge(x_out, 2 * v + 2)
                if isinstance(v, int) and v < 2:
                    if v == 0:
                        pe.wait_ge(sh_hid, B)
                else:
                    pe.wait_ge(hid_ready, v - 1)
                for w, ps in enumerate((ps_g, ps_u)):
                    for j in range(2):
                        last = pe.matmul(ps[half][FF * j:FF * j + FF, 0:COLS], wgu[par][:, w, j, :],
                                         xT[:, half, j, :], start=True, stop=True)
                last.then_inc(gu_done, 1)

            def down(v, half, par):
                pe.wait_ge(hid_ready, v + 1)
                if isinstance(v, int) and v == 0:
                    pe.wait_ge(sh_added, B)
                else:
                    pe.wait_ge(y_ready, 2 * v)
                for k in range(HALF):
                    for j in range(2):
                        last = pe.matmul(ps_y[j][:, k * P:(k + 1) * P],
                                         hid[FF * j:FF * j + FF, half, k * P:(k + 1) * P],
                                         wdn[par][FF * j:FF * j + FF, :], start=True, stop=True)
                last.then_inc(down_done, 1)

            def turn(i, n):
                v, half, par = 4 * i + n, n % 2, (n // 2) % 2
                if half == 0:
                    pe.wait_ge(rows_in[par], LOADS * (i + n // 4) + LOADS)
                for j in range(2):
                    m = 2 * v + j
                    if not (isinstance(m, int) and m < 2):
                        pe.wait_ge(x_out, m - 1)
                    for k in range(HALF):
                        last = pe.transpose(ps_x[j][:, k * P:(k + 1) * P],
                                            rows[par][:, j, half * HALF + k, 0:D], ident[:])
                    last.then_inc(x_turned, 1)

            turn(0, 0)
            turn(0, 1)
            up(0, 0, 0)

            def body(i, last):
                for n in range(4):
                    if n + 2 < 4 or not last:
                        turn(i, n + 2)
                    if n + 1 < 4 or not last:
                        up(4 * i + n + 1, (n + 1) % 2, ((n + 1) // 2) % 2)
                    down(4 * i + n, n % 2, n // 2)

            with pe.Fori(0, PAIRS // 2 - 1) as i:
                body(i, False)
            body(PAIRS // 2 - 1, True)

        @block.scalar
        def _(act):
            def shared(b):
                act.wait_ge(sh_mm, b + 1)
                act.activation(act_g[:, 0, :], ps_g[0][:], ACT.Silu).then_inc(sh_gated, 1)

            with act.Fori(0, B) as b:
                shared(b)

            def take(v, half):
                for j in range(2):
                    act.wait_ge(x_turned, 2 * v + j + 1)
                    if j == 0 and not (isinstance(v, int) and v < 2):
                        act.wait_ge(gu_done, v - 1)
                    act.activation(xT[:, half, j, :], ps_x[j][:, 0:COLS], ACT.Copy).then_inc(x_out, 1)

            def gate(v, half):
                act.wait_ge(gu_done, v + 1)
                if isinstance(v, int) and v < 2:
                    act.wait_ge(sh_hid, B)
                else:
                    act.wait_ge(hid_ready, v - 1)
                act.activation(act_g[:, half, 0:COLS], ps_g[half][:, 0:COLS], ACT.Silu).then_inc(gated, 1)

            take(0, 0)
            take(1, 1)
            gate(0, 0)

            def body(i, last):
                for n in range(4):
                    if n + 2 < 4 or not last:
                        take(4 * i + n + 2, n % 2)
                    if n + 1 < 4 or not last:
                        gate(4 * i + n + 1, (n + 1) % 2)

            with act.Fori(0, PAIRS // 2 - 1) as i:
                body(i, False)
            body(PAIRS // 2 - 1, True)

            def keep(i, n):
                act.wait_ge(res_ready, NG * i + n + 1)
                act.dma_start(out[i, n * P:(n + 1) * P, :], res[n][:]).then_inc(stored[n], 16)

            with act.Fori(0, B) as i:
                for n in range(NG):
                    keep(i, n)
            for n in range(NG):
                act.wait_ge(stored[n], 16 * B)

        @block.vector
        def _(dve):
            dve.memset(zero[:], 0.0).then_inc(zero3_ready, 1)

            def shared_hidden(b):
                dve.wait_ge(sh_gated, b + 1)
                if not (isinstance(b, int) and b == 0):
                    dve.wait_ge(sh_down, b)
                dve.tensor_tensor(hid[:, 0, :], ps_u[0][:], act_g[:, 0, :], ALU.mult).then_inc(sh_hid, 1)

            def shared_add(b):
                dve.wait_ge(sh_down, b + 1)
                dve.scalar_tensor_tensor(out=H2[:, b].rearrange("p q d -> p (q d)"), in0=ps_y[0][:],
                                         scalar=1.0 / 2, in1=H2[:, b].rearrange("p q d -> p (q d)"),
                                         op0=ALU.mult, op1=ALU.add).then_inc(sh_added, 1)

            shared_hidden(0)
            with dve.Fori(1, B) as b:
                shared_add(b - 1)
                shared_hidden(b)
            shared_add(B - 1)

            def hidden(v, half):
                dve.wait_ge(gated, v + 1)
                if not (isinstance(v, int) and v < 2):
                    dve.wait_ge(down_done, v - 1)
                elif v == 0:
                    dve.wait_ge(sh_down, B)
                dve.tensor_tensor(hid[:, half, 0:COLS], ps_u[half][:, 0:COLS], act_g[:, half, 0:COLS],
                                  ALU.mult).then_inc(hid_ready, 1)

            def weigh(i, n):
                v, half, par = 4 * i + n, n % 2, n // 2
                dve.wait_ge(down_done, v + 1)
                if half == 0 and not (isinstance(i, int) and i == 0):
                    dve.wait_ge(y_written[par], 16 * i)
                for j in range(2):
                    g = rows[par][:, j, half * HALF:(half + 1) * HALF, bass.ds((2 * i + par) * 2 + (D + j), 1)]
                    dve.tensor_tensor(yt[par][:, j, half * HALF:(half + 1) * HALF, :],
                                      ps_y[j][:, 0:COLS].rearrange("p (n d) -> p n d", n=HALF),
                                      g.to_broadcast([P, HALF, D]), ALU.mult).then_inc(y_ready, 1)

            hidden(0, 0)

            def body(i, last):
                for n in range(4):
                    if n + 1 < 4 or not last:
                        hidden(4 * i + n + 1, (n + 1) % 2)
                    weigh(i, n)

            body(0, False)
            with dve.Fori(1, PAIRS // 2 - 1) as i:
                body(i, False)
            body(PAIRS // 2 - 1, True)

            def indices(i, n):
                if not (isinstance(i, int) and i == 0):
                    dve.wait_ge(gathered[n], 16 * TOPK * i)
                dve.tensor_copy(idx[n][:], slots[:, i, n]).then_inc(idx_ready, 1)

            def combine(i, n):
                m = NG * i + n
                dve.wait_ge(gathered[n], 16 * TOPK * (i + 1))
                dve.tensor_reduce(total[n][:], got[n][:].rearrange("p k d -> p d k"), AX.X, ALU.add
                                  ).then_inc(summed, 1)
                dve.wait_ge(summed, m + 1)
                if not (isinstance(i, int) and i == 0):
                    dve.wait_ge(stored[n], 16 * i)
                dve.tensor_tensor(res[n][:], total[n][:], H2[:, i, n, :], ALU.add).then_inc(res_ready, 1)

            for n in range(NG):
                indices(0, n)
            for n in range(NG):
                combine(0, n)
                indices(1, n)
            with dve.Fori(1, B - 1) as i:
                for n in range(NG):
                    combine(i, n)
                    indices(i + 1, n)
            for n in range(NG):
                combine(B - 1, n)

        @block.gpsimd
        def _(pool):
            pool.wait_ge(zero3_ready, 1).then_inc(pool_passed, 1)
            pool.dma_start(dram["rows_y"][0:1, :], zero[:]).then_inc(zero3_written, 16)

            def write(i, par):
                p = 2 * i + par
                pool.wait_ge(y_ready, 4 * p + 4).then_inc(pool_passed, 1)
                pool.dma_start(dram["rows_y"][1:1 + E * CAP, :].rearrange("(e p n) c -> p e n c", e=E, n=TILES)[
                    :, bass.ds(p * 2, 2)], yt[par][:]).then_inc(y_written[par], 16)

            with pool.Fori(0, PAIRS // 2) as i:
                write(i, 0)
                write(i, 1)
            pool.wait_ge(zero3_written, 16).then_inc(pool_passed, 1)
            for par in range(2):
                pool.wait_ge(y_written[par], 16 * (PAIRS // 2)).then_inc(pool_passed, 1)

            def gather(i, n):
                pool.wait_ge(idx_ready, NG * i + n + 1).then_inc(pool_passed, 1)
                if not (isinstance(i, int) and i == 0):
                    pool.wait_ge(summed, NG * (i - 1) + n + 1).then_inc(pool_passed, 1)
                for k in range(TOPK):
                    pool.indirect_dma_start(got[n][:, k, :], None, dram["rows_y"],
                                            bass.IndirectOffsetOnAxis(ap=idx[n][:, k:k + 1], axis=0)
                                            ).then_inc(gathered[n], 16)

            for n in range(NG):
                gather(0, n)
            with pool.Fori(1, B) as i:
                for n in range(NG):
                    gather(i, n)


def build(nc, io, out):
    dram = {
        "parts": nc.dram_tensor("parts_scratch", [4, 3, P, S], BF16, kind="Internal").ap(),
        "rows": nc.dram_tensor("maxima_scratch", [3, UNITS, P], BF16, kind="Internal").ap(),
        "rows_x": nc.dram_tensor("dispatched", [E * CAP, ROW], F32, kind="Internal").ap(),
        "rows_y": nc.dram_tensor("expert_out", [1 + E * CAP, D], F32, kind="Internal").ap(),
    }
    with ExitStack() as ctx:
        H2 = ctx.enter_context(nc.sbuf_tensor("H2", [P, B, QT, D], F32))
        Z2 = ctx.enter_context(nc.sbuf_tensor("Z2", [P, B, S], F32))
        slots = ctx.enter_context(nc.sbuf_tensor("slots", [P, B, QT, 8], I32))
        with nc.sbuf_tensor("X", [P, B, S + 2], F32) as X:
            tower(nc, io, X, dram["rows_x"])
            attention(nc, io, X, H2, Z2, slots, dram)
        experts(nc, io, H2, Z2, slots, dram, out)


def host_constants():
    f = np.float32
    place = np.arange(S - 1, -1, -1, dtype=f)
    freq = (f(1) / f(10000.0) ** (np.arange(0, D, 2, dtype=f) / f(D))).astype(f)
    angle = place[:, None] * freq[None, :]
    i = np.arange(P)
    return {
        "pe": np.concatenate([np.sin(angle), np.cos(angle)], -1).astype(f),
        "ident": np.eye(P, dtype=f),
        "iota": np.arange(P, dtype=f).reshape(P, 1),
        "grp": (i[:, None] // 32 == i[None] // 32).astype(f) / f(32),
        "tri": (i[:, None] < i[None]).astype(f),
        "base1": (np.arange(E) * CAP + 1).astype(f),
    }


def laid_out(inputs):
    a = {k: np.asarray(v) for k, v in inputs.items()}
    out = {k: a[k] for k in ("x", "L0_tok_emb", "L0_tok_ln0_g", "L0_tok_ln0_b", "L0_tok_W1", "L0_tok_W2",
                             "L0_attn_lambda_q1", "L0_attn_lambda_k1", "L0_attn_lambda_q2", "L0_attn_lambda_k2",
                             "L0_attn_gn_w", "L0_attn_gn_b", "L0_attn_out_b", "L0_ffn_bias")}
    for k in ("L0_tok_g1", "L0_tok_b1", "L0_tok_g2", "L0_tok_b2", "L0_attn_V_w", "L0_attn_out_w",
              "L0_ffn_router_w"):
        out[k] = a[k].T
    order = np.arange(D).reshape(HEADS, HD).T.reshape(-1)
    for k in ("Q1", "K1", "Q2", "K2"):
        out[f"L0_attn_{k}_w"] = a[f"L0_attn_{k}_w"][order].T
    for k in ("K1", "K2"):
        out[f"L0_attn_{k}_b"] = a[f"L0_attn_{k}_b"][order]
    gu = np.stack([a["L0_ffn_w_gate"], a["L0_ffn_w_up"]], 0).reshape(2, PAIRS, 2, FF, D)
    out["experts_gu"] = gu.transpose(1, 4, 0, 2, 3).reshape(PAIRS, D, 4 * FF)
    out["experts_down"] = a["L0_ffn_w_down"].transpose(0, 2, 1).reshape(PAIRS, 2 * FF, D)
    sh = np.stack([a["L0_ffn_shared_w_gate"], a["L0_ffn_shared_w_up"]], 0).reshape(2, 2 * FF, D)
    out["shared_gu"] = sh.transpose(2, 0, 1)
    out["shared_down"] = a["L0_ffn_shared_w_down"].transpose(0, 2, 1).reshape(2 * FF, D)
    out.update(host_constants())
    return {k: np.ascontiguousarray(v) for k, v in out.items()}


def kernel(**inputs):
    from concourse import bacc
    from concourse.bass_utils import run_bass_kernel_spmd

    nc = bacc.Bacc("TRN2", target_bir_lowering=False, num_devices=1)
    arrays, io = {}, {}
    for name, a in laid_out(inputs).items():
        arrays["in_" + name] = a
        io[name] = nc.dram_tensor("in_" + name, a.shape, mybir.dt.from_np(a.dtype), kind="ExternalInput").ap()
    out = nc.dram_tensor("out_0", [B, S, D], F32, kind="ExternalOutput").ap()
    build(nc, io, out)
    r = run_bass_kernel_spmd(nc, [arrays], core_ids=[0])
    return r.results[0]["out_0"]
```

```python
from contextlib import ExitStack

import numpy as np

import concourse.bass as bass
from concourse import mybir

F32 = mybir.dt.float32
BF16 = mybir.dt.bfloat16
I32 = mybir.dt.int32
ALU = mybir.AluOpType
ACT = mybir.ActivationFunctionType
AX = mybir.AxisListType

P = 128
B, S, D = 8, 512, 128
QT = S // P
LAYERS, TAPS, VOCAB, PAD = 8, 3, 33, 1
CONVS = 2 * B
E, TOPK, CAP, FF = 64, 6, 768, 64
ZROWS = 8
LAG = 3
RING = 4


def tower(nc, io, X, rows_x, later_loads, later_in, passed):
    with ExitStack() as ctx:
        def sb(name, shape, dt=F32):
            return ctx.enter_context(nc.sbuf_tensor(name, shape, dt))

        def sem(name):
            return ctx.enter_context(nc.semaphore(name))

        H = sb("hidden", [P, B, S + 2])
        W = sb("conv_w", [P, LAYERS, 2, TAPS, D])
        wmean = sb("wmean", [P, 2 * TAPS])
        gb = sb("gb", [P, 4, LAYERS])
        gb0 = sb("gb0", [P, 2])
        eps = sb("eps_tower", [P, 2])
        tok = sb("tok", [P, B, S], I32)
        onehot = sb("onehot", [P, 2, S])
        mask = sb("mask", [P, 2, S])
        emb = sb("emb", [P, D])
        pe = sb("pe", [P, QT, D])
        zrow = sb("zrow", [P, ZROWS * D])
        ident = sb("ident_t", [P, P])
        iota = sb("iota_t", [P, 1])
        sq = sb("sq", [P, 2, S])
        z = sb("z_tower", [P, RING, QT, D])
        sumsq = sb("sumsq", [P, RING, QT])
        std = sb("std", [P, RING, QT])
        rstd = sb("rstd", [P, RING, QT])
        stats = sb("stats", [P, QT, 6])
        mv = sb("mv", [P, 2, QT, 2])
        ps_y = [ctx.enter_context(nc.psum_tensor(f"y{n}", [P, QT, D], F32)) for n in range(RING)]
        ps_t = [ctx.enter_context(nc.psum_tensor(f"t{n}", [P, S], F32)) for n in range(RING)]

        zeros_ready = sem("zeros_ready")
        zeros_written = sem("zeros_written")
        consts_in = sem("consts_in")
        tokens_in = sem("tokens_in")
        weights_in = [sem(f"weights_in{n}") for n in range(LAYERS)]
        emb_zero = sem("emb_zero")
        emb_in = sem("emb_in")
        edges_zero = sem("edges_zero")
        onehot_ready = sem("onehot_ready")
        embedded = sem("embedded")
        stats_ready = sem("stats_ready")
        var_ready = sem("var_ready")
        std0_ready = sem("std0_ready")
        rstd0_ready = sem("rstd0_ready")
        z0_ready = sem("z0_ready")
        turned0 = sem("turned0")
        scaled0 = sem("scaled0")
        mask_ready = sem("mask_ready")
        wsum_ready = sem("wsum_ready")
        w_ready = sem("w_ready")
        conv_done = sem("conv_done")
        sq_ready = sem("sq_ready")
        sumsq_ready = sem("sumsq_ready")
        std_ready = sem("std_ready")
        rstd_ready = sem("rstd_ready")
        z_ready = sem("z_ready")
        turned = sem("turned")
        hidden_ready = sem("hidden_ready")
        x_ready = sem("x_ready")
        bias_added = sem("bias_added")

        sp_passed, pool_passed, act_passed, _ = passed
        block = ctx.enter_context(nc.Block())

        @block.sync
        def _(sp):
            sp.dma_start(tok[:], io["x"].unsqueeze(0).to_broadcast([P, B, S])).then_inc(tokens_in, 16)
            sp.dma_start(iota[:], io["iota"]).then_inc(consts_in, 16)
            sp.dma_start(ident[:], io["ident"]).then_inc(consts_in, 16)
            sp.dma_start(pe[:], io["pe"].rearrange("(q p) d -> p q d", p=P)).then_inc(consts_in, 16)
            sp.dma_start(gb0[:, 0:1], io["L0_tok_ln0_g"].unsqueeze(1)).then_inc(consts_in, 16)
            sp.dma_start(gb0[:, 1:2], io["L0_tok_ln0_b"].unsqueeze(1)).then_inc(consts_in, 16)
            for n, name in enumerate(("g1", "b1", "g2", "b2")):
                sp.dma_start(gb[:, n, :], io["L0_tok_" + name]).then_inc(consts_in, 16)
            sp.wait_ge(emb_zero, 1).then_inc(sp_passed, 1)
            sp.dma_start(emb[0:VOCAB, :], io["L0_tok_emb"]).then_inc(emb_in, 16)
            for layer in range(LAYERS):
                for c, name in enumerate(("W1", "W2")):
                    sp.dma_start(W[:, layer, c], io["L0_tok_" + name][layer].rearrange("t i o -> i t o")
                                 ).then_inc(weights_in[layer], 16)
            for dst, src in later_loads:
                sp.dma_start(dst, src).then_inc(later_in, 16)
            sp.wait_ge(zeros_ready, 1).then_inc(sp_passed, 1)
            filled = rows_x.rearrange("(a p r) c -> a p (r c)", p=P, r=ZROWS)
            with sp.Fori(0, E * CAP // (P * ZROWS)) as i:
                sp.dma_start(filled[i], zrow[:]).then_inc(zeros_written, 16)
            sp.wait_ge(zeros_written, 16 * (E * CAP // (P * ZROWS))).then_inc(sp_passed, 1)

        @block.gpsimd
        def _(pool):
            pool.memset(zrow[:], 0.0).then_inc(zeros_ready, 1)
            pool.memset(emb[:], 0.0).then_inc(emb_zero, 1)
            for buf in (X, H):
                for col in (0, S + 1):
                    pool.memset(buf[:, :, col:col + 1], 0.0).then_inc(edges_zero, 1)
            pool.memset(eps[:, 0:1], 1e-12).then_inc(edges_zero, 1)
            pool.memset(eps[:, 1:2], 1e-5).then_inc(edges_zero, 1)
            pool.wait_ge(consts_in, 16 * 9).then_inc(pool_passed, 1)
            with pool.Fori(0, LAYERS) as layer:
                for s in range(B):
                    pool.wait_ge(conv_done, layer * CONVS + s + 1).then_inc(pool_passed, 1)
                    pool.tensor_tensor(X[:, s, 1:S + 1], X[:, s, 1:S + 1],
                                       gb[:, 3, bass.ds(layer, 1)].to_broadcast([P, S]), ALU.add
                                       ).then_inc(bias_added, 1)

        @block.tensor
        def _(pe_):
            def transposes(s, src, dst, inc):
                for q in range(QT):
                    last = pe_.transpose(dst[:, q * P:(q + 1) * P], src[:, q, :], ident[:])
                last.then_inc(inc, 1)

            pe_.wait_ge(consts_in, 16 * 9)
            pe_.wait_ge(emb_in, 16)
            for s in range(B + 2):
                if s < B:
                    pe_.wait_ge(onehot_ready, s + 1)
                    if s >= RING:
                        pe_.wait_ge(z0_ready, s - RING + 1)
                    for q in range(QT):
                        pe_.matmul(ps_y[s % RING][:, q, :], onehot[:, s % 2, q * P:(q + 1) * P], emb[:],
                                   start=True, stop=False)
                        last = pe_.matmul(ps_y[s % RING][:, q, :], ident[:], pe[:, q, :],
                                          start=False, stop=True)
                    last.then_inc(embedded, 1)
                if s >= 2:
                    pe_.wait_ge(z0_ready, s - 1)
                    if s - 2 >= RING:
                        pe_.wait_ge(scaled0, s - 2 - RING + 1)
                    transposes(s - 2, z[:, (s - 2) % RING], ps_t[(s - 2) % RING], turned0)

            def conv(layer, c):
                n, s = c // B, c % B
                at = layer * CONVS + c
                src = H if n else X
                if n:
                    pe_.wait_ge(hidden_ready, layer * B + s + 1)
                else:
                    pe_.wait_ge(x_ready, layer * B + s + 1)
                    if s == 0:
                        pe_.wait_ge(w_ready, layer + 1)
                if isinstance(at, int) and at < RING:
                    pe_.wait_ge(z0_ready, B)
                else:
                    pe_.wait_ge(z_ready, at - RING + 1)
                for q in range(QT):
                    for t in range(TAPS):
                        last = pe_.matmul(ps_y[c % RING][:, q, :], src[:, s, q * P + t:q * P + t + P],
                                          W[:, layer, n, t, :], start=(t == 0), stop=(t == TAPS - 1))
                last.then_inc(conv_done, 1)

            def turn(layer, k, first=False):
                pe_.wait_ge(z_ready, layer * CONVS + k + 1)
                j = k - RING
                if j >= B:
                    pe_.wait_ge(x_ready, B + layer * B + j - B + 1)
                elif j >= 0:
                    pe_.wait_ge(hidden_ready, layer * B + j + 1)
                else:
                    pe_.wait_ge(x_ready, layer * B + B + j + 1)
                transposes(k % B, z[:, k % RING], ps_t[k % RING], turned)

            for c in range(LAG):
                conv(0, c)

            def body(layer, last):
                for k in range(CONVS):
                    turn(layer, k)
                    c = k + LAG
                    if c < CONVS:
                        conv(layer, c)
                    elif not last:
                        conv(layer + 1, c - CONVS)

            body(0, False)
            with pe_.Fori(1, LAYERS - 1) as layer:
                body(layer, False)
            body(LAYERS - 1, True)

        @block.scalar
        def _(act):
            act.wait_ge(consts_in, 16 * 9)
            act.wait_ge(edges_zero, 6)
            for s in range(B + 2):
                if s < B:
                    act.wait_ge(var_ready, s + 1)
                    act.activation(std[:, s % RING, :], mv[:, s % 2, :, 1], ACT.Sqrt, bias=eps[:, 0:1]
                                   ).then_inc(std0_ready, 1)
                if s >= 2:
                    act.wait_ge(turned0, s - 1)
                    act.activation(X[:, s - 2, 1:S + 1], ps_t[(s - 2) % RING][:], ACT.Identity,
                                   scale=gb0[:, 0:1], bias=gb0[:, 1:2]).then_inc(scaled0, 1)

            def square(layer, c):
                at = layer * CONVS + c
                act.wait_ge(conv_done, at + 1)
                if not (isinstance(at, int) and at < 2):
                    act.wait_ge(sumsq_ready, at - 1)
                act.activation(sq[:, c % 2, :], ps_y[c % RING][:].rearrange("p q d -> p (q d)"), ACT.Square
                               ).then_inc(sq_ready, 1)

            def root(layer, c):
                act.wait_ge(sumsq_ready, layer * CONVS + c + 1)
                act.activation(std[:, c % RING, :], sumsq[:, c % RING, :], ACT.Sqrt, scale=1.0 / D,
                               bias=eps[:, 1:2]).then_inc(std_ready, 1)

            square(0, 0)
            root(0, 0)
            square(0, 1)
            root(0, 1)
            square(0, 2)

            def body(layer, last):
                for k in range(CONVS):
                    c = k + LAG - 1
                    if c < CONVS:
                        root(layer, c)
                    elif not last:
                        root(layer + 1, c - CONVS)
                    if k < B:
                        act.wait_ge(turned, layer * CONVS + k + 1).then_inc(act_passed, 1)
                        act.activation(H[:, k, 1:S + 1], ps_t[k % RING][:], ACT.Relu,
                                       scale=gb[:, 0, bass.ds(layer, 1)], bias=gb[:, 1, bass.ds(layer, 1)]
                                       ).then_inc(hidden_ready, 1)
                    c = k + LAG
                    if c < CONVS:
                        square(layer, c)
                    elif not last:
                        square(layer + 1, c - CONVS)

            body(0, False)
            with act.Fori(1, LAYERS - 1) as layer:
                body(layer, False)
            body(LAYERS - 1, True)

        @block.vector
        def _(dve):
            dve.wait_ge(tokens_in, 16)
            dve.wait_ge(consts_in, 16 * 9)

            def masked(s):
                dve.wait_ge(scaled0, s + 1)
                dve.tensor_tensor(X[:, s, 1:S + 1], X[:, s, 1:S + 1], mask[:, s % 2, :], ALU.mult
                                  ).then_inc(x_ready, 1)

            for s in range(B + 3):
                if s < B:
                    if s >= 2:
                        dve.wait_ge(embedded, s - 1)
                    dve.tensor_scalar(onehot[:, s % 2, :], tok[:, s, :], iota[:, 0:1], None, ALU.is_equal
                                      ).then_inc(onehot_ready, 1)
                if 1 <= s <= B:
                    q_s = s - 1
                    dve.wait_ge(embedded, q_s + 1)
                    for q in range(QT):
                        dve.bn_stats(stats[:, q, :], ps_y[q_s % RING][:, q, :]).then_inc(stats_ready, 1)
                    dve.wait_ge(stats_ready, QT * (q_s + 1))
                    for q in range(QT):
                        last = dve.bn_aggr(mv[:, q_s % 2, q, :], stats[:, q, :])
                    last.then_inc(var_ready, 1)
                    dve.wait_ge(std0_ready, q_s + 1)
                    dve.reciprocal(rstd[:, q_s % RING, :], std[:, q_s % RING, :]).then_inc(rstd0_ready, 1)
                    dve.wait_ge(rstd0_ready, q_s + 1)
                    if q_s >= RING:
                        dve.wait_ge(turned0, q_s - RING + 1)
                    for q in range(QT):
                        last = dve.tensor_scalar(z[:, q_s % RING, q, :], ps_y[q_s % RING][:, q, :],
                                                 mv[:, q_s % 2, q, 0:1], rstd[:, q_s % RING, q:q + 1],
                                                 ALU.subtract, ALU.mult)
                    last.then_inc(z0_ready, 1)
                if s >= 3:
                    m = s - 3
                    dve.tensor_scalar(mask[:, m % 2, :], tok[:, m, :], float(PAD), None, ALU.not_equal
                                      ).then_inc(mask_ready, 1)
                    dve.wait_ge(mask_ready, m + 1)
                    masked(m)

            def centre(layer):
                w = W[:, layer].rearrange("p c t o -> p (c t) o")
                dve.tensor_reduce(wmean[:], w, AX.X, ALU.add).then_inc(wsum_ready, 1)
                dve.wait_ge(wsum_ready, layer * 2 + 1)
                dve.tensor_scalar(wmean[:], wmean[:], -1.0 / D, None, ALU.mult).then_inc(wsum_ready, 1)
                dve.wait_ge(wsum_ready, layer * 2 + 2)
                dve.tensor_tensor(w, w, wmean[:].unsqueeze(2).to_broadcast([P, 2 * TAPS, D]), ALU.add
                                  ).then_inc(w_ready, 1)

            def sums(layer, c):
                dve.wait_ge(sq_ready, layer * CONVS + c + 1)
                dve.tensor_reduce(sumsq[:, c % RING, :], sq[:, c % 2, :].rearrange("p (q d) -> p q d", q=QT),
                                  AX.X, ALU.add).then_inc(sumsq_ready, 1)

            def normalise(layer, c):
                at = layer * CONVS + c
                dve.wait_ge(std_ready, at + 1)
                dve.reciprocal(rstd[:, c % RING, :], std[:, c % RING, :]).then_inc(rstd_ready, 1)
                dve.wait_ge(rstd_ready, at + 1)
                if isinstance(at, int) and at < RING:
                    dve.wait_ge(turned0, B)
                else:
                    dve.wait_ge(turned, at - RING + 1)
                dve.tensor_tensor(z[:, c % RING], ps_y[c % RING][:],
                                  rstd[:, c % RING, :].unsqueeze(2).to_broadcast([P, QT, D]), ALU.mult
                                  ).then_inc(z_ready, 1)

            dve.wait_ge(weights_in[0], 32)
            centre(0)
            for n in range(1, LAYERS):
                dve.wait_ge(weights_in[n], 32)
            sums(0, 0)
            normalise(0, 0)
            sums(0, 1)
            normalise(0, 1)
            sums(0, 2)

            def body(layer, last):
                for k in range(CONVS):
                    c = k + LAG - 1
                    if c < CONVS:
                        normalise(layer, c)
                    elif not last:
                        normalise(layer + 1, c - CONVS)
                    if k >= B:
                        s = k - B
                        dve.wait_ge(turned, layer * CONVS + k + 1)
                        dve.wait_ge(bias_added, layer * B + s + 1)
                        dve.scalar_tensor_tensor(out=X[:, s, 1:S + 1], in0=ps_t[k % RING][:],
                                                 scalar=gb[:, 2, bass.ds(layer, 1)], in1=X[:, s, 1:S + 1],
                                                 op0=ALU.mult, op1=ALU.add).then_inc(x_ready, 1)
                    c = k + LAG
                    if c < CONVS:
                        sums(layer, c)
                    elif not last:
                        sums(layer + 1, c - CONVS)
                    if k == 4 and not last:
                        centre(layer + 1)

            body(0, False)
            with dve.Fori(1, LAYERS - 1) as layer:
                body(layer, False)
            body(LAYERS - 1, True)
HEADS, HD = 8, 16
MAPS = 2
GROUPS = 4
UNITS = 16
TERMS = 6
Q_PART = (0, 0, 1, 1, 0, 2)
K_PART = (0, 1, 0, 1, 2, 0)
KT = TERMS * HD
KM = KT + 3
NR = 14
FAR = float(1 << 17)


def attention_constants(nc, ctx):
    shapes = {"ident": [P, P], "wproj": [P, 4, D], "kbias": [P, 4], "wv": [P, D], "wout": [P, D], "outb": [P, D],
              "gnw": [P, 2], "grp": [P, P], "wrout": [P, E], "rbias": [P, E], "base1": [P, E], "tri_f": [P, P],
              "lam": [P, 4, HEADS], "shw": [P, 2, 2 * FF], "shd": [P, D]}
    return [ctx.enter_context(nc.sbuf_tensor(name, shape, F32)) for name, shape in shapes.items()]


def constant_loads(consts, io):
    ident, wproj, kbias, wv, wout, outb, gnw, grp, wrout, rbias, base1, tri_f, lam, shw, shd = consts
    loads = [(ident[:], io["ident"]), (wv[:], io["L0_attn_V_w"]), (wout[:], io["L0_attn_out_w"]),
             (grp[:], io["grp"]), (tri_f[:], io["tri"]), (wrout[:], io["L0_ffn_router_w"]),
             (outb[:], io["L0_attn_out_b"].unsqueeze(0).to_broadcast([P, D])),
             (rbias[:], io["L0_ffn_bias"].unsqueeze(0).to_broadcast([P, E])),
             (base1[:], io["base1"].unsqueeze(0).to_broadcast([P, E])),
             (gnw[:, 0:1], io["L0_attn_gn_w"].unsqueeze(1)), (gnw[:, 1:2], io["L0_attn_gn_b"].unsqueeze(1)),
             (kbias[:, 1:2], io["L0_attn_K1_b"].unsqueeze(1)), (kbias[:, 3:4], io["L0_attn_K2_b"].unsqueeze(1)),
             (shw[:], io["shared_gu"]), (shd[:], io["shared_down"])]
    for j, name in enumerate(("Q1", "K1", "Q2", "K2")):
        loads.append((wproj[:, j, :], io[f"L0_attn_{name}_w"]))
    for j, name in enumerate(("q1", "k1", "q2", "k2")):
        loads.append((lam[:, j, :], io["L0_attn_lambda_" + name].rearrange("h o -> o h").to_broadcast([P, HEADS])))
    return loads


consts_count = 16 * 23


def attention(nc, io, X, H2, Z2, picks, picked, dram, consts, consts_in, passed):
    with ExitStack() as ctx:
        def sb(name, shape, dt=F32):
            return ctx.enter_context(nc.sbuf_tensor(name, shape, dt))

        def sem(name):
            return ctx.enter_context(nc.semaphore(name))

        def bank(name, shape=(P, S)):
            return ctx.enter_context(nc.psum_tensor(name, list(shape), F32))

        ident, wproj, kbias, wv, wout, outb, gnw, grp, wrout, rbias, base1, tri_f, lam, shw, shd = consts
        tri = sb("tri", [P, P], BF16)
        ones = sb("ones", [P, P], BF16)
        neglam = sb("neglam", [P, HEADS])
        half = sb("half", [P, QT])
        hc = sb("hc", [P, S])
        htok = sb("htok", [P, QT, D])
        ztok = sb("ztok", [P, QT, D])
        zT = sb("zT", [P, S])
        fstats = sb("fstats", [P, QT, 6])
        fmv = sb("fmv", [P, QT, 2])
        fve = sb("fve", [P, QT])
        frstd = sb("frstd", [P, QT])
        q32 = sb("q32", [P, S])
        rest = sb("rest", [P, S])
        parts = sb("parts", [P, 2, 3, S], BF16)
        stack = [[sb(f"stack{p}{j}", [P, HEADS, S], BF16) for j in range(4)] for p in range(2)]
        Vx = [sb(f"Vx{p}", [P, QT, HEADS, 32]) for p in range(2)]
        nm = sb("nm", [P, 2, UNITS])
        mp = sb("mp", [UNITS, 3, P], BF16)
        mrest = sb("mrest", [UNITS, P])
        ex = sb("ex", [P, 8, S])
        act_g = ex[:, 0:2, :]
        hid = ex[:, 2:4, :]
        OT = sb("OT", [P, S])
        rsum = sb("rsum", [P, QT, 4])
        on = sb("on", [P, QT, 4, HD])
        otok = sb("otok", [P, QT, HEADS, HD])
        gst = sb("gst", [P, 6])
        gmv = sb("gmv", [P, 2])
        gm = sb("gm", [P, 1])
        gd = sb("gd", [P, 1])
        gv = sb("gv", [P, 1])
        gvar = sb("gvar", [P, 1])
        gve = sb("gve", [P, 1])
        grs = sb("grs", [P, 1])
        gsc = sb("gsc", [P, 1])
        gbi = sb("gbi", [P, 1])
        xn = sb("xn", [P, S])
        h2c = sb("h2c", [P, QT, D])
        tstats = sb("tstats", [P, QT, 6])
        tmv = sb("tmv", [P, QT, 2])
        tve = sb("tve", [P, QT])
        trstd = sb("trstd", [P, QT])
        R = [sb(f"R{p}", [P, QT, D]) for p in range(2)]
        z2c = sb("z2c", [P, S])
        logit = sb("logit", [P, QT, E])
        lmax = sb("lmax", [P, QT])
        lsum = sb("lsum", [P, QT])
        lrec = sb("lrec", [P, QT])
        prob = sb("prob", [P, QT, E + 2])
        top = sb("top", [P, QT, 8])
        repl = sb("repl", [P, QT, E + 2])
        M = sb("M", [P, QT, E], BF16)
        Macc = sb("Macc", [P, E], BF16)
        mnew = sb("mnew", [P, E])
        gsum = sb("gsum", [P, QT])
        grec = sb("grec", [P, QT])
        Mv = sb("Mv", [P, QT, E])
        gate = sb("gate", [P, QT, E])
        slot1 = sb("slot1", [P, QT, E])
        v8 = sb("v8", [P, QT, 8])
        none = sb("none", [P, QT, 8])
        freed = sb("freed", [P, 1])
        sidx = sb("sidx", [P, QT, 8], I32)

        ps_m = [bank(f"ps_m{i}") for i in range(2)]
        ps_e = [bank(f"ps_e{i}") for i in range(2)]
        ps_o = bank("ps_o")
        psA, psB, psC = bank("psA"), bank("psB"), bank("psC")

        names = """lam_ready consts_ready ones_rows vones hc_ready f_turned htok_ready f_stats
            f_var f_eps f_rstd resid_ready ztok_ready z_turned zT_ready proj_done hi_ready rest_ready
            mid_ready parts_ready v_done v_ready mxmm_done max_ready nm_turned mp_chain rows_ready
            rows_stored rows_loaded smm_done exp_done pv_done o_copied o_turned o_chain o_norm
            t_turned gn_chain gn_mean_done gn_var_done gn_var_out gn_eps gn_rstd gn_ready xn_ready y_done
            h2_ready h2_kept t_chain t_var t_eps t_rstd z2_ready z2_turned z2c_ready logit_done
            shifted_ready prob_exp r_chain mask_ready rank_done rows_out slots_ready scattered macc_ready t_chain2 rows_free
            sh_mm sh_gated sh_hid sh_down sh_added""".split()
        (lam_ready, consts_ready, ones_rows, vones, hc_ready, f_turned, htok_ready, f_stats,
         f_var, f_eps, f_rstd, resid_ready, ztok_ready, z_turned, zT_ready, proj_done, hi_ready, rest_ready,
         mid_ready, parts_ready, v_done, v_ready, mxmm_done, max_ready, nm_turned, mp_chain, rows_ready,
         rows_stored, rows_loaded, smm_done, exp_done, pv_done, o_copied, o_turned, o_chain, o_norm,
         t_turned, gn_chain, gn_mean_done, gn_var_done, gn_var_out, gn_eps, gn_rstd, gn_ready, xn_ready, y_done,
         h2_ready, h2_kept, t_chain, t_var, t_eps, t_rstd, z2_ready, z2_turned, z2c_ready, logit_done,
         shifted_ready, prob_exp, r_chain, mask_ready, rank_done, rows_out, slots_ready, scattered,
         macc_ready, t_chain2, rows_free, sh_mm, sh_gated, sh_hid, sh_down, sh_added) = [sem(n) for n in names]
        stored = [sem(f"stored{j}") for j in range(4)]
        loaded = [sem(f"loaded{j}") for j in range(4)]

        sp_passed, pool_passed, act_passed, dve_passed = passed
        block = ctx.enter_context(nc.Block())

        def has(t, g, stage):
            if not isinstance(t, int):
                return True
            n = 4 * t + g
            return {"F": t + 1 < B, "M": t < B, "Mprev": 0 <= n - 1 < 4 * B, "X": 0 <= n - 2 < 4 * B,
                    "Xprev": 0 <= n - 3 < 4 * B, "T": 0 <= t - 1 < B, "R": 0 <= t - 2 < B}[stage]

        def run(eng, step, first):
            first()

            def seq(t, par):
                for g in range(GROUPS):
                    step(t, g, par)
            seq(0, 0)
            seq(1, 1)
            seq(2, 0)
            with eng.Fori(1, 3) as i:
                seq(i * 2 + 1, 1)
                seq(i * 2 + 2, 0)
            for t in range(7, B + 2):
                seq(t, t % 2)

        def at(t, g, back):
            return 4 * t + g - back, t + (g - back) // 4, (g - back) % 4, ((g - back) // 4) % 2

        @block.sync
        def _(sp):
            def keep_parts(b, j):
                sp.wait_ge(parts_ready, 4 * b + j + 1).then_inc(sp_passed, 1)
                if not (isinstance(b, int) and b == 0):
                    sp.wait_ge(loaded[j], 16 * TERMS * b).then_inc(sp_passed, 1)
                sp.dma_start(dram["parts"][j].rearrange("a p t -> p a t"), parts[:, j % 2]).then_inc(stored[j], 16)

            def load_stack(b, j, par):
                sp.wait_ge(stored[j], 16 * b + 16).then_inc(sp_passed, 1)
                if isinstance(b, int) and b < 2:
                    pass
                else:
                    sp.wait_ge(smm_done, 4 * UNITS * (b - 1)).then_inc(sp_passed, 1)
                for k in range(TERMS):
                    part = (Q_PART, K_PART)[j % 2][k]
                    sp.dma_start(stack[par][j][k * HD:(k + 1) * HD],
                                 dram["parts"][j, part].rearrange("(d h) t -> d h t", h=HEADS)
                                 ).then_inc(loaded[j], 16)

            def first():
                keep_parts(0, 0)
                keep_parts(0, 1)
                load_stack(0, 0, 0)
                keep_parts(0, 2)
                load_stack(0, 1, 0)
                keep_parts(0, 3)
                load_stack(0, 2, 0)
                load_stack(0, 3, 0)

            def step(t, g, par):
                if has(t, g, "Mprev"):
                    n, b, gg, flip = at(t, g, 1)
                    p = par ^ flip
                    sp.wait_ge(rows_ready, n + 1).then_inc(sp_passed, 1)
                    if not (isinstance(n, int) and n == 0):
                        sp.wait_ge(rows_loaded, 32 * n).then_inc(sp_passed, 1)
                    sp.dma_start(dram["rows"].rearrange("a u t -> u a t"), mp[:]).then_inc(rows_stored, 16)
                    sp.wait_ge(rows_stored, 16 * n + 16).then_inc(sp_passed, 1)
                    for m in range(MAPS):
                        sp.dma_start(stack[p][2 * m][KT:KM, 2 * gg:2 * gg + 2, :],
                                     dram["rows"][:, 8 * m:8 * m + 8, :].rearrange("a (h q) t -> a h (q t)", h=2)
                                     ).then_inc(rows_loaded, 16)
                if has(t, g, "F"):
                    if g == 1:
                        keep_parts(t + 1, 0)
                        keep_parts(t + 1, 1)
                    if g == 2:
                        keep_parts(t + 1, 2)
                        load_stack(t + 1, 0, 1 - par)
                        load_stack(t + 1, 1, 1 - par)
                        keep_parts(t + 1, 3)
                    if g == 3:
                        load_stack(t + 1, 2, 1 - par)
                        load_stack(t + 1, 3, 1 - par)

            run(sp, step, first)

        @block.tensor
        def _(pe):
            def turn(dst, src, inc):
                for q in range(QT):
                    last = pe.transpose(dst[:, q * P:(q + 1) * P], src[:, q], ident[:])
                last.then_inc(inc, 1)

            def tokens(b):
                pe.wait_ge(hc_ready, b + 1)
                if not (isinstance(b, int) and b == 0):
                    pe.wait_ge(v_ready, b)
                turn(psA, hc[:].rearrange("p (q t) -> p q t", q=QT), f_turned)

            def features(b):
                pe.wait_ge(ztok_ready, b + 1)
                turn(psA, ztok, z_turned)

            def project(b, j):
                if j == 0:
                    pe.wait_ge(zT_ready, b + 1)
                else:
                    pe.wait_ge(hi_ready, 4 * b + j)
                pe.matmul(psA[:], wproj[:, j, :], zT[:], start=True, stop=True).then_inc(proj_done, 1)

            def values(b):
                pe.wait_ge(hi_ready, 4 * b + 4)
                for q in range(QT):
                    last = pe.matmul(psA[:, q * P:(q + 1) * P], zT[:, q * P:(q + 1) * P], wv[:],
                                     start=True, stop=True)
                last.then_inc(v_done, 1)

            pe.wait_ge(consts_in, consts_count)
            pe.wait_ge(consts_ready, 5)
            pe.wait_ge(vones, 4)

            def first():
                tokens(0)
                features(0)
                for j in range(4):
                    project(0, j)
                values(0)

            def step(t, g, par):
                xn_, xb, xg, xf = at(t, g, 2)
                pn, pb, pg, pf = at(t, g, 3)
                mn, mb, mg, mf = at(t, g, 1)

                def pv(n, b, gg, p, c):
                    pe.wait_ge(exp_done, UNITS * n + 4 * c + 4)
                    if c == 0:
                        if not (isinstance(n, int) and n == 0):
                            pe.wait_ge(o_copied, n)
                        if gg == 0:
                            pe.wait_ge(v_ready, b + 1)
                    for j in range(4):
                        last = pe.matmul(ps_o[32 * j:32 * j + 32, :], Vx[p][:, c, 2 * gg + j % 2, :],
                                         ex[:, 4 * (c % 2) + j, :], start=(c == 0), stop=(c == QT - 1))
                    last.then_inc(pv_done, 1)

                for u in range(UNITS):
                    if has(t, g, "M"):
                        if g == 0 and u % 8 == 0:
                            for j in (0, 1) if u == 0 else (2, 3):
                                pe.wait_ge(loaded[j], 16 * TERMS * (t + 1))
                        m = 4 * UNITS * t + UNITS * g + u
                        if not (isinstance(m, int) and m < 2):
                            pe.wait_ge(max_ready, m - 1)
                        mp_, h, q = u // 8, 2 * g + (u // 4) % 2, u % 4
                        pe.matmul(ps_m[u % 2][:], stack[par][2 * mp_][0:KT, h, q * P:(q + 1) * P],
                                  stack[par][2 * mp_ + 1][0:KT, h, :], start=True, stop=True
                                  ).then_inc(mxmm_done, 1)
                    if has(t, g, "X"):
                        p = par ^ xf
                        if u == 0:
                            pe.wait_ge(rows_loaded, 32 * xn_ + 32)
                            if isinstance(xn_, int) and xn_ == 0:
                                pe.wait_ge(ones_rows, 4)
                        e = UNITS * xn_ + u
                        if not (isinstance(e, int) and e < 2):
                            pe.wait_ge(exp_done, e - 1)
                        c, j = u // 4, u % 4
                        m_, h = j // 2, 2 * xg + j % 2
                        pe.matmul(ps_e[u % 2][:], stack[p][2 * m_ + 1][0:KM, h, c * P:(c + 1) * P],
                                  stack[p][2 * m_][0:KM, h, :], start=True, stop=True).then_inc(smm_done, 1)
                        if u in (6, 10, 14):
                            pv(xn_, xb, xg, p, (u - 6) // 4)
                    if u == 2 and has(t, g, "Xprev"):
                        pv(pn, pb, pg, par ^ pf, 3)
                    if u == 3 and has(t, g, "Mprev"):
                        pe.wait_ge(max_ready, UNITS * (mn + 1))
                        if not (isinstance(t, int) and 4 * t + g < 4):
                            pe.wait_ge(o_norm, pn)
                        if g == 3 and has(t, g, "T"):
                            pe.wait_ge(gn_chain, 4 * (t - 1) + 3)
                        pe.transpose(psB[0:UNITS, 0:P], nm[:, (g - 1) % 2, :], ident[:]).then_inc(nm_turned, 1)
                    if u == 8 and has(t, g, "Xprev"):
                        pe.wait_ge(o_copied, pn + 1)
                        if has(t, g, "Mprev"):
                            pe.wait_ge(rows_ready, mn + 1)
                        else:
                            pe.wait_ge(o_norm, pn)
                        if g == 3 and has(t, g, "T"):
                            pe.wait_ge(gn_var_out, t)
                        turn(psB, OT[:].rearrange("p (q t) -> p q t", q=QT), o_turned)
                    b = t + 1
                    if has(t, g, "F"):
                        if (g, u) == (0, 1):
                            tokens(b)
                        if (g, u) == (0, 13):
                            features(b)
                        if (g, u) == (1, 1):
                            project(b, 0)
                        if (g, u) == (1, 7):
                            project(b, 1)
                        if (g, u) == (1, 13):
                            project(b, 2)
                        if (g, u) == (2, 4):
                            project(b, 3)
                        if (g, u) == (3, 2):
                            values(b)
                    b = t - 1
                    if has(t, g, "T"):
                        if (g, u) == (2, 14):
                            pe.wait_ge(o_norm, 4 * b + 4)
                            if not (isinstance(b, int) and b == 0):
                                pe.wait_ge(rows_out, b)
                            turn(psC, otok[:].rearrange("p q h d -> p q (h d)"), t_turned)
                        if (g, u) == (3, 1):
                            pe.wait_ge(gn_chain, 4 * b + 2)
                            pe.matmul(psB[:, 0:1], grp[:], gmv[:, 0:1], start=True, stop=True
                                      ).then_inc(gn_mean_done, 1)
                        if (g, u) == (3, 6):
                            pe.wait_ge(gn_chain, 4 * b + 4)
                            if has(t, g, "Mprev"):
                                pe.wait_ge(rows_ready, mn + 1)
                            pe.matmul(psB[:, 0:1], grp[:], gv[:], start=True, stop=True
                                      ).then_inc(gn_var_done, 1)
                        if (g, u) == (3, 13):
                            pe.wait_ge(xn_ready, b + 1)
                            for q in range(QT):
                                last = pe.matmul(psC[:, q * P:(q + 1) * P], xn[:, q * P:(q + 1) * P], wout[:],
                                                 start=True, stop=True)
                            last.then_inc(y_done, 1)
                    b = t - 2
                    if has(t, g, "R"):
                        if (g, u) == (0, 5):
                            pe.wait_ge(z2_ready, b + 1)
                            turn(psC, R[par][:], z2_turned)
                        if (g, u) == (0, 9):
                            pe.wait_ge(z2c_ready, b + 1)
                            for q in range(QT):
                                last = pe.matmul(psC[:, q * E:(q + 1) * E], z2c[:, q * P:(q + 1) * P], wrout[:],
                                                 start=True, stop=True)
                            last.then_inc(logit_done, 1)
                        if (g, u) == (1, 4):
                            pe.wait_ge(mask_ready, b + 1)
                            pe.wait_ge(macc_ready, b + 1)
                            for q in range(QT):
                                out = psC[:, q * E:(q + 1) * E]
                                pe.matmul(out, ones[:], Macc[:], start=True, stop=False)
                                for q2 in range(q):
                                    pe.matmul(out, ones[:], M[:, q2, :], start=False, stop=False)
                                last = pe.matmul(out, tri[:], M[:, q, :], start=False, stop=True)
                            last.then_inc(rank_done, 1)

            run(pe, step, first)

            def shared_up(b):
                if b >= 2:
                    pe.wait_ge(sh_hid, b - 1)
                for ps, w in (((ps_m, ps_e)[b % 2][0], 0), ((ps_m, ps_e)[b % 2][1], 1)):
                    last = pe.matmul(ps[:], shw[:, w, :], Z2[:, b, :], start=True, stop=True)
                last.then_inc(sh_mm, 1)

            def shared_down(b):
                pe.wait_ge(sh_hid, b + 1)
                if b >= 2:
                    pe.wait_ge(sh_added, b - 1)
                for q in range(QT):
                    last = pe.matmul((psA, psB)[b % 2][:, q * P:(q + 1) * P],
                                     hid[:, b % 2, q * P:(q + 1) * P], shd[:], start=True, stop=True)
                last.then_inc(sh_down, 1)

            pe.wait_ge(z2c_ready, B)
            shared_up(0)
            for b in range(1, B):
                shared_up(b)
                shared_down(b - 1)
            shared_down(B - 1)

        @block.scalar
        def _(act):
            act.wait_ge(consts_in, consts_count)
            act.wait_ge(lam_ready, 1)
            act.activation(lam[:, 0, :], lam[:, 1, :], ACT.Exp).then_inc(lam_ready, 1)
            act.activation(lam[:, 2, :], lam[:, 3, :], ACT.Exp).then_inc(lam_ready, 1)

            def take(b):
                if not (isinstance(b, int) and b == 0):
                    act.wait_ge(f_turned, b).then_inc(act_passed, 1)
                act.activation(hc[:], X[:, b, 1:S + 1], ACT.Copy).then_inc(hc_ready, 1)

            def tokens(b):
                act.wait_ge(f_turned, b + 1)
                if not (isinstance(b, int) and b == 0):
                    act.wait_ge(resid_ready, b)
                    act.wait_ge(ztok_ready, b)
                act.activation(htok[:].rearrange("p q d -> p (q d)"), psA[:], ACT.Copy).then_inc(htok_ready, 1)

            def features(b):
                act.wait_ge(z_turned, b + 1)
                act.activation(zT[:], psA[:], ACT.Copy).then_inc(zT_ready, 1)

            def split(b, j):
                n = 4 * b + j
                act.wait_ge(proj_done, n + 1)
                if not (isinstance(n, int) and n == 0):
                    act.wait_ge(rest_ready, n)
                if not (isinstance(n, int) and n < 2):
                    act.wait_ge(stored[j ^ 2], (16 * b if j < 2 else 16 * b + 16))
                bias = {"bias": kbias[:, j:j + 1]} if j % 2 else {}
                f = ACT.Identity if j % 2 else ACT.Copy
                act.activation(q32[:], psA[:], f, **bias)
                act.activation(parts[:, j % 2, 0, :], psA[:], f, **bias).then_inc(hi_ready, 1)

            def middle(b, j):
                n = 4 * b + j
                act.wait_ge(rest_ready, n + 1)
                act.activation(parts[:, j % 2, 1, :], rest[:], ACT.Copy).then_inc(mid_ready, 1)

            def values(b, par):
                act.wait_ge(v_done, b + 1)
                if not (isinstance(b, int) and b < 2):
                    act.wait_ge(pv_done, 4 * QT * (b - 1))
                act.activation(Vx[par][:, :, :, 0:HD], psA[:].rearrange("p (q h d) -> p q h d", q=QT, h=HEADS),
                               ACT.Copy).then_inc(v_ready, 1)

            act.wait_ge(vones, 4)

            def first():
                take(0)
                tokens(0)
                features(0)
                for j in range(4):
                    split(0, j)
                    middle(0, j)
                values(0, 0)

            def step(t, g, par):
                xn_, xb, xg, xf = at(t, g, 2)
                pn, pb, pg, pf = at(t, g, 3)
                for u in range(UNITS):
                    if has(t, g, "X"):
                        e = UNITS * xn_ + u
                        c = u // 4
                        act.wait_ge(smm_done, e + 1)
                        if u % 4 == 0:
                            k = 4 * xn_ + c
                            if not (isinstance(k, int) and k < 2):
                                act.wait_ge(pv_done, k - 1)
                        act.activation(ex[:, 4 * (c % 2) + u % 4, :], ps_e[u % 2][:], ACT.Exp,
                                       scale=float(HD) ** -0.5).then_inc(exp_done, 1)
                    if u == 4 and has(t, g, "Xprev"):
                        act.wait_ge(pv_done, 4 * pn + 4)
                        if not (isinstance(pn, int) and pn == 0):
                            act.wait_ge(o_turned, pn)
                        act.activation(OT[:], ps_o[:], ACT.Copy).then_inc(o_copied, 1)
                    b = t + 1
                    if has(t, g, "F"):
                        if (g, u) == (0, 0):
                            take(b)
                        if (g, u) == (0, 3):
                            tokens(b)
                        if (g, u) == (0, 14):
                            features(b)
                        for j, when in enumerate(((1, 2), (1, 8), (1, 14), (2, 5))):
                            if (g, u) == when:
                                split(b, j)
                        for j, when in enumerate(((1, 5), (1, 11), (2, 1), (2, 8))):
                            if (g, u) == when:
                                middle(b, j)
                        if (g, u) == (3, 3):
                            values(b, 1 - par)
                    b = t - 1
                    if has(t, g, "T"):
                        if (g, u) == (3, 11):
                            act.wait_ge(gn_ready, b + 1)
                            act.activation(xn[:], psC[:], ACT.Identity, scale=gsc[:], bias=gbi[:]
                                           ).then_inc(xn_ready, 1)
                        if (g, u) == (3, 15):
                            act.wait_ge(h2_ready, b + 1).then_inc(act_passed, 1)
                            act.activation(H2[:, b].rearrange("p q d -> p (q d)"), h2c[:].rearrange("p q d -> p (q d)"),
                                           ACT.Copy).then_inc(h2_kept, 1)
                    b = t - 2
                    if has(t, g, "R"):
                        if (g, u) == (0, 7):
                            act.wait_ge(z2_turned, b + 1)
                            act.activation(z2c[:], psC[:], ACT.Copy)
                            act.activation(Z2[:, b], psC[:], ACT.Copy).then_inc(z2c_ready, 1)
                        if (g, u) == (0, 13):
                            act.wait_ge(shifted_ready, b + 1)
                            act.activation(prob[:, :, 0:E], logit[:], ACT.Exp).then_inc(prob_exp, 1)

            run(act, step, first)
            act.wait_ge(pv_done, 4 * QT * B)
            for b in range(B):
                act.wait_ge(sh_mm, b + 1)
                if b >= 2:
                    act.wait_ge(sh_hid, b - 1)
                act.activation(act_g[:, b % 2, :], (ps_m, ps_e)[b % 2][0][:], ACT.Silu).then_inc(sh_gated, 1)

        @block.gpsimd
        def _(pool):
            def ones_of(p, count):
                for j in (1, 3):
                    pool.memset(stack[p][j][KT:KM], 1.0).then_inc(ones_rows, 1)
                    count += 1
                    pool.wait_ge(ones_rows, count)

            ones_of(0, 0)
            for p in range(2):
                pool.memset(Vx[p][:, :, :, HD:32], 0.0).then_inc(vones, 1)
            for p in range(2):
                pool.wait_ge(vones, 2).then_inc(pool_passed, 1)
                pool.memset(Vx[p][:, :, :, HD:HD + 1], 1.0).then_inc(vones, 1)
            pool.memset(half[:], -0.5).then_inc(consts_ready, 1)
            pool.memset(ones[:], 1.0).then_inc(consts_ready, 1)
            pool.memset(Macc[:], 0.0).then_inc(consts_ready, 1)
            pool.memset(prob[:, :, E:E + 2], -1.0).then_inc(consts_ready, 1)
            pool.wait_ge(consts_in, consts_count).then_inc(pool_passed, 1)
            pool.tensor_copy(tri[:], tri_f[:]).then_inc(consts_ready, 1)
            pool.wait_ge(consts_ready, 5).then_inc(pool_passed, 1)

            def rstd_of(src, tmp, out, wait, n, count, eps_sem, done, width):
                pool.wait_ge(wait, count).then_inc(pool_passed, 1)
                pool.tensor_scalar(tmp, src, 1e-5, None, ALU.add).then_inc(eps_sem, 1)
                pool.wait_ge(eps_sem, n + 1).then_inc(pool_passed, 1)
                pool.tensor_tensor(out, tmp, half[:, 0:width], ALU.pow).then_inc(done, 1)

            def norm(b):
                rstd_of(fmv[:, :, 1], fve[:], frstd[:], f_var, b, b + 1, f_eps, f_rstd, QT)
                pool.tensor_tensor(H2[:, b], htok[:], outb[:].unsqueeze(1).to_broadcast([P, QT, D]), ALU.add
                                   ).then_inc(resid_ready, 1)

            def low(b, j):
                pool.wait_ge(mid_ready, 4 * b + j + 1).then_inc(pool_passed, 1)
                pool.tensor_tensor(parts[:, j % 2, 2, :], rest[:], parts[:, j % 2, 1, :], ALU.subtract
                                   ).then_inc(parts_ready, 1)

            def first():
                norm(0)
                for j in range(4):
                    low(0, j)
                pool.wait_ge(parts_ready, 4)
                ones_of(1, 2)

            def scatter(b, par, lo, hi):
                if lo == 0:
                    pool.wait_ge(slots_ready, b + 1).then_inc(pool_passed, 1)
                for i in range(lo, hi):
                    q, k = i // TOPK, i % TOPK
                    pool.indirect_dma_start(dram["rows_x"], bass.IndirectOffsetOnAxis(ap=sidx[:, q, k:k + 1], axis=0),
                                            R[par][:, q, :], None, bounds_check=E * CAP - 1, oob_is_err=False
                                            ).then_inc(scattered, 16)

            def step(t, g, par):
                F, T, routed, earlier = has(t, g, "F"), has(t, g, "T"), has(t, g, "R"), has(t - 1, g, "R")
                if g == 0:
                    if earlier:
                        scatter(t - 3, 1 - par, 12 if isinstance(t, int) and t == B + 1 else 19, 22)
                    if F:
                        norm(t + 1)
                    if earlier:
                        scatter(t - 3, 1 - par, 22, 24)
                if g == 1:
                    if earlier:
                        pool.wait_ge(scattered, 16 * QT * TOPK * (t - 2)).then_inc(pool_passed, 1)
                        pool.memset(freed[:], 0.0).then_inc(rows_free, 1)
                    if F:
                        low(t + 1, 0)
                        low(t + 1, 1)
                cuts = (0, 4, 10, 15, 19)
                if isinstance(t, int) and t == B:
                    cuts = (0, 2, 4, 8, 12)
                if g == 2:
                    if F:
                        low(t + 1, 2)
                    if routed:
                        scatter(t - 2, par, *cuts[0:2])
                    if F:
                        low(t + 1, 3)
                    if routed:
                        scatter(t - 2, par, *cuts[1:3])
                if g == 3:
                    b = t - 1
                    if routed:
                        scatter(t - 2, par, *cuts[2:4])
                    if T:
                        rstd_of(gvar[:], gve[:], grs[:], gn_var_out, b, b + 1, gn_eps, gn_rstd, 1)
                    if routed:
                        scatter(t - 2, par, *cuts[3:5])
                    if T:
                        rstd_of(tmv[:, :, 1], tve[:], trstd[:], t_var, b, b + 1, t_eps, t_rstd, QT)

            run(pool, step, first)
            scatter(B - 1, (B - 1) % 2, 19, 24)
            pool.wait_ge(scattered, 16 * QT * TOPK * B)

        @block.vector
        def _(dve):
            dve.wait_ge(consts_in, consts_count)
            dve.tensor_tensor(lam[:, 1, :], lam[:, 0, :], lam[:, 1, :], ALU.mult)
            dve.tensor_tensor(lam[:, 3, :], lam[:, 2, :], lam[:, 3, :], ALU.mult).then_inc(lam_ready, 1)
            dve.wait_ge(lam_ready, 3)
            dve.tensor_tensor(neglam[:], lam[:, 2, :], lam[:, 0, :], ALU.subtract).then_inc(lam_ready, 1)
            dve.wait_ge(lam_ready, 4)
            dve.tensor_scalar(neglam[:], neglam[:], -0.2, None, ALU.add).then_inc(lam_ready, 1)
            dve.wait_ge(lam_ready, 5)
            dve.wait_ge(consts_ready, 5)
            dve.memset(M[:], 0.0).then_inc(rows_free, 2)

            def stats(b):
                dve.wait_ge(htok_ready, b + 1)
                for q in range(QT):
                    last = dve.bn_stats(fstats[:, q, :], htok[:, q, :])
                last.then_inc(f_stats, 1)
                dve.wait_ge(f_stats, b + 1).then_inc(dve_passed, 1)
                for q in range(QT):
                    last = dve.bn_aggr(fmv[:, q, :], fstats[:, q, :])
                last.then_inc(f_var, 1)

            def norm(b):
                dve.wait_ge(f_rstd, b + 1)
                if not (isinstance(b, int) and b == 0):
                    dve.wait_ge(z_turned, b)
                for q in range(QT):
                    last = dve.tensor_scalar(ztok[:, q, :], htok[:, q, :], fmv[:, q, 0:1], frstd[:, q:q + 1],
                                             ALU.subtract, ALU.mult)
                last.then_inc(ztok_ready, 1)

            def take_rest(b, j):
                n = 4 * b + j
                dve.wait_ge(hi_ready, n + 1)
                if not (isinstance(n, int) and n == 0):
                    dve.wait_ge(parts_ready, n)
                dve.tensor_tensor(rest[:], q32[:], parts[:, j % 2, 0, :], ALU.subtract).then_inc(rest_ready, 1)

            def first():
                stats(0)
                norm(0)
                for j in range(4):
                    take_rest(0, j)

            def split_rows(n):
                dve.wait_ge(nm_turned, n + 1)
                if not (isinstance(n, int) and n == 0):
                    dve.wait_ge(rows_stored, 16 * n)
                src = psB[0:UNITS, 0:P]
                dve.tensor_copy(mp[:, 0, :], src).then_inc(mp_chain, 1)
                dve.wait_ge(mp_chain, 3 * n + 1)
                dve.tensor_tensor(mrest[:], src, mp[:, 0, :], ALU.subtract).then_inc(mp_chain, 1)
                dve.wait_ge(mp_chain, 3 * n + 2)
                dve.tensor_copy(mp[:, 1, :], mrest[:]).then_inc(mp_chain, 1)
                dve.wait_ge(mp_chain, 3 * n + 3)
                dve.tensor_tensor(mp[:, 2, :], mrest[:], mp[:, 1, :], ALU.subtract).then_inc(rows_ready, 1)

            def output(n, gg):
                dve.wait_ge(o_turned, n + 1)
                o = psB[:].rearrange("p (q j c) -> p q j c", q=QT, j=4)
                dve.reciprocal(rsum[:], o[:, :, :, HD]).then_inc(o_chain, 1)
                dve.wait_ge(o_chain, 3 * n + 1)
                dve.tensor_tensor(rsum[:, :, 2:4], rsum[:, :, 2:4],
                                  neglam[:, 2 * gg:2 * gg + 2].unsqueeze(1).to_broadcast([P, QT, 2]), ALU.mult
                                  ).then_inc(o_chain, 1)
                dve.wait_ge(o_chain, 3 * n + 2)
                dve.tensor_tensor(on[:], o[:, :, :, 0:HD], rsum[:].unsqueeze(3).to_broadcast([P, QT, 4, HD]),
                                  ALU.mult).then_inc(o_chain, 1)
                dve.wait_ge(o_chain, 3 * n + 3)
                dve.tensor_tensor(otok[:, :, 2 * gg:2 * gg + 2, :], on[:, :, 0:2, :], on[:, :, 2:4, :], ALU.add
                                  ).then_inc(o_norm, 1)

            def step(t, g, par):
                pn, pb, pg, pf = at(t, g, 3)
                mn, mb, mg, mf = at(t, g, 1)
                for u in range(UNITS):
                    if has(t, g, "M"):
                        m = 4 * UNITS * t + UNITS * g + u
                        dve.wait_ge(mxmm_done, m + 1)
                        if u == 0 and not (isinstance(t, int) and 4 * t + g < 2):
                            dve.wait_ge(nm_turned, mn)
                        dve.tensor_reduce(nm[:, g % 2, u:u + 1], ps_m[u % 2][:], AX.X, ALU.max, negate=True
                                          ).then_inc(max_ready, 1)
                    if u == 4 and has(t, g, "Mprev"):
                        split_rows(mn)
                    if u == 10 and has(t, g, "Xprev"):
                        if pg == 0 and not (isinstance(t, int) and pb == 0):
                            dve.wait_ge(t_turned, pb)
                        output(pn, pg)
                    b = t + 1
                    if has(t, g, "F"):
                        if (g, u) == (0, 5):
                            stats(b)
                        if (g, u) == (0, 9):
                            norm(b)
                        for j, when in enumerate(((1, 4), (1, 9), (1, 15), (2, 7))):
                            if (g, u) == when:
                                take_rest(b, j)
                    b = t - 1
                    if has(t, g, "T"):
                        if (g, u) == (2, 15):
                            dve.wait_ge(t_turned, b + 1)
                            dve.bn_stats(gst[:], psC[:]).then_inc(gn_chain, 1)
                            dve.wait_ge(gn_chain, 4 * b + 1).then_inc(dve_passed, 1)
                            dve.bn_aggr(gmv[:], gst[:]).then_inc(gn_chain, 1)
                        if (g, u) == (3, 2):
                            dve.wait_ge(gn_mean_done, b + 1)
                            dve.tensor_copy(gm[:], psB[:, 0:1])
                            dve.tensor_tensor(gd[:], gmv[:, 0:1], psB[:, 0:1], ALU.subtract).then_inc(gn_chain, 1)
                            dve.wait_ge(gn_chain, 4 * b + 3)
                            dve.scalar_tensor_tensor(out=gv[:], in0=gd[:], scalar=gd[:], in1=gmv[:, 1:2],
                                                     op0=ALU.mult, op1=ALU.add).then_inc(gn_chain, 1)
                        if (g, u) == (3, 7):
                            dve.wait_ge(gn_var_done, b + 1)
                            dve.tensor_copy(gvar[:], psB[:, 0:1]).then_inc(gn_var_out, 1)
                        if (g, u) == (3, 9):
                            dve.wait_ge(gn_rstd, b + 1)
                            dve.tensor_tensor(gsc[:], grs[:], gnw[:, 0:1], ALU.mult).then_inc(t_chain, 1)
                            dve.wait_ge(t_chain, 3 * b + 1)
                            dve.tensor_tensor(gbi[:], gm[:], gsc[:], ALU.mult).then_inc(t_chain, 1)
                            dve.wait_ge(t_chain, 3 * b + 2)
                            dve.tensor_tensor(gbi[:], gnw[:, 1:2], gbi[:], ALU.subtract).then_inc(gn_ready, 1)
                        if (g, u) == (3, 14):
                            dve.wait_ge(y_done, b + 1)
                            dve.wait_ge(resid_ready, b + 1)
                            if not (isinstance(b, int) and b == 0):
                                dve.wait_ge(h2_kept, b)
                            dve.tensor_tensor(h2c[:], psC[:].rearrange("p (q d) -> p q d", q=QT), H2[:, b], ALU.add
                                              ).then_inc(h2_ready, 1)
                            dve.wait_ge(h2_ready, b + 1)
                            for q in range(QT):
                                last = dve.bn_stats(tstats[:, q, :], h2c[:, q, :])
                            last.then_inc(t_chain, 1)
                            dve.wait_ge(t_chain, 3 * b + 3).then_inc(dve_passed, 1)
                            for q in range(QT):
                                last = dve.bn_aggr(tmv[:, q, :], tstats[:, q, :])
                            last.then_inc(t_var, 1)
                    b = t - 2
                    if has(t, g, "R"):
                        if (g, u) == (0, 2):
                            dve.wait_ge(t_rstd, b + 1)
                            dve.wait_ge(rows_free, b + 1)
                            for q in range(QT):
                                last = dve.tensor_scalar(R[par][:, q, :], h2c[:, q, :], tmv[:, q, 0:1],
                                                         trstd[:, q:q + 1], ALU.subtract, ALU.mult)
                            last.then_inc(z2_ready, 1)
                            dve.tensor_reduce(mnew[:], M[:].rearrange("p q e -> p e q"), AX.X, ALU.add
                                              ).then_inc(t_chain2, 1)
                            dve.wait_ge(t_chain2, b + 1)
                            dve.tensor_tensor(Macc[:], Macc[:], mnew[:], ALU.add).then_inc(macc_ready, 1)
                        if (g, u) == (0, 11):
                            dve.wait_ge(logit_done, b + 1)
                            dve.tensor_tensor(logit[:], psC[:, 0:QT * E].rearrange("p (q e) -> p q e", q=QT),
                                              rbias[:].unsqueeze(1).to_broadcast([P, QT, E]), ALU.add
                                              ).then_inc(r_chain, 1)
                            dve.wait_ge(r_chain, NR * b + 1)
                            dve.tensor_reduce(lmax[:], logit[:], AX.X, ALU.max).then_inc(r_chain, 1)
                            dve.wait_ge(r_chain, NR * b + 2)
                            dve.tensor_tensor(logit[:], logit[:], lmax[:].unsqueeze(2).to_broadcast([P, QT, E]),
                                              ALU.subtract).then_inc(shifted_ready, 1)
                        if (g, u) == (0, 15):
                            dve.wait_ge(prob_exp, b + 1)
                            pr = prob[:, :, 0:E]
                            dve.tensor_reduce(lsum[:], pr, AX.X, ALU.add).then_inc(r_chain, 1)
                            dve.wait_ge(r_chain, NR * b + 3)
                            dve.reciprocal(lrec[:], lsum[:]).then_inc(r_chain, 1)
                            dve.wait_ge(r_chain, NR * b + 4)
                            dve.tensor_tensor(pr, pr, lrec[:].unsqueeze(2).to_broadcast([P, QT, E]), ALU.mult
                                              ).then_inc(r_chain, 1)
                            dve.wait_ge(r_chain, NR * b + 5).then_inc(dve_passed, 1)
                            for q in range(QT):
                                last = dve.max(top[:, q, :], prob[:, q, 0:E])
                            last.then_inc(r_chain, 1)
                            dve.wait_ge(r_chain, NR * b + 6)
                            dve.tensor_reduce(gsum[:], top[:, :, 0:TOPK], AX.X, ALU.add)
                            dve.memset(top[:, :, TOPK:8], -1.0).then_inc(r_chain, 1)
                            dve.wait_ge(r_chain, NR * b + 7).then_inc(dve_passed, 1)
                            for q in range(QT):
                                last = dve.match_replace(repl[:, q, :], top[:, q, :], prob[:, q, :], -2.0)
                            last.then_inc(r_chain, 1)
                            dve.wait_ge(r_chain, NR * b + 8)
                            dve.tensor_tensor(M[:], repl[:, :, 0:E], pr, ALU.not_equal).then_inc(mask_ready, 1)
                        if (g, u) == (1, 1):
                            dve.tensor_scalar(gsum[:], gsum[:], 1e-9, None, ALU.add).then_inc(r_chain, 1)
                            dve.wait_ge(r_chain, NR * b + 9)
                            dve.reciprocal(grec[:], gsum[:]).then_inc(r_chain, 1)
                            dve.wait_ge(r_chain, NR * b + 10)
                            dve.tensor_tensor(gate[:], prob[:, :, 0:E],
                                              grec[:].unsqueeze(2).to_broadcast([P, QT, E]), ALU.mult
                                              ).then_inc(r_chain, 1)
                            dve.wait_ge(r_chain, NR * b + 11)
                        if (g, u) == (1, 6):
                            dve.wait_ge(rank_done, b + 1)
                            rank = psC[:, 0:QT * E].rearrange("p (q e) -> p q e", q=QT)
                            dve.scalar_tensor_tensor(out=Mv[:], in0=rank, scalar=float(CAP), in1=M[:],
                                                     op0=ALU.is_lt, op1=ALU.mult)
                            dve.tensor_tensor(slot1[:], rank, base1[:].unsqueeze(1).to_broadcast([P, QT, E]),
                                              ALU.add).then_inc(rows_out, 1)
                            dve.wait_ge(rows_out, b + 1)
                            dve.tensor_tensor(slot1[:], slot1[:], Mv[:], ALU.mult).then_inc(r_chain, 1)
                            dve.tensor_tensor(picks[:, b, :, 1, :], gate[:], Mv[:], ALU.mult)
                            dve.wait_ge(r_chain, NR * b + 12).then_inc(dve_passed, 1)
                            for q in range(QT):
                                last = dve.max(v8[:, q, :], slot1[:, q, :])
                            last.then_inc(r_chain, 1)
                            dve.wait_ge(r_chain, NR * b + 13)
                            dve.tensor_copy(picks[:, b, :, 0, :], slot1[:])
                            dve.tensor_copy(picked[:, b], v8[:])
                            dve.tensor_scalar(none[:], v8[:], 0.0, FAR, ALU.is_equal, ALU.mult).then_inc(r_chain, 1)
                            dve.wait_ge(r_chain, NR * b + 14)
                            dve.wait_ge(rows_free, b + 2)
                            dve.scalar_tensor_tensor(out=sidx[:], in0=v8[:], scalar=-1.0, in1=none[:],
                                                     op0=ALU.add, op1=ALU.add).then_inc(slots_ready, 1)

            run(dve, step, first)

            def shared_hidden(b):
                dve.wait_ge(sh_gated, b + 1)
                if b >= 2:
                    dve.wait_ge(sh_down, b - 1)
                dve.tensor_tensor(hid[:, b % 2, :], (ps_m, ps_e)[b % 2][1][:], act_g[:, b % 2, :], ALU.mult
                                  ).then_inc(sh_hid, 1)

            def shared_add(b):
                dve.wait_ge(sh_down, b + 1)
                dve.scalar_tensor_tensor(out=H2[:, b].rearrange("p q d -> p (q d)"), in0=(psA, psB)[b % 2][:],
                                         scalar=1.0 / 2, in1=H2[:, b].rearrange("p q d -> p (q d)"),
                                         op0=ALU.mult, op1=ALU.add).then_inc(sh_added, 1)

            shared_hidden(0)
            dve.wait_ge(h2_kept, B)
            for b in range(1, B):
                shared_hidden(b)
                shared_add(b - 1)
            shared_add(B - 1)
PAIRS = E // 2
TILES = CAP // P
HALF = TILES // 2
COLS = HALF * P
AHEAD = 4


def experts(nc, io, H2, picks, picked, dram, ident, out, passed):
    with ExitStack() as ctx:
        def sb(name, shape, dt=F32):
            return ctx.enter_context(nc.sbuf_tensor(name, shape, dt))

        def sem(name):
            return ctx.enter_context(nc.semaphore(name))

        rows = [sb(f"rows{i}", [P, 2, TILES, D]) for i in range(AHEAD)]
        wgu = [sb(f"wgu{i}", [P, 2, 2, FF]) for i in range(AHEAD)]
        wdn = [sb(f"wdn{i}", [P, D]) for i in range(AHEAD)]
        xT = sb("xT3", [P, 2, 2, COLS])
        act_g = sb("act_g", [P, 2, S])
        hid = sb("hid", [P, 2, S])
        yt = [sb(f"yt{i}", [P, 2, TILES, D]) for i in range(AHEAD)]
        zero = sb("zero3", [1, D])
        NG = 4
        got = [sb(f"got{i}", [P, TOPK, D]) for i in range(NG)]
        idx = [sb(f"idx{i}", [P, 8], I32) for i in range(NG)]
        same = sb("same", [P, TOPK, E])
        taken = sb("taken", [P, TOPK, E])
        share = sb("share", [P, B * QT, TOPK])
        gated_rows = sb("gated_rows", [P, TOPK, D])
        total = [sb(f"total{i}", [P, D]) for i in range(NG)]
        res = [sb(f"res{i}", [P, D]) for i in range(NG)]

        ps_x = [ctx.enter_context(nc.psum_tensor(f"px{i}", [P, S], F32)) for i in range(2)]
        ps_g = [ctx.enter_context(nc.psum_tensor(f"pg{i}", [P, S], F32)) for i in range(2)]
        ps_u = [ctx.enter_context(nc.psum_tensor(f"pu{i}", [P, S], F32)) for i in range(2)]
        ps_y = [ctx.enter_context(nc.psum_tensor(f"py{i}", [P, S], F32)) for i in range(2)]

        (zero3_ready, zero3_written, x_turned, x_out,
         gu_done, gated, hid_ready, down_done, y_ready) = [sem(n) for n in (
             "zero3_ready", "zero3_written", "x_turned", "x_out", "gu_done", "gated", "hid_ready", "down_done", "y_ready")]
        rows_in = [sem(f"rows_in{i}") for i in range(AHEAD)]
        y_written = [sem(f"y_written{i}") for i in range(AHEAD)]
        share_chain = sem("share_chain")
        weighed = sem("weighed")
        idx_ready = sem("idx_ready")
        gathered = [sem(f"gathered{i}") for i in range(NG)]
        summed = sem("summed")
        res_ready = sem("res_ready")
        stored = [sem(f"res_stored{i}") for i in range(NG)]

        LOADS = 16 * 3
        UB = 2 * AHEAD
        sp_passed, pool_passed, _, dve_passed = passed
        block = ctx.enter_context(nc.Block())

        @block.sync
        def _(sp):
            def load_rows(p, par):
                sp.dma_start(rows[par][:], dram["rows_x"].rearrange("(e p n) c -> p e n c", e=E, n=TILES)[
                    :, bass.ds(p * 2, 2)]).then_inc(rows_in[par], 16)

            def load_weights(p, par):
                sp.dma_start(wgu[par][:].rearrange("p a b f -> p (a b f)"), io["experts_gu"][p]).then_inc(rows_in[par], 16)
                sp.dma_start(wdn[par][:], io["experts_down"][p]).then_inc(rows_in[par], 16)

            for p in range(AHEAD):
                load_rows(p, p)
                load_weights(p, p)
            sp.wait_ge(zero3_ready, 1)
            sp.dma_start(dram["rows_y"][0:1, :], zero[:]).then_inc(zero3_written, 16)

            def following(p, par, more):
                if more:
                    sp.wait_ge(x_out, 4 * p + 4).then_inc(sp_passed, 1)
                    load_rows(p + AHEAD, par)
                    sp.wait_ge(down_done, 2 * p + 2).then_inc(sp_passed, 1)
                    load_weights(p + AHEAD, par)
                sp.wait_ge(y_ready, 4 * p + 4).then_inc(sp_passed, 1)
                sp.dma_start(dram["rows_y"][1:1 + E * CAP, :].rearrange("(e p n) c -> p e n c", e=E, n=TILES)[
                    :, bass.ds(p * 2, 2)], yt[par][:]).then_inc(y_written[par], 16)

            with sp.Fori(0, PAIRS // AHEAD - 1) as i:
                for n in range(AHEAD):
                    following(i * AHEAD + n, n, True)
            for n in range(AHEAD):
                following(PAIRS - AHEAD + n, n, False)

        @block.tensor
        def _(pe):
            def up(v, half, par):
                pe.wait_ge(x_out, 2 * v + 2)
                if not (isinstance(v, int) and v < 2):
                    pe.wait_ge(hid_ready, v - 1)
                for w, ps in enumerate((ps_g, ps_u)):
                    for j in range(2):
                        last = pe.matmul(ps[half][FF * j:FF * j + FF, 0:COLS], wgu[par][:, w, j, :],
                                         xT[:, half, j, :], start=True, stop=True)
                last.then_inc(gu_done, 1)

            def down(v, half, par):
                pe.wait_ge(hid_ready, v + 1)
                if not (isinstance(v, int) and v == 0):
                    pe.wait_ge(y_ready, 2 * v)
                for k in range(HALF):
                    for j in range(2):
                        last = pe.matmul(ps_y[j][:, k * P:(k + 1) * P],
                                         hid[FF * j:FF * j + FF, half, k * P:(k + 1) * P],
                                         wdn[par][FF * j:FF * j + FF, :], start=True, stop=True)
                last.then_inc(down_done, 1)

            def turn(i, n):
                v, half, par = UB * i + n, n % 2, (n // 2) % AHEAD
                if half == 0:
                    pe.wait_ge(rows_in[par], LOADS * (i + n // UB) + LOADS)
                for j in range(2):
                    m = 2 * v + j
                    if not (isinstance(m, int) and m < 2):
                        pe.wait_ge(x_out, m - 1)
                    for k in range(HALF):
                        last = pe.transpose(ps_x[j][:, k * P:(k + 1) * P],
                                            rows[par][:, j, half * HALF + k, :], ident[:])
                    last.then_inc(x_turned, 1)

            turn(0, 0)
            turn(0, 1)
            up(0, 0, 0)

            def body(i, last):
                for n in range(UB):
                    if n + 2 < UB or not last:
                        turn(i, n + 2)
                    if n + 1 < UB or not last:
                        up(UB * i + n + 1, (n + 1) % 2, ((n + 1) // 2) % AHEAD)
                    down(UB * i + n, n % 2, n // 2)

            with pe.Fori(0, PAIRS // AHEAD - 1) as i:
                body(i, False)
            body(PAIRS // AHEAD - 1, True)

        @block.scalar
        def _(act):
            def take(v, half):
                for j in range(2):
                    act.wait_ge(x_turned, 2 * v + j + 1)
                    if j == 0 and not (isinstance(v, int) and v < 2):
                        act.wait_ge(gu_done, v - 1)
                    act.activation(xT[:, half, j, :], ps_x[j][:, 0:COLS], ACT.Copy).then_inc(x_out, 1)

            def gate(v, half):
                act.wait_ge(gu_done, v + 1)
                if not (isinstance(v, int) and v < 2):
                    act.wait_ge(hid_ready, v - 1)
                act.activation(act_g[:, half, 0:COLS], ps_g[half][:, 0:COLS], ACT.Silu).then_inc(gated, 1)

            take(0, 0)
            take(1, 1)
            gate(0, 0)

            def body(i, last):
                for n in range(UB):
                    if n + 2 < UB or not last:
                        take(UB * i + n + 2, n % 2)
                    if n + 1 < UB or not last:
                        gate(UB * i + n + 1, (n + 1) % 2)

            with act.Fori(0, PAIRS // AHEAD - 1) as i:
                body(i, False)
            body(PAIRS // AHEAD - 1, True)

            def keep(i, n):
                act.wait_ge(res_ready, NG * i + n + 1)
                act.dma_start(out[i, n * P:(n + 1) * P, :], res[n][:]).then_inc(stored[n], 16)

            with act.Fori(0, B) as i:
                for n in range(NG):
                    keep(i, n)
            for n in range(NG):
                act.wait_ge(stored[n], 16 * B)

        @block.vector
        def _(dve):
            dve.memset(zero[:], 0.0).then_inc(zero3_ready, 1)

            def hidden(v, half):
                dve.wait_ge(gated, v + 1)
                if not (isinstance(v, int) and v < 2):
                    dve.wait_ge(down_done, v - 1)
                dve.tensor_tensor(hid[:, half, 0:COLS], ps_u[half][:, 0:COLS], act_g[:, half, 0:COLS],
                                  ALU.mult).then_inc(hid_ready, 1)

            def leave(i, n):
                v, half, par = UB * i + n, n % 2, n // 2
                dve.wait_ge(down_done, v + 1)
                if half == 0 and not (isinstance(i, int) and i == 0):
                    dve.wait_ge(y_written[par], 16 * i)
                for j in range(2):
                    dve.tensor_copy(yt[par][:, j, half * HALF:(half + 1) * HALF, :],
                                    ps_y[j][:, 0:COLS].rearrange("p (n d) -> p n d", n=HALF)).then_inc(y_ready, 1)

            flat = picks[:].rearrange("p b q a e -> p (b q) a e")
            largest = picked[:].rearrange("p b q k -> p (b q) k")

            def shares(tile):
                if not (isinstance(tile, int) and tile == 0):
                    dve.wait_ge(share_chain, 3 * tile).then_inc(dve_passed, 1)
                dve.tensor_tensor(same[:], flat[:, tile, 0, :].unsqueeze(1).to_broadcast([P, TOPK, E]),
                                  largest[:, tile, 0:TOPK].unsqueeze(2).to_broadcast([P, TOPK, E]), ALU.is_equal
                                  ).then_inc(share_chain, 1)
                dve.wait_ge(share_chain, 3 * tile + 1)
                dve.tensor_tensor(taken[:], same[:], flat[:, tile, 1, :].unsqueeze(1).to_broadcast([P, TOPK, E]),
                                  ALU.mult).then_inc(share_chain, 1)
                dve.wait_ge(share_chain, 3 * tile + 2)
                dve.tensor_reduce(share[:, tile, :], taken[:], AX.X, ALU.add).then_inc(share_chain, 1)

            hidden(0, 0)

            def body(i, last):
                for n in range(UB):
                    if n + 1 < UB or not last:
                        hidden(UB * i + n + 1, (n + 1) % 2)
                    leave(i, n)
                    if n % 2:
                        shares(AHEAD * i + n // 2)

            body(0, False)
            with dve.Fori(1, PAIRS // AHEAD - 1) as i:
                body(i, False)
            body(PAIRS // AHEAD - 1, True)
            dve.wait_ge(share_chain, 3 * B * QT)

            def indices(i, n):
                if not (isinstance(i, int) and i == 0):
                    dve.wait_ge(gathered[n], 16 * TOPK * i)
                dve.tensor_copy(idx[n][:], picked[:, i, n]).then_inc(idx_ready, 1)

            def combine(i, n):
                m = NG * i + n
                dve.wait_ge(gathered[n], 16 * TOPK * (i + 1))
                if not (isinstance(m, int) and m == 0):
                    dve.wait_ge(summed, m).then_inc(dve_passed, 1)
                dve.tensor_tensor(gated_rows[:], got[n][:],
                                  share[:, m, :].unsqueeze(2).to_broadcast([P, TOPK, D]), ALU.mult).then_inc(weighed, 1)
                dve.wait_ge(weighed, m + 1)
                dve.tensor_reduce(total[n][:], gated_rows[:].rearrange("p k d -> p d k"), AX.X, ALU.add
                                  ).then_inc(summed, 1)
                dve.wait_ge(summed, m + 1)
                if not (isinstance(i, int) and i == 0):
                    dve.wait_ge(stored[n], 16 * i)
                dve.tensor_tensor(res[n][:], total[n][:], H2[:, i, n, :], ALU.add).then_inc(res_ready, 1)

            for n in range(NG):
                indices(0, n)
            for n in range(NG):
                combine(0, n)
                indices(1, n)
            with dve.Fori(1, B - 1) as i:
                for n in range(NG):
                    combine(i, n)
                    indices(i + 1, n)
            for n in range(NG):
                combine(B - 1, n)

        @block.gpsimd
        def _(pool):
            pool.wait_ge(zero3_written, 16)
            for par in range(AHEAD):
                pool.wait_ge(y_written[par], 16 * (PAIRS // AHEAD))

            def gather(i, n):
                pool.wait_ge(idx_ready, NG * i + n + 1).then_inc(pool_passed, 1)
                if not (isinstance(i, int) and i == 0):
                    pool.wait_ge(weighed, NG * (i - 1) + n + 1).then_inc(pool_passed, 1)
                for k in range(TOPK):
                    pool.indirect_dma_start(got[n][:, k, :], None, dram["rows_y"],
                                            bass.IndirectOffsetOnAxis(ap=idx[n][:, k:k + 1], axis=0)
                                            ).then_inc(gathered[n], 16)

            for n in range(NG):
                gather(0, n)
            with pool.Fori(1, B) as i:
                for n in range(NG):
                    gather(i, n)


def build(nc, io, out):
    dram = {
        "parts": nc.dram_tensor("parts_scratch", [4, 3, P, S], BF16, kind="Internal").ap(),
        "rows": nc.dram_tensor("maxima_scratch", [3, UNITS, P], BF16, kind="Internal").ap(),
        "rows_x": nc.dram_tensor("dispatched", [E * CAP, D], F32, kind="Internal").ap(),
        "rows_y": nc.dram_tensor("expert_out", [1 + E * CAP, D], F32, kind="Internal").ap(),
    }
    with ExitStack() as ctx:
        H2 = ctx.enter_context(nc.sbuf_tensor("H2", [P, B, QT, D], F32))
        Z2 = ctx.enter_context(nc.sbuf_tensor("Z2", [P, B, S], F32))
        picks = ctx.enter_context(nc.sbuf_tensor("picks", [P, B, QT, 2, E], F32))
        picked = ctx.enter_context(nc.sbuf_tensor("picked", [P, B, QT, 8], F32))
        passed = [ctx.enter_context(nc.semaphore(n + "_passed")) for n in ("sp", "pool", "act", "dve")]
        consts = attention_constants(nc, ctx)
        consts_in = ctx.enter_context(nc.semaphore("attention_consts_in"))
        with nc.sbuf_tensor("X", [P, B, S + 2], F32) as X:
            tower(nc, io, X, dram["rows_x"], constant_loads(consts, io), consts_in, passed)
            attention(nc, io, X, H2, Z2, picks, picked, dram, consts, consts_in, passed)
        experts(nc, io, H2, picks, picked, dram, consts[0], out, passed)


def host_constants():
    f = np.float32
    place = np.arange(S - 1, -1, -1, dtype=f)
    freq = (f(1) / f(10000.0) ** (np.arange(0, D, 2, dtype=f) / f(D))).astype(f)
    angle = place[:, None] * freq[None, :]
    i = np.arange(P)
    return {
        "pe": np.concatenate([np.sin(angle), np.cos(angle)], -1).astype(f),
        "ident": np.eye(P, dtype=f),
        "iota": np.arange(P, dtype=f).reshape(P, 1),
        "grp": (i[:, None] // 32 == i[None] // 32).astype(f) / f(32),
        "tri": (i[:, None] < i[None]).astype(f),
        "base1": (np.arange(E) * CAP + 1).astype(f),
    }


def laid_out(inputs):
    a = {k: np.asarray(v) for k, v in inputs.items()}
    out = {k: a[k] for k in ("x", "L0_tok_emb", "L0_tok_ln0_g", "L0_tok_ln0_b", "L0_tok_W1", "L0_tok_W2",
                             "L0_attn_lambda_q1", "L0_attn_lambda_k1", "L0_attn_lambda_q2", "L0_attn_lambda_k2",
                             "L0_attn_gn_w", "L0_attn_gn_b", "L0_attn_out_b", "L0_ffn_bias")}
    for k in ("L0_tok_g1", "L0_tok_b1", "L0_tok_g2", "L0_tok_b2", "L0_attn_V_w", "L0_attn_out_w",
              "L0_ffn_router_w"):
        out[k] = a[k].T
    order = np.arange(D).reshape(HEADS, HD).T.reshape(-1)
    for k in ("Q1", "K1", "Q2", "K2"):
        out[f"L0_attn_{k}_w"] = a[f"L0_attn_{k}_w"][order].T
    for k in ("K1", "K2"):
        out[f"L0_attn_{k}_b"] = a[f"L0_attn_{k}_b"][order]
    gu = np.stack([a["L0_ffn_w_gate"], a["L0_ffn_w_up"]], 0).reshape(2, PAIRS, 2, FF, D)
    out["experts_gu"] = gu.transpose(1, 4, 0, 2, 3).reshape(PAIRS, D, 4 * FF)
    out["experts_down"] = a["L0_ffn_w_down"].transpose(0, 2, 1).reshape(PAIRS, 2 * FF, D)
    sh = np.stack([a["L0_ffn_shared_w_gate"], a["L0_ffn_shared_w_up"]], 0).reshape(2, 2 * FF, D)
    out["shared_gu"] = sh.transpose(2, 0, 1)
    out["shared_down"] = a["L0_ffn_shared_w_down"].transpose(0, 2, 1).reshape(2 * FF, D)
    out.update(host_constants())
    return {k: np.ascontiguousarray(v) for k, v in out.items()}


def kernel(**inputs):
    from concourse import bacc
    from concourse.bass_utils import run_bass_kernel_spmd

    nc = bacc.Bacc("TRN2", target_bir_lowering=False, num_devices=1)
    arrays, io = {}, {}
    for name, a in laid_out(inputs).items():
        arrays["in_" + name] = a
        io[name] = nc.dram_tensor("in_" + name, a.shape, mybir.dt.from_np(a.dtype), kind="ExternalInput").ap()
    out = nc.dram_tensor("out_0", [B, S, D], F32, kind="ExternalOutput").ap()
    build(nc, io, out)
    r = run_bass_kernel_spmd(nc, [arrays], core_ids=[0])
    return r.results[0]["out_0"]
```

```python
from contextlib import ExitStack

import numpy as np

import concourse.bass as bass
from concourse import mybir

F32 = mybir.dt.float32
BF16 = mybir.dt.bfloat16
I32 = mybir.dt.int32
ALU = mybir.AluOpType
ACT = mybir.ActivationFunctionType
AX = mybir.AxisListType

P = 128
B, S, D = 8, 512, 128
QT = S // P
LAYERS, TAPS, VOCAB, PAD = 8, 3, 33, 1
CONVS = 2 * B
E, TOPK, CAP, FF = 64, 6, 768, 64
ZROWS = 8
LAG = 3
RING = 4


def tower(nc, io, X, rows_x, later_loads, later_in, passed):
    with ExitStack() as ctx:
        def sb(name, shape, dt=F32):
            return ctx.enter_context(nc.sbuf_tensor(name, shape, dt))

        def sem(name):
            return ctx.enter_context(nc.semaphore(name))

        H = sb("hidden", [P, B, S + 2])
        W = sb("conv_w", [P, LAYERS, 2, TAPS, D])
        wmean = sb("wmean", [P, 2 * TAPS])
        gb = sb("gb", [P, 4, LAYERS])
        gb0 = sb("gb0", [P, 2])
        eps = sb("eps_tower", [P, 2])
        tok = sb("tok", [P, B, S], I32)
        onehot = sb("onehot", [P, 2, S])
        mask = sb("mask", [P, RING, S])
        emb = sb("emb", [P, D])
        pe = sb("pe", [P, QT, D])
        zrow = sb("zrow", [P, ZROWS * D])
        ident = sb("ident_t", [P, P])
        iota = sb("iota_t", [P, 1])
        sq = sb("sq", [P, 2, S])
        z = sb("z_tower", [P, RING, QT, D])
        sumsq = sb("sumsq", [P, RING, QT])
        std = sb("std", [P, RING, QT])
        rstd = sb("rstd", [P, RING, QT])
        tmean = sb("tmean", [P, 1 + QT])
        ps_y = [ctx.enter_context(nc.psum_tensor(f"y{n}", [P, QT, D], F32)) for n in range(RING)]
        ps_t = [ctx.enter_context(nc.psum_tensor(f"t{n}", [P, S], F32)) for n in range(RING)]

        zeros_ready = sem("zeros_ready")
        zeros_written = sem("zeros_written")
        consts_in = sem("consts_in")
        token_groups = ((0, 1), (1, 4), (4, B))
        tokens_in = [sem(f"tokens_in{n}") for n in range(len(token_groups))]
        scales_in = sem("scales_in")
        table_centred = sem("table_centred")
        sq0_ready = sem("sq0_ready")
        sumsq0_ready = sem("sumsq0_ready")
        weights_in = [sem(f"weights_in{n}") for n in range(LAYERS)]
        emb_zero = sem("emb_zero")
        emb_in = sem("emb_in")
        edges_zero = sem("edges_zero")
        onehot_ready = sem("onehot_ready")
        embedded = sem("embedded")
        std0_ready = sem("std0_ready")
        rstd0_ready = sem("rstd0_ready")
        z0_ready = sem("z0_ready")
        turned0 = sem("turned0")
        scaled0 = sem("scaled0")
        mask_ready = sem("mask_ready")
        wsum_ready = sem("wsum_ready")
        w_ready = sem("w_ready")
        conv_done = sem("conv_done")
        sq_ready = sem("sq_ready")
        sumsq_ready = sem("sumsq_ready")
        std_ready = sem("std_ready")
        rstd_ready = sem("rstd_ready")
        z_ready = sem("z_ready")
        turned = sem("turned")
        hidden_ready = sem("hidden_ready")
        x_ready = sem("x_ready")
        bias_added = sem("bias_added")

        sp_passed, pool_passed, act_passed, _ = passed
        block = ctx.enter_context(nc.Block())

        @block.sync
        def _(sp):
            def load_tokens(n):
                lo, hi = token_groups[n]
                sp.dma_start(tok[:, lo:hi], io["x"][lo:hi].unsqueeze(0).to_broadcast([P, hi - lo, S])
                             ).then_inc(tokens_in[n], 16)

            def load_weights(layer):
                for c, name in enumerate(("W1", "W2")):
                    sp.dma_start(W[:, layer, c], io["L0_tok_" + name][layer].rearrange("t i o -> i t o")
                                 ).then_inc(weights_in[layer], 16)

            load_tokens(0)
            sp.wait_ge(emb_zero, 1).then_inc(sp_passed, 1)
            sp.dma_start(emb[0:VOCAB, :], io["L0_tok_emb"]).then_inc(emb_in, 16)
            sp.dma_start(iota[:], io["iota"]).then_inc(consts_in, 16)
            sp.dma_start(ident[:], io["ident"]).then_inc(consts_in, 16)
            sp.dma_start(pe[:], io["pe"].rearrange("(q p) d -> p q d", p=P)).then_inc(consts_in, 16)
            sp.dma_start(gb0[:, 0:1], io["L0_tok_ln0_g"].unsqueeze(1)).then_inc(scales_in, 16)
            sp.dma_start(gb0[:, 1:2], io["L0_tok_ln0_b"].unsqueeze(1)).then_inc(scales_in, 16)
            for n, name in enumerate(("g1", "b1", "g2", "b2")):
                sp.dma_start(gb[:, n, :], io["L0_tok_" + name]).then_inc(scales_in, 16)
            load_tokens(1)
            load_weights(0)
            load_tokens(2)
            for layer in range(1, LAYERS):
                load_weights(layer)
            for dst, src in later_loads:
                sp.dma_start(dst, src).then_inc(later_in, 16)
            sp.wait_ge(zeros_ready, 1).then_inc(sp_passed, 1)
            filled = rows_x.rearrange("(a p r) c -> a p (r c)", p=P, r=ZROWS)
            with sp.Fori(0, E * CAP // (P * ZROWS)) as i:
                sp.dma_start(filled[i], zrow[:]).then_inc(zeros_written, 16)
            sp.wait_ge(zeros_written, 16 * (E * CAP // (P * ZROWS))).then_inc(sp_passed, 1)

        @block.gpsimd
        def _(pool):
            pool.memset(emb[:], 0.0).then_inc(emb_zero, 1)
            for buf in (X, H):
                for col in (0, S + 1):
                    pool.memset(buf[:, :, col:col + 1], 0.0).then_inc(edges_zero, 1)
            pool.memset(eps[:, 0:1], 1e-12).then_inc(edges_zero, 1)
            pool.memset(eps[:, 1:2], 1e-5).then_inc(edges_zero, 1)
            pool.memset(zrow[:], 0.0).then_inc(zeros_ready, 1)
            for s in range(B):
                pool.wait_ge(mask_ready, s + 1)
                pool.wait_ge(scaled0, s + 1)
                pool.tensor_tensor(X[:, s, 1:S + 1], X[:, s, 1:S + 1], mask[:, s % RING, :], ALU.mult
                                   ).then_inc(x_ready, 1)
            with pool.Fori(0, LAYERS) as layer:
                for s in range(B):
                    pool.wait_ge(conv_done, layer * CONVS + s + 1).then_inc(pool_passed, 1)
                    pool.tensor_tensor(X[:, s, 1:S + 1], X[:, s, 1:S + 1],
                                       gb[:, 3, bass.ds(layer, 1)].to_broadcast([P, S]), ALU.add
                                       ).then_inc(bias_added, 1)

        @block.tensor
        def _(pe_):
            def transposes(s, src, dst, inc):
                for q in range(QT):
                    last = pe_.transpose(dst[:, q * P:(q + 1) * P], src[:, q, :], ident[:])
                last.then_inc(inc, 1)

            pe_.wait_ge(consts_in, 16 * 3)
            pe_.wait_ge(table_centred, 4)
            for s in range(B + 3):
                if s < B:
                    pe_.wait_ge(onehot_ready, s + 1)
                    if s >= RING:
                        pe_.wait_ge(z0_ready, s - RING + 1)
                    for q in range(QT):
                        pe_.matmul(ps_y[s % RING][:, q, :], onehot[:, s % 2, q * P:(q + 1) * P], emb[:],
                                   start=True, stop=False)
                        last = pe_.matmul(ps_y[s % RING][:, q, :], ident[:], pe[:, q, :],
                                          start=False, stop=True)
                    last.then_inc(embedded, 1)
                if s >= 3:
                    pe_.wait_ge(z0_ready, s - 2)
                    if s - 3 >= RING:
                        pe_.wait_ge(scaled0, s - 3 - RING + 1)
                    transposes(s - 3, z[:, (s - 3) % RING], ps_t[(s - 3) % RING], turned0)

            def conv(layer, c):
                n, s = c // B, c % B
                at = layer * CONVS + c
                src = H if n else X
                if n:
                    pe_.wait_ge(hidden_ready, layer * B + s + 1)
                else:
                    pe_.wait_ge(x_ready, layer * B + s + 1)
                    if s == 0:
                        pe_.wait_ge(w_ready, layer + 1)
                if isinstance(at, int) and at < RING:
                    pe_.wait_ge(z0_ready, B)
                else:
                    pe_.wait_ge(z_ready, at - RING + 1)
                for q in range(QT):
                    for t in range(TAPS):
                        last = pe_.matmul(ps_y[c % RING][:, q, :], src[:, s, q * P + t:q * P + t + P],
                                          W[:, layer, n, t, :], start=(t == 0), stop=(t == TAPS - 1))
                last.then_inc(conv_done, 1)

            def turn(layer, k, first=False):
                pe_.wait_ge(z_ready, layer * CONVS + k + 1)
                j = k - RING
                if j >= B:
                    pe_.wait_ge(x_ready, B + layer * B + j - B + 1)
                elif j >= 0:
                    pe_.wait_ge(hidden_ready, layer * B + j + 1)
                else:
                    pe_.wait_ge(x_ready, layer * B + B + j + 1)
                transposes(k % B, z[:, k % RING], ps_t[k % RING], turned)

            for c in range(LAG):
                conv(0, c)

            def body(layer, last):
                for k in range(CONVS):
                    turn(layer, k)
                    c = k + LAG
                    if c < CONVS:
                        conv(layer, c)
                    elif not last:
                        conv(layer + 1, c - CONVS)

            body(0, False)
            with pe_.Fori(1, LAYERS - 1) as layer:
                body(layer, False)
            body(LAYERS - 1, True)

        @block.scalar
        def _(act):
            act.wait_ge(edges_zero, 6)
            for s in range(B + 4):
                if s < B:
                    act.wait_ge(embedded, s + 1)
                    if s >= 2:
                        act.wait_ge(sumsq0_ready, s - 1)
                    act.activation(sq[:, s % 2, :], ps_y[s % RING][:].rearrange("p q d -> p (q d)"), ACT.Square
                                   ).then_inc(sq0_ready, 1)
                if 1 <= s <= B:
                    act.wait_ge(sumsq0_ready, s)
                    act.activation(std[:, (s - 1) % RING, :], sumsq[:, (s - 1) % RING, :], ACT.Sqrt, scale=1.0 / D,
                                   bias=eps[:, 0:1]).then_inc(std0_ready, 1)
                if s == 4:
                    act.wait_ge(scales_in, 16 * 6)
                if s >= 4:
                    act.wait_ge(turned0, s - 3)
                    act.activation(X[:, s - 4, 1:S + 1], ps_t[(s - 4) % RING][:], ACT.Identity,
                                   scale=gb0[:, 0:1], bias=gb0[:, 1:2]).then_inc(scaled0, 1)

            def square(layer, c):
                at = layer * CONVS + c
                act.wait_ge(conv_done, at + 1)
                if not (isinstance(at, int) and at < 2):
                    act.wait_ge(sumsq_ready, at - 1)
                act.activation(sq[:, c % 2, :], ps_y[c % RING][:].rearrange("p q d -> p (q d)"), ACT.Square
                               ).then_inc(sq_ready, 1)

            def root(layer, c):
                act.wait_ge(sumsq_ready, layer * CONVS + c + 1)
                act.activation(std[:, c % RING, :], sumsq[:, c % RING, :], ACT.Sqrt, scale=1.0 / D,
                               bias=eps[:, 1:2]).then_inc(std_ready, 1)

            square(0, 0)
            root(0, 0)
            square(0, 1)
            root(0, 1)
            square(0, 2)

            def body(layer, last):
                for k in range(CONVS):
                    c = k + LAG - 1
                    if c < CONVS:
                        root(layer, c)
                    elif not last:
                        root(layer + 1, c - CONVS)
                    if k < B:
                        act.wait_ge(turned, layer * CONVS + k + 1).then_inc(act_passed, 1)
                        act.activation(H[:, k, 1:S + 1], ps_t[k % RING][:], ACT.Relu,
                                       scale=gb[:, 0, bass.ds(layer, 1)], bias=gb[:, 1, bass.ds(layer, 1)]
                                       ).then_inc(hidden_ready, 1)
                    c = k + LAG
                    if c < CONVS:
                        square(layer, c)
                    elif not last:
                        square(layer + 1, c - CONVS)

            body(0, False)
            with act.Fori(1, LAYERS - 1) as layer:
                body(layer, False)
            body(LAYERS - 1, True)

        @block.vector
        def _(dve):
            def centre(layer):
                w = W[:, layer].rearrange("p c t o -> p (c t) o")
                dve.tensor_reduce(wmean[:], w, AX.X, ALU.add).then_inc(wsum_ready, 1)
                dve.wait_ge(wsum_ready, layer * 2 + 1)
                dve.tensor_scalar(wmean[:], wmean[:], -1.0 / D, None, ALU.mult).then_inc(wsum_ready, 1)
                dve.wait_ge(wsum_ready, layer * 2 + 2)
                dve.tensor_tensor(w, w, wmean[:].unsqueeze(2).to_broadcast([P, 2 * TAPS, D]), ALU.add
                                  ).then_inc(w_ready, 1)

            def embed_columns(s):
                for n, (lo, hi) in enumerate(token_groups):
                    if s == lo:
                        dve.wait_ge(tokens_in[n], 16)
                if s >= 2:
                    dve.wait_ge(embedded, s - 1)
                dve.tensor_scalar(onehot[:, s % 2, :], tok[:, s, :], iota[:, 0:1], None, ALU.is_equal
                                  ).then_inc(onehot_ready, 1)

            dve.wait_ge(consts_in, 16 * 3)
            embed_columns(0)
            dve.wait_ge(emb_in, 16)
            dve.tensor_reduce(tmean[:, 0:1], emb[:], AX.X, ALU.add)
            dve.tensor_reduce(tmean[:, 1:1 + QT], pe[:], AX.X, ALU.add).then_inc(table_centred, 1)
            dve.wait_ge(table_centred, 1)
            dve.tensor_scalar(tmean[:], tmean[:], -1.0 / D, None, ALU.mult).then_inc(table_centred, 1)
            dve.wait_ge(table_centred, 2)
            dve.tensor_tensor(emb[:], emb[:], tmean[:, 0:1].to_broadcast([P, D]), ALU.add).then_inc(table_centred, 1)
            dve.tensor_tensor(pe[:], pe[:], tmean[:, 1:1 + QT].unsqueeze(2).to_broadcast([P, QT, D]), ALU.add
                              ).then_inc(table_centred, 1)
            for s in range(1, B + 3):
                if s < B:
                    embed_columns(s)
                if s >= 3:
                    if s >= 3 + RING:
                        dve.wait_ge(x_ready, s - 2 - RING)
                    dve.tensor_scalar(mask[:, (s - 3) % RING, :], tok[:, s - 3, :], float(PAD), None, ALU.not_equal
                                      ).then_inc(mask_ready, 1)
                if s <= B:
                    dve.wait_ge(sq0_ready, s)
                    dve.tensor_reduce(sumsq[:, (s - 1) % RING, :],
                                      sq[:, (s - 1) % 2, :].rearrange("p (q d) -> p q d", q=QT),
                                      AX.X, ALU.add).then_inc(sumsq0_ready, 1)
                if s == 5:
                    dve.wait_ge(weights_in[0], 32)
                    centre(0)
                if 2 <= s < B + 2:
                    n = s - 2
                    dve.wait_ge(std0_ready, n + 1)
                    dve.reciprocal(rstd[:, n % RING, :], std[:, n % RING, :]).then_inc(rstd0_ready, 1)
                    dve.wait_ge(rstd0_ready, n + 1)
                    if n >= RING:
                        dve.wait_ge(turned0, n - RING + 1)
                    dve.tensor_tensor(z[:, n % RING], ps_y[n % RING][:],
                                      rstd[:, n % RING, :].unsqueeze(2).to_broadcast([P, QT, D]), ALU.mult
                                      ).then_inc(z0_ready, 1)

            def sums(layer, c):
                dve.wait_ge(sq_ready, layer * CONVS + c + 1)
                dve.tensor_reduce(sumsq[:, c % RING, :], sq[:, c % 2, :].rearrange("p (q d) -> p q d", q=QT),
                                  AX.X, ALU.add).then_inc(sumsq_ready, 1)

            def normalise(layer, c):
                at = layer * CONVS + c
                dve.wait_ge(std_ready, at + 1)
                dve.reciprocal(rstd[:, c % RING, :], std[:, c % RING, :]).then_inc(rstd_ready, 1)
                dve.wait_ge(rstd_ready, at + 1)
                if isinstance(at, int) and at < RING:
                    dve.wait_ge(turned0, B)
                else:
                    dve.wait_ge(turned, at - RING + 1)
                dve.tensor_tensor(z[:, c % RING], ps_y[c % RING][:],
                                  rstd[:, c % RING, :].unsqueeze(2).to_broadcast([P, QT, D]), ALU.mult
                                  ).then_inc(z_ready, 1)

            for n in range(1, LAYERS):
                dve.wait_ge(weights_in[n], 32)
            sums(0, 0)
            normalise(0, 0)
            sums(0, 1)
            normalise(0, 1)
            sums(0, 2)

            def body(layer, last):
                for k in range(CONVS):
                    c = k + LAG - 1
                    if c < CONVS:
                        normalise(layer, c)
                    elif not last:
                        normalise(layer + 1, c - CONVS)
                    if k >= B:
                        s = k - B
                        dve.wait_ge(turned, layer * CONVS + k + 1)
                        dve.wait_ge(bias_added, layer * B + s + 1)
                        dve.scalar_tensor_tensor(out=X[:, s, 1:S + 1], in0=ps_t[k % RING][:],
                                                 scalar=gb[:, 2, bass.ds(layer, 1)], in1=X[:, s, 1:S + 1],
                                                 op0=ALU.mult, op1=ALU.add).then_inc(x_ready, 1)
                    c = k + LAG
                    if c < CONVS:
                        sums(layer, c)
                    elif not last:
                        sums(layer + 1, c - CONVS)
                    if k == 4 and not last:
                        centre(layer + 1)

            body(0, False)
            with dve.Fori(1, LAYERS - 1) as layer:
                body(layer, False)
            body(LAYERS - 1, True)
HEADS, HD = 8, 16
MAPS = 2
GROUPS = 4
UNITS = 16
TERMS = 6
Q_PART = (0, 0, 1, 1, 0, 2)
K_PART = (0, 1, 0, 1, 2, 0)
KT = TERMS * HD
KM = KT + 3
NR = 14
FAR = float(1 << 17)


def attention_constants(nc, ctx):
    shapes = {"ident": [P, P], "wproj": [P, 4, D], "kbias": [P, 4], "wv": [P, D], "wout": [P, D], "outb": [P, D],
              "gnw": [P, 2], "grp": [P, P], "wrout": [P, E], "rbias": [P, E], "base1": [P, E], "tri_f": [P, P],
              "lam": [P, 4, HEADS], "shw": [P, 2, 2 * FF], "shd": [P, D]}
    return [ctx.enter_context(nc.sbuf_tensor(name, shape, F32)) for name, shape in shapes.items()]


def constant_loads(consts, io):
    ident, wproj, kbias, wv, wout, outb, gnw, grp, wrout, rbias, base1, tri_f, lam, shw, shd = consts
    loads = [(ident[:], io["ident"]), (wv[:], io["L0_attn_V_w"]), (wout[:], io["L0_attn_out_w"]),
             (grp[:], io["grp"]), (tri_f[:], io["tri"]), (wrout[:], io["L0_ffn_router_w"]),
             (outb[:], io["L0_attn_out_b"].unsqueeze(0).to_broadcast([P, D])),
             (rbias[:], io["L0_ffn_bias"].unsqueeze(0).to_broadcast([P, E])),
             (base1[:], io["base1"].unsqueeze(0).to_broadcast([P, E])),
             (gnw[:, 0:1], io["L0_attn_gn_w"].unsqueeze(1)), (gnw[:, 1:2], io["L0_attn_gn_b"].unsqueeze(1)),
             (kbias[:, 1:2], io["L0_attn_K1_b"].unsqueeze(1)), (kbias[:, 3:4], io["L0_attn_K2_b"].unsqueeze(1)),
             (shw[:], io["shared_gu"]), (shd[:], io["shared_down"])]
    for j, name in enumerate(("Q1", "K1", "Q2", "K2")):
        loads.append((wproj[:, j, :], io[f"L0_attn_{name}_w"]))
    for j, name in enumerate(("q1", "k1", "q2", "k2")):
        loads.append((lam[:, j, :], io["L0_attn_lambda_" + name].rearrange("h o -> o h").to_broadcast([P, HEADS])))
    return loads


consts_count = 16 * 23


def attention(nc, io, X, H2, Z2, picks, picked, dram, consts, consts_in, passed):
    with ExitStack() as ctx:
        def sb(name, shape, dt=F32):
            return ctx.enter_context(nc.sbuf_tensor(name, shape, dt))

        def sem(name):
            return ctx.enter_context(nc.semaphore(name))

        def bank(name, shape=(P, S)):
            return ctx.enter_context(nc.psum_tensor(name, list(shape), F32))

        ident, wproj, kbias, wv, wout, outb, gnw, grp, wrout, rbias, base1, tri_f, lam, shw, shd = consts
        tri = sb("tri", [P, P], BF16)
        ones = sb("ones", [P, P], BF16)
        neglam = sb("neglam", [P, HEADS])
        half = sb("half", [P, QT])
        hc = sb("hc", [P, S])
        htok = sb("htok", [P, QT, D])
        ztok = sb("ztok", [P, QT, D])
        zT = sb("zT", [P, S])
        fstats = sb("fstats", [P, QT, 6])
        fmv = sb("fmv", [P, QT, 2])
        fve = sb("fve", [P, QT])
        frstd = sb("frstd", [P, QT])
        q32 = sb("q32", [P, S])
        rest = sb("rest", [P, S])
        parts = sb("parts", [P, 2, 3, S], BF16)
        stack = [[sb(f"stack{p}{j}", [P, HEADS, S], BF16) for j in range(4)] for p in range(2)]
        Vx = [sb(f"Vx{p}", [P, QT, HEADS, 32]) for p in range(2)]
        nm = sb("nm", [P, 2, UNITS])
        mp = sb("mp", [UNITS, 3, P], BF16)
        mrest = sb("mrest", [UNITS, P])
        ex = sb("ex", [P, 8, S])
        act_g = ex[:, 0:2, :]
        hid = ex[:, 2:4, :]
        OT = sb("OT", [P, S])
        rsum = sb("rsum", [P, QT, 4])
        on = sb("on", [P, QT, 4, HD])
        otok = sb("otok", [P, QT, HEADS, HD])
        gst = sb("gst", [P, 6])
        gmv = sb("gmv", [P, 2])
        gm = sb("gm", [P, 1])
        gd = sb("gd", [P, 1])
        gv = sb("gv", [P, 1])
        gvar = sb("gvar", [P, 1])
        gve = sb("gve", [P, 1])
        grs = sb("grs", [P, 1])
        gsc = sb("gsc", [P, 1])
        gbi = sb("gbi", [P, 1])
        xn = sb("xn", [P, S])
        h2c = sb("h2c", [P, QT, D])
        tstats = sb("tstats", [P, QT, 6])
        tmv = sb("tmv", [P, QT, 2])
        tve = sb("tve", [P, QT])
        trstd = sb("trstd", [P, QT])
        R = [sb(f"R{p}", [P, QT, D]) for p in range(2)]
        z2c = sb("z2c", [P, S])
        logit = sb("logit", [P, QT, E])
        lmax = sb("lmax", [P, QT])
        lsum = sb("lsum", [P, QT])
        lrec = sb("lrec", [P, QT])
        prob = sb("prob", [P, QT, E + 2])
        top = sb("top", [P, QT, 8])
        repl = sb("repl", [P, QT, E + 2])
        M = sb("M", [P, QT, E], BF16)
        Macc = sb("Macc", [P, E], BF16)
        mnew = sb("mnew", [P, E])
        gsum = sb("gsum", [P, QT])
        grec = sb("grec", [P, QT])
        Mv = sb("Mv", [P, QT, E])
        gate = sb("gate", [P, QT, E])
        slot1 = sb("slot1", [P, QT, E])
        v8 = sb("v8", [P, QT, 8])
        none = sb("none", [P, QT, 8])
        freed = sb("freed", [P, 1])
        sidx = sb("sidx", [P, QT, 8], I32)

        ps_m = [bank(f"ps_m{i}") for i in range(3)]
        ps_e = [bank(f"ps_e{i}") for i in range(2)]
        ps_o = bank("ps_o")
        psB, psC = bank("psB"), bank("psC")

        names = """lam_ready consts_ready ones_rows vones hc_ready f_turned htok_ready f_stats
            f_var f_eps f_rstd resid_ready ztok_ready z_turned zT_ready proj_done hi_ready rest_ready
            mid_ready parts_ready v_done v_ready mxmm_done max_ready nm_turned mp_chain rows_ready
            rows_stored rows_loaded smm_done exp_done pv_done o_copied o_turned o_chain o_norm
            t_turned gn_chain gn_mean_done gn_var_done gn_var_out gn_eps gn_rstd gn_ready xn_ready y_done
            h2_ready h2_kept t_chain t_var t_eps t_rstd z2_ready z2_turned z2c_ready logit_done
            shifted_ready prob_exp r_chain mask_ready rank_done rows_out slots_ready scattered macc_ready t_chain2 rows_free
            picks_kept
            sh_mm sh_gated sh_hid sh_down sh_added""".split()
        (lam_ready, consts_ready, ones_rows, vones, hc_ready, f_turned, htok_ready, f_stats,
         f_var, f_eps, f_rstd, resid_ready, ztok_ready, z_turned, zT_ready, proj_done, hi_ready, rest_ready,
         mid_ready, parts_ready, v_done, v_ready, mxmm_done, max_ready, nm_turned, mp_chain, rows_ready,
         rows_stored, rows_loaded, smm_done, exp_done, pv_done, o_copied, o_turned, o_chain, o_norm,
         t_turned, gn_chain, gn_mean_done, gn_var_done, gn_var_out, gn_eps, gn_rstd, gn_ready, xn_ready, y_done,
         h2_ready, h2_kept, t_chain, t_var, t_eps, t_rstd, z2_ready, z2_turned, z2c_ready, logit_done,
         shifted_ready, prob_exp, r_chain, mask_ready, rank_done, rows_out, slots_ready, scattered,
         macc_ready, t_chain2, rows_free, picks_kept, sh_mm, sh_gated, sh_hid, sh_down, sh_added) = [sem(n) for n in names]
        stored = [sem(f"stored{j}") for j in range(4)]
        loaded = [sem(f"loaded{j}") for j in range(4)]

        sp_passed, pool_passed, act_passed, dve_passed = passed
        block = ctx.enter_context(nc.Block())

        M_BANK = [u % 3 for u in range(UNITS - 1)] + [1]
        M_BACK = [4, 2, 4] + [3] * (UNITS - 4) + [2]

        def has(t, g, stage):
            if not isinstance(t, int):
                return True
            n = 4 * t + g
            return {"F": t + 1 < B, "M": t < B, "Mprev": 0 <= n - 1 < 4 * B, "X": 0 <= n - 2 < 4 * B,
                    "Xprev": 0 <= n - 3 < 4 * B, "T": 0 <= t - 1 < B, "R": 0 <= t - 2 < B}[stage]

        def run(eng, step, first):
            first()

            def seq(t, par):
                for g in range(GROUPS):
                    step(t, g, par)
            seq(0, 0)
            seq(1, 1)
            seq(2, 0)
            with eng.Fori(1, 3) as i:
                seq(i * 2 + 1, 1)
                seq(i * 2 + 2, 0)
            for t in range(7, B + 2):
                seq(t, t % 2)

        def at(t, g, back):
            return 4 * t + g - back, t + (g - back) // 4, (g - back) % 4, ((g - back) // 4) % 2

        @block.sync
        def _(sp):
            def keep_parts(b, j):
                sp.wait_ge(parts_ready, 4 * b + j + 1).then_inc(sp_passed, 1)
                if not (isinstance(b, int) and b == 0):
                    sp.wait_ge(loaded[j], 16 * TERMS * b).then_inc(sp_passed, 1)
                sp.dma_start(dram["parts"][j].rearrange("a p t -> p a t"), parts[:, j % 2]).then_inc(stored[j], 16)

            def load_stack(b, j, par):
                sp.wait_ge(stored[j], 16 * b + 16).then_inc(sp_passed, 1)
                if not (isinstance(b, int) and b < 2):
                    sp.wait_ge(smm_done, 4 * UNITS * (b - 1)).then_inc(sp_passed, 1)
                for k in range(TERMS):
                    part = (Q_PART, K_PART)[j % 2][k]
                    sp.dma_start(stack[par][j][k * HD:(k + 1) * HD],
                                 dram["parts"][j, part].rearrange("(d h) t -> d h t", h=HEADS)
                                 ).then_inc(loaded[j], 16)

            sp.wait_ge(consts_ready, 2).then_inc(sp_passed, 1)
            for p in range(2):
                for j in (1, 3):
                    sp.dma_start(stack[p][j][KT:KM].rearrange("a h (n c) -> a (h n) c", c=P),
                                 ones[0:KM - KT, :].unsqueeze(1).to_broadcast([KM - KT, HEADS * QT, P])
                                 ).then_inc(ones_rows, 16)

            def first():
                keep_parts(0, 0)
                keep_parts(0, 1)
                load_stack(0, 0, 0)
                keep_parts(0, 2)
                load_stack(0, 1, 0)
                keep_parts(0, 3)
                load_stack(0, 2, 0)
                load_stack(0, 3, 0)

            def step(t, g, par):
                if has(t, g, "Mprev"):
                    n, b, gg, flip = at(t, g, 1)
                    p = par ^ flip
                    sp.wait_ge(rows_ready, n + 1).then_inc(sp_passed, 1)
                    if not (isinstance(n, int) and n == 0):
                        sp.wait_ge(rows_loaded, 32 * n).then_inc(sp_passed, 1)
                    sp.dma_start(dram["rows"].rearrange("a u t -> u a t"), mp[:]).then_inc(rows_stored, 16)
                    sp.wait_ge(rows_stored, 16 * n + 16).then_inc(sp_passed, 1)
                    for m in range(MAPS):
                        sp.dma_start(stack[p][2 * m][KT:KM, 2 * gg:2 * gg + 2, :],
                                     dram["rows"][:, 8 * m:8 * m + 8, :].rearrange("a (h q) t -> a h (q t)", h=2)
                                     ).then_inc(rows_loaded, 16)
                if has(t, g, "F"):
                    if g == 1:
                        keep_parts(t + 1, 0)
                        keep_parts(t + 1, 1)
                    if g == 2:
                        keep_parts(t + 1, 2)
                        load_stack(t + 1, 0, 1 - par)
                        load_stack(t + 1, 1, 1 - par)
                        keep_parts(t + 1, 3)
                    if g == 3:
                        load_stack(t + 1, 2, 1 - par)
                        load_stack(t + 1, 3, 1 - par)

            run(sp, step, first)

        @block.tensor
        def _(pe):
            def turn(dst, src, inc):
                for q in range(QT):
                    last = pe.transpose(dst[:, q * P:(q + 1) * P], src[:, q], ident[:])
                last.then_inc(inc, 1)

            def tokens(b):
                pe.wait_ge(hc_ready, b + 1)
                if not (isinstance(b, int) and b < 3):
                    pe.wait_ge(h2_ready, b - 2)
                turn(psC, hc[:].rearrange("p (q t) -> p q t", q=QT), f_turned)

            def features(b):
                pe.wait_ge(ztok_ready, b + 1)
                turn(psC, ztok, z_turned)

            def project(b, j):
                if j == 0:
                    pe.wait_ge(zT_ready, b + 1)
                else:
                    pe.wait_ge(hi_ready, 4 * b + j)
                pe.matmul(psC[:], wproj[:, j, :], zT[:], start=True, stop=True).then_inc(proj_done, 1)

            def values(b):
                pe.wait_ge(hi_ready, 4 * b + 4)
                for q in range(QT):
                    last = pe.matmul(psC[:, q * P:(q + 1) * P], zT[:, q * P:(q + 1) * P], wv[:],
                                     start=True, stop=True)
                last.then_inc(v_done, 1)

            pe.wait_ge(consts_in, consts_count)

            def first():
                tokens(0)
                features(0)
                for j in range(4):
                    project(0, j)
                values(0)

            def step(t, g, par):
                xn_, xb, xg, xf = at(t, g, 2)
                pn, pb, pg, pf = at(t, g, 3)
                mn = at(t, g, 1)[0]

                def pv(n, b, gg, p, c):
                    pe.wait_ge(exp_done, UNITS * n + 4 * c + 4)
                    if c == 0:
                        if not (isinstance(n, int) and n == 0):
                            pe.wait_ge(o_copied, n)
                        if gg == 0:
                            pe.wait_ge(v_ready, b + 1)
                    for j in range(4):
                        last = pe.matmul(ps_o[32 * j:32 * j + 32, :], Vx[p][:, c, 2 * gg + j % 2, :],
                                         ex[:, 4 * (c % 2) + j, :], start=(c == 0), stop=(c == QT - 1))
                    last.then_inc(pv_done, 1)

                for u in range(UNITS):
                    if has(t, g, "M"):
                        if g == 0 and u % 8 == 0:
                            for j in (0, 1) if u == 0 else (2, 3):
                                pe.wait_ge(loaded[j], 16 * TERMS * (t + 1))
                        m = 4 * UNITS * t + UNITS * g + u
                        if not (isinstance(m, int) and m < 3):
                            pe.wait_ge(max_ready, m - M_BACK[u] + 1)
                        mp_, h, q = u // 8, 2 * g + (u // 4) % 2, u % 4
                        pe.matmul(ps_m[M_BANK[u]][:], stack[par][2 * mp_][0:KT, h, q * P:(q + 1) * P],
                                  stack[par][2 * mp_ + 1][0:KT, h, :], start=True, stop=True
                                  ).then_inc(mxmm_done, 1)
                    if has(t, g, "X"):
                        p = par ^ xf
                        if u == 0:
                            pe.wait_ge(rows_loaded, 32 * xn_ + 32)
                            if isinstance(xn_, int) and xn_ == 0:
                                pe.wait_ge(ones_rows, 16 * 4)
                                pe.wait_ge(consts_ready, 5)
                        e = UNITS * xn_ + u
                        if not (isinstance(e, int) and e < 2):
                            pe.wait_ge(exp_done, e - 1)
                        c, j = u // 4, u % 4
                        m_, h = j // 2, 2 * xg + j % 2
                        pe.matmul(ps_e[u % 2][:], stack[p][2 * m_ + 1][0:KM, h, c * P:(c + 1) * P],
                                  stack[p][2 * m_][0:KM, h, :], start=True, stop=True).then_inc(smm_done, 1)
                        if u in (6, 10, 14):
                            pv(xn_, xb, xg, p, (u - 6) // 4)
                    if u == 2 and has(t, g, "Xprev"):
                        pv(pn, pb, pg, par ^ pf, 3)
                    if u == 3 and has(t, g, "Mprev"):
                        pe.wait_ge(max_ready, UNITS * (mn + 1))
                        if not (isinstance(t, int) and 4 * t + g < 4):
                            pe.wait_ge(o_chain, 3 * pn)
                        if g == 3 and has(t, g, "T"):
                            pe.wait_ge(gn_chain, 4 * (t - 1) + 3)
                        pe.transpose(psB[0:UNITS, 0:P], nm[:, (g - 1) % 2, :], ident[:]).then_inc(nm_turned, 1)
                    if u == 8 and has(t, g, "Xprev"):
                        pe.wait_ge(o_copied, pn + 1)
                        if has(t, g, "Mprev"):
                            pe.wait_ge(mp_chain, 3 * mn + 2)
                        else:
                            pe.wait_ge(o_norm, pn)
                        if g == 3 and has(t, g, "T"):
                            pe.wait_ge(gn_var_out, t)
                        turn(psB, OT[:].rearrange("p (q t) -> p q t", q=QT), o_turned)
                    b = t + 1
                    if has(t, g, "F"):
                        if (g, u) == (0, 3):
                            tokens(b)
                        if (g, u) == (1, 0):
                            if has(t, g, "R"):
                                pe.wait_ge(r_chain, NR * (t - 2) + 1)
                            features(b)
                        if (g, u) == (1, 1):
                            project(b, 0)
                        if (g, u) == (1, 9):
                            if has(t, g, "R"):
                                pe.wait_ge(rows_out, t - 1)
                            project(b, 1)
                        if (g, u) == (1, 12):
                            project(b, 2)
                        if (g, u) == (2, 4):
                            project(b, 3)
                        if (g, u) == (2, 9):
                            values(b)
                    b = t - 1
                    if has(t, g, "T"):
                        if (g, u) == (2, 14):
                            pe.wait_ge(o_norm, 4 * b + 4)
                            if not (isinstance(b, int) and b == 0):
                                pe.wait_ge(rows_out, b)
                            if has(t, g, "F"):
                                pe.wait_ge(v_ready, t + 2)
                            turn(psC, otok[:].rearrange("p q h d -> p q (h d)"), t_turned)
                        if (g, u) == (3, 1):
                            pe.wait_ge(gn_chain, 4 * b + 2)
                            pe.matmul(psB[:, 0:1], grp[:], gmv[:, 0:1], start=True, stop=True
                                      ).then_inc(gn_mean_done, 1)
                        if (g, u) == (3, 6):
                            pe.wait_ge(gn_chain, 4 * b + 4)
                            if has(t, g, "Mprev"):
                                pe.wait_ge(mp_chain, 3 * mn + 2)
                            pe.matmul(psB[:, 0:1], grp[:], gv[:], start=True, stop=True
                                      ).then_inc(gn_var_done, 1)
                        if (g, u) == (3, 13):
                            pe.wait_ge(xn_ready, b + 1)
                            for q in range(QT):
                                last = pe.matmul(psC[:, q * P:(q + 1) * P], xn[:, q * P:(q + 1) * P], wout[:],
                                                 start=True, stop=True)
                            last.then_inc(y_done, 1)
                    b = t - 2
                    if has(t, g, "R"):
                        if (g, u) == (0, 9):
                            pe.wait_ge(z2_ready, b + 1)
                            if has(t, g, "F"):
                                pe.wait_ge(htok_ready, t + 2)
                            turn(psC, R[par][:], z2_turned)
                        if (g, u) == (0, 11):
                            pe.wait_ge(z2c_ready, 2 * b + 1)
                            for q in range(QT):
                                last = pe.matmul(psC[:, q * E:(q + 1) * E], z2c[:, q * P:(q + 1) * P], wrout[:],
                                                 start=True, stop=True)
                            last.then_inc(logit_done, 1)
                        if (g, u) == (1, 4):
                            pe.wait_ge(mask_ready, b + 1)
                            pe.wait_ge(macc_ready, b + 1)
                            if has(t, g, "F"):
                                pe.wait_ge(hi_ready, 4 * (t + 1) + 1)
                            for q in range(QT):
                                out = psC[:, q * E:(q + 1) * E]
                                pe.matmul(out, ones[:], Macc[:], start=True, stop=False)
                                for q2 in range(q):
                                    pe.matmul(out, ones[:], M[:, q2, :], start=False, stop=False)
                                last = pe.matmul(out, tri[:], M[:, q, :], start=False, stop=True)
                            last.then_inc(rank_done, 1)

            run(pe, step, first)

            def shared_up(b):
                if b >= 2:
                    pe.wait_ge(sh_hid, b - 1)
                for ps, w in (((ps_m, ps_e)[b % 2][0], 0), ((ps_m, ps_e)[b % 2][1], 1)):
                    last = pe.matmul(ps[:], shw[:, w, :], Z2[:, b, :], start=True, stop=True)
                last.then_inc(sh_mm, 1)

            def shared_down(b):
                pe.wait_ge(sh_hid, b + 1)
                if b >= 2:
                    pe.wait_ge(sh_added, b - 1)
                for q in range(QT):
                    last = pe.matmul((psC, psB)[b % 2][:, q * P:(q + 1) * P],
                                     hid[:, b % 2, q * P:(q + 1) * P], shd[:], start=True, stop=True)
                last.then_inc(sh_down, 1)

            pe.wait_ge(z2c_ready, 2 * B)
            shared_up(0)
            for b in range(1, B):
                shared_up(b)
                shared_down(b - 1)
            shared_down(B - 1)

        @block.scalar
        def _(act):
            act.wait_ge(consts_in, consts_count)
            act.wait_ge(lam_ready, 1)
            act.activation(lam[:, 0, :], lam[:, 1, :], ACT.Exp).then_inc(lam_ready, 1)
            act.activation(lam[:, 2, :], lam[:, 3, :], ACT.Exp).then_inc(lam_ready, 1)

            def take(b):
                if not (isinstance(b, int) and b == 0):
                    act.wait_ge(f_turned, b).then_inc(act_passed, 1)
                act.activation(hc[:], X[:, b, 1:S + 1], ACT.Copy).then_inc(hc_ready, 1)

            def tokens(b):
                act.wait_ge(f_turned, b + 1)
                if not (isinstance(b, int) and b == 0):
                    act.wait_ge(resid_ready, b)
                    act.wait_ge(ztok_ready, b)
                act.activation(htok[:].rearrange("p q d -> p (q d)"), psC[:], ACT.Copy).then_inc(htok_ready, 1)

            def features(b):
                act.wait_ge(z_turned, b + 1)
                act.activation(zT[:], psC[:], ACT.Copy).then_inc(zT_ready, 1)

            def split(b, j):
                n = 4 * b + j
                act.wait_ge(proj_done, n + 1)
                if not (isinstance(n, int) and n == 0):
                    act.wait_ge(rest_ready, n)
                if not (isinstance(n, int) and n < 2):
                    act.wait_ge(stored[j ^ 2], (16 * b if j < 2 else 16 * b + 16))
                bias = {"bias": kbias[:, j:j + 1]} if j % 2 else {}
                f = ACT.Identity if j % 2 else ACT.Copy
                act.activation(q32[:], psC[:], f, **bias)
                act.activation(parts[:, j % 2, 0, :], psC[:], f, **bias).then_inc(hi_ready, 1)

            def middle(b, j):
                n = 4 * b + j
                act.wait_ge(rest_ready, n + 1)
                act.activation(parts[:, j % 2, 1, :], rest[:], ACT.Copy).then_inc(mid_ready, 1)

            def values(b, par):
                act.wait_ge(v_done, b + 1)
                if isinstance(b, int) and b == 0:
                    act.wait_ge(vones, 4)
                if not (isinstance(b, int) and b < 2):
                    act.wait_ge(pv_done, 4 * QT * (b - 1))
                act.activation(Vx[par][:, :, :, 0:HD], psC[:].rearrange("p (q h d) -> p q h d", q=QT, h=HEADS),
                               ACT.Copy).then_inc(v_ready, 1)

            def first():
                take(0)
                tokens(0)
                features(0)
                for j in range(4):
                    split(0, j)
                    middle(0, j)
                values(0, 0)

            def step(t, g, par):
                xn_, xb, xg, xf = at(t, g, 2)
                pn, pb, pg, pf = at(t, g, 3)
                for u in range(UNITS):
                    if has(t, g, "X"):
                        e = UNITS * xn_ + u
                        c = u // 4
                        act.wait_ge(smm_done, e + 1)
                        if u % 4 == 0:
                            k = 4 * xn_ + c
                            if not (isinstance(k, int) and k < 2):
                                act.wait_ge(pv_done, k - 1)
                        act.activation(ex[:, 4 * (c % 2) + u % 4, :], ps_e[u % 2][:], ACT.Exp,
                                       scale=float(HD) ** -0.5).then_inc(exp_done, 1)
                    if u == 4 and has(t, g, "Xprev"):
                        act.wait_ge(pv_done, 4 * pn + 4)
                        if not (isinstance(pn, int) and pn == 0):
                            act.wait_ge(o_turned, pn)
                        act.activation(OT[:], ps_o[:], ACT.Copy).then_inc(o_copied, 1)
                    b = t + 1
                    if has(t, g, "F"):
                        if (g, u) == (0, 0):
                            take(b)
                        if (g, u) == (0, 3):
                            tokens(b)
                        if (g, u) == (0, 15):
                            features(b)
                        for j, when in enumerate(((1, 1), (1, 9), (1, 14), (2, 5))):
                            if (g, u) == when:
                                split(b, j)
                        for j, when in enumerate(((1, 5), (1, 12), (2, 1), (2, 8))):
                            if (g, u) == when:
                                middle(b, j)
                        if (g, u) == (2, 10):
                            values(b, 1 - par)
                    b = t - 1
                    if has(t, g, "T"):
                        if (g, u) == (3, 10):
                            act.wait_ge(gn_ready, b + 1)
                            act.activation(xn[:], psC[:], ACT.Identity, scale=gsc[:], bias=gbi[:]
                                           ).then_inc(xn_ready, 1)
                        if (g, u) == (3, 15):
                            act.wait_ge(h2_ready, b + 1).then_inc(act_passed, 1)
                            act.activation(H2[:, b].rearrange("p q d -> p (q d)"), h2c[:].rearrange("p q d -> p (q d)"),
                                           ACT.Copy).then_inc(h2_kept, 1)
                    b = t - 2
                    if has(t, g, "R"):
                        if (g, u) == (0, 9):
                            act.wait_ge(z2_turned, b + 1)
                            act.activation(z2c[:], psC[:], ACT.Copy).then_inc(z2c_ready, 1)
                            act.wait_ge(z2c_ready, 2 * b + 1)
                            act.activation(Z2[:, b], z2c[:], ACT.Copy).then_inc(z2c_ready, 1)
                        if (g, u) == (0, 13):
                            act.wait_ge(shifted_ready, b + 1)
                            act.activation(prob[:, :, 0:E], logit[:], ACT.Exp).then_inc(prob_exp, 1)

            run(act, step, first)
            act.wait_ge(pv_done, 4 * QT * B)
            for b in range(B):
                act.wait_ge(sh_mm, b + 1)
                if b >= 2:
                    act.wait_ge(sh_hid, b - 1)
                act.activation(act_g[:, b % 2, :], (ps_m, ps_e)[b % 2][0][:], ACT.Silu).then_inc(sh_gated, 1)

        @block.gpsimd
        def _(pool):
            pool.memset(half[:], -0.5).then_inc(consts_ready, 1)
            pool.memset(ones[:], 1.0).then_inc(consts_ready, 1)
            pool.memset(Macc[:], 0.0).then_inc(consts_ready, 1)
            pool.memset(prob[:, :, E:E + 2], -1.0).then_inc(consts_ready, 1)
            pool.wait_ge(consts_in, consts_count).then_inc(pool_passed, 1)
            pool.tensor_copy(tri[:], tri_f[:]).then_inc(consts_ready, 1)
            pool.wait_ge(consts_ready, 5).then_inc(pool_passed, 1)

            def rstd_of(src, tmp, out, wait, n, count, eps_sem, done, width):
                pool.wait_ge(wait, count).then_inc(pool_passed, 1)
                pool.tensor_scalar(tmp, src, 1e-5, None, ALU.add).then_inc(eps_sem, 1)
                pool.wait_ge(eps_sem, n + 1).then_inc(pool_passed, 1)
                pool.tensor_tensor(out, tmp, half[:, 0:width], ALU.pow).then_inc(done, 1)

            def norm(b):
                rstd_of(fmv[:, :, 1], fve[:], frstd[:], f_var, b, b + 1, f_eps, f_rstd, QT)
                pool.wait_ge(f_rstd, b + 1).then_inc(pool_passed, 1)
                if not (isinstance(b, int) and b == 0):
                    pool.wait_ge(z_turned, b).then_inc(pool_passed, 1)
                for q in range(QT):
                    last = pool.tensor_scalar(ztok[:, q, :], htok[:, q, :], fmv[:, q, 0:1], frstd[:, q:q + 1],
                                              ALU.subtract, ALU.mult)
                last.then_inc(ztok_ready, 1)
                pool.tensor_tensor(H2[:, b], htok[:], outb[:].unsqueeze(1).to_broadcast([P, QT, D]), ALU.add
                                   ).then_inc(resid_ready, 1)

            def take_rest(b, j):
                pool.wait_ge(hi_ready, 4 * b + j + 1).then_inc(pool_passed, 1)
                pool.wait_ge(parts_ready, 4 * b + j).then_inc(pool_passed, 1)
                pool.tensor_tensor(rest[:], q32[:], parts[:, j % 2, 0, :], ALU.subtract).then_inc(rest_ready, 1)

            def low(b, j):
                pool.wait_ge(mid_ready, 4 * b + j + 1).then_inc(pool_passed, 1)
                pool.tensor_tensor(parts[:, j % 2, 2, :], rest[:], parts[:, j % 2, 1, :], ALU.subtract
                                   ).then_inc(parts_ready, 1)

            def first():
                norm(0)
                for p in range(2):
                    pool.memset(Vx[p][:, :, :, HD:32], 0.0).then_inc(vones, 1)
                pool.wait_ge(vones, 2)
                for p in range(2):
                    pool.memset(Vx[p][:, :, :, HD:HD + 1], 1.0).then_inc(vones, 1)
                for j in range(4):
                    low(0, j)

            def keep_picks(b):
                pool.wait_ge(slots_ready, b + 1).then_inc(pool_passed, 1)
                pool.tensor_tensor(picks[:, b, :, 1, :], gate[:], Mv[:], ALU.mult)
                pool.tensor_copy(picks[:, b, :, 0, :], slot1[:])
                pool.tensor_copy(picked[:, b], v8[:]).then_inc(picks_kept, 1)

            def scatter(b, par, lo, hi):
                if lo == 0:
                    pool.wait_ge(slots_ready, b + 1).then_inc(pool_passed, 1)
                for i in range(lo, hi):
                    q, k = i // TOPK, i % TOPK
                    pool.indirect_dma_start(dram["rows_x"], bass.IndirectOffsetOnAxis(ap=sidx[:, q, k:k + 1], axis=0),
                                            R[par][:, q, :], None, bounds_check=E * CAP - 1, oob_is_err=False
                                            ).then_inc(scattered, 16)

            def step(t, g, par):
                F, T, routed, earlier = has(t, g, "F"), has(t, g, "T"), has(t, g, "R"), has(t - 1, g, "R")
                if g == 0:
                    if F:
                        norm(t + 1)
                    if earlier:
                        scatter(t - 3, 1 - par, 12 if isinstance(t, int) and t == B + 1 else 19, 24)
                if g == 1:
                    if earlier:
                        pool.wait_ge(scattered, 16 * QT * TOPK * (t - 2)).then_inc(pool_passed, 1)
                        pool.memset(freed[:], 0.0).then_inc(rows_free, 1)
                    if F:
                        take_rest(t + 1, 0)
                        low(t + 1, 0)
                        take_rest(t + 1, 1)
                        low(t + 1, 1)
                        take_rest(t + 1, 2)
                cuts = (0, 4, 10, 15, 19)
                if isinstance(t, int) and t == B:
                    cuts = (0, 2, 4, 8, 12)
                if g == 2:
                    if F:
                        low(t + 1, 2)
                    if routed:
                        scatter(t - 2, par, *cuts[0:2])
                    if F:
                        take_rest(t + 1, 3)
                        low(t + 1, 3)
                    if routed:
                        scatter(t - 2, par, *cuts[1:3])
                if g == 3:
                    b = t - 1
                    if routed:
                        scatter(t - 2, par, *cuts[2:4])
                    if T:
                        rstd_of(gvar[:], gve[:], grs[:], gn_var_out, b, b + 1, gn_eps, gn_rstd, 1)
                    if routed:
                        scatter(t - 2, par, *cuts[3:5])
                    if T:
                        rstd_of(tmv[:, :, 1], tve[:], trstd[:], t_var, b, b + 1, t_eps, t_rstd, QT)
                        pool.wait_ge(t_rstd, b + 1).then_inc(pool_passed, 1)
                        if not (isinstance(t, int) and t == B):
                            for q in range(QT):
                                last = pool.tensor_scalar(R[1 - par][:, q, :], h2c[:, q, :], tmv[:, q, 0:1],
                                                          trstd[:, q:q + 1], ALU.subtract, ALU.mult)
                            last.then_inc(z2_ready, 1)
                    if routed and not (isinstance(t, int) and t == B + 1):
                        keep_picks(t - 2)

            run(pool, step, first)
            scatter(B - 1, (B - 1) % 2, 19, 24)
            keep_picks(B - 1)
            pool.wait_ge(scattered, 16 * QT * TOPK * B)

        @block.vector
        def _(dve):
            dve.wait_ge(consts_in, consts_count)
            dve.tensor_tensor(lam[:, 1, :], lam[:, 0, :], lam[:, 1, :], ALU.mult)
            dve.tensor_tensor(lam[:, 3, :], lam[:, 2, :], lam[:, 3, :], ALU.mult).then_inc(lam_ready, 1)
            dve.wait_ge(lam_ready, 3)
            dve.tensor_tensor(neglam[:], lam[:, 2, :], lam[:, 0, :], ALU.subtract).then_inc(lam_ready, 1)
            dve.wait_ge(lam_ready, 4)
            dve.tensor_scalar(neglam[:], neglam[:], -0.2, None, ALU.add).then_inc(lam_ready, 1)
            dve.wait_ge(lam_ready, 5)
            dve.wait_ge(consts_ready, 5)
            dve.memset(M[:], 0.0).then_inc(rows_free, 2)
            dve.wait_ge(rows_free, 2)

            def stats(b):
                dve.wait_ge(htok_ready, b + 1)
                for q in range(QT):
                    last = dve.bn_stats(fstats[:, q, :], htok[:, q, :])
                last.then_inc(f_stats, 1)
                dve.wait_ge(f_stats, b + 1).then_inc(dve_passed, 1)
                for q in range(QT):
                    last = dve.bn_aggr(fmv[:, q, :], fstats[:, q, :])
                last.then_inc(f_var, 1)

            def take_rest(b, j):
                n = 4 * b + j
                dve.wait_ge(hi_ready, n + 1)
                if not (isinstance(n, int) and n == 0):
                    dve.wait_ge(parts_ready, n)
                dve.tensor_tensor(rest[:], q32[:], parts[:, j % 2, 0, :], ALU.subtract).then_inc(rest_ready, 1)

            def first():
                stats(0)
                for j in range(4):
                    take_rest(0, j)

            def split_rows(n):
                dve.wait_ge(nm_turned, n + 1)
                if not (isinstance(n, int) and n == 0):
                    dve.wait_ge(rows_stored, 16 * n)
                src = psB[0:UNITS, 0:P]
                dve.tensor_copy(mp[:, 0, :], src).then_inc(mp_chain, 1)
                dve.wait_ge(mp_chain, 3 * n + 1)
                dve.tensor_tensor(mrest[:], src, mp[:, 0, :], ALU.subtract).then_inc(mp_chain, 1)
                dve.wait_ge(mp_chain, 3 * n + 2)
                dve.tensor_copy(mp[:, 1, :], mrest[:]).then_inc(mp_chain, 1)
                dve.wait_ge(mp_chain, 3 * n + 3)
                dve.tensor_tensor(mp[:, 2, :], mrest[:], mp[:, 1, :], ALU.subtract).then_inc(rows_ready, 1)

            def output(n, gg):
                dve.wait_ge(o_turned, n + 1)
                o = psB[:].rearrange("p (q j c) -> p q j c", q=QT, j=4)
                dve.reciprocal(rsum[:], o[:, :, :, HD]).then_inc(o_chain, 1)
                dve.wait_ge(o_chain, 3 * n + 1)
                dve.tensor_tensor(rsum[:, :, 2:4], rsum[:, :, 2:4],
                                  neglam[:, 2 * gg:2 * gg + 2].unsqueeze(1).to_broadcast([P, QT, 2]), ALU.mult
                                  ).then_inc(o_chain, 1)
                dve.wait_ge(o_chain, 3 * n + 2)
                dve.tensor_tensor(on[:], o[:, :, :, 0:HD], rsum[:].unsqueeze(3).to_broadcast([P, QT, 4, HD]),
                                  ALU.mult).then_inc(o_chain, 1)
                dve.wait_ge(o_chain, 3 * n + 3)
                dve.tensor_tensor(otok[:, :, 2 * gg:2 * gg + 2, :], on[:, :, 0:2, :], on[:, :, 2:4, :], ALU.add
                                  ).then_inc(o_norm, 1)

            def step(t, g, par):
                pn, pb, pg, pf = at(t, g, 3)
                mn = at(t, g, 1)[0]
                for u in range(UNITS):
                    if has(t, g, "M"):
                        m = 4 * UNITS * t + UNITS * g + u
                        dve.wait_ge(mxmm_done, m + 1)
                        if u == 0 and not (isinstance(t, int) and 4 * t + g < 2):
                            dve.wait_ge(nm_turned, mn)
                        dve.tensor_reduce(nm[:, g % 2, u:u + 1], ps_m[M_BANK[u]][:], AX.X, ALU.max, negate=True
                                          ).then_inc(max_ready, 1)
                    if u == 3 and has(t, g, "Mprev"):
                        split_rows(mn)
                    if u == 10 and has(t, g, "Xprev"):
                        if pg == 0 and not (isinstance(t, int) and pb == 0):
                            dve.wait_ge(t_turned, pb)
                        output(pn, pg)
                    b = t + 1
                    if has(t, g, "F"):
                        if (g, u) == (0, 5):
                            stats(b)
                    b = t - 1
                    if has(t, g, "T"):
                        if (g, u) == (2, 15):
                            dve.wait_ge(t_turned, b + 1)
                            dve.bn_stats(gst[:], psC[:]).then_inc(gn_chain, 1)
                            dve.wait_ge(gn_chain, 4 * b + 1).then_inc(dve_passed, 1)
                            dve.bn_aggr(gmv[:], gst[:]).then_inc(gn_chain, 1)
                        if (g, u) == (3, 1):
                            dve.wait_ge(gn_mean_done, b + 1)
                            dve.tensor_copy(gm[:], psB[:, 0:1])
                            dve.tensor_tensor(gd[:], gmv[:, 0:1], psB[:, 0:1], ALU.subtract).then_inc(gn_chain, 1)
                            dve.wait_ge(gn_chain, 4 * b + 3)
                            dve.scalar_tensor_tensor(out=gv[:], in0=gd[:], scalar=gd[:], in1=gmv[:, 1:2],
                                                     op0=ALU.mult, op1=ALU.add).then_inc(gn_chain, 1)
                        if (g, u) == (3, 7):
                            dve.wait_ge(gn_var_done, b + 1)
                            dve.tensor_copy(gvar[:], psB[:, 0:1]).then_inc(gn_var_out, 1)
                        if (g, u) == (3, 9):
                            dve.wait_ge(gn_rstd, b + 1)
                            dve.tensor_tensor(gsc[:], grs[:], gnw[:, 0:1], ALU.mult).then_inc(t_chain, 1)
                            dve.wait_ge(t_chain, 3 * b + 1)
                            dve.tensor_tensor(gbi[:], gm[:], gsc[:], ALU.mult).then_inc(t_chain, 1)
                            dve.wait_ge(t_chain, 3 * b + 2)
                            dve.tensor_tensor(gbi[:], gnw[:, 1:2], gbi[:], ALU.subtract).then_inc(gn_ready, 1)
                        if (g, u) == (3, 14):
                            dve.wait_ge(y_done, b + 1)
                            dve.wait_ge(resid_ready, b + 1)
                            if not (isinstance(b, int) and b == 0):
                                dve.wait_ge(h2_kept, b)
                                dve.wait_ge(z2_ready, b)
                            dve.tensor_tensor(h2c[:], psC[:].rearrange("p (q d) -> p q d", q=QT), H2[:, b], ALU.add
                                              ).then_inc(h2_ready, 1)
                            dve.wait_ge(h2_ready, b + 1)
                            for q in range(QT):
                                last = dve.bn_stats(tstats[:, q, :], h2c[:, q, :])
                            last.then_inc(t_chain, 1)
                            dve.wait_ge(t_chain, 3 * b + 3).then_inc(dve_passed, 1)
                            for q in range(QT):
                                last = dve.bn_aggr(tmv[:, q, :], tstats[:, q, :])
                            last.then_inc(t_var, 1)
                            if isinstance(t, int) and t == B:
                                dve.wait_ge(t_rstd, B)
                                dve.wait_ge(rows_free, B)
                                for q in range(QT):
                                    last = dve.tensor_scalar(R[1 - par][:, q, :], h2c[:, q, :], tmv[:, q, 0:1],
                                                             trstd[:, q:q + 1], ALU.subtract, ALU.mult)
                                last.then_inc(z2_ready, 1)
                    b = t - 2
                    if has(t, g, "R"):
                        if (g, u) == (0, 2):
                            dve.tensor_reduce(mnew[:], M[:].rearrange("p q e -> p e q"), AX.X, ALU.add
                                              ).then_inc(t_chain2, 1)
                            dve.wait_ge(t_chain2, b + 1)
                            dve.tensor_tensor(Macc[:], Macc[:], mnew[:], ALU.add).then_inc(macc_ready, 1)
                        if (g, u) == (0, 11):
                            dve.wait_ge(logit_done, b + 1)
                            dve.tensor_tensor(logit[:], psC[:, 0:QT * E].rearrange("p (q e) -> p q e", q=QT),
                                              rbias[:].unsqueeze(1).to_broadcast([P, QT, E]), ALU.add
                                              ).then_inc(r_chain, 1)
                            dve.wait_ge(r_chain, NR * b + 1)
                            dve.tensor_reduce(lmax[:], logit[:], AX.X, ALU.max).then_inc(r_chain, 1)
                            dve.wait_ge(r_chain, NR * b + 2)
                            dve.tensor_tensor(logit[:], logit[:], lmax[:].unsqueeze(2).to_broadcast([P, QT, E]),
                                              ALU.subtract).then_inc(shifted_ready, 1)
                        if (g, u) == (0, 15):
                            dve.wait_ge(prob_exp, b + 1)
                            pr = prob[:, :, 0:E]
                            dve.tensor_reduce(lsum[:], pr, AX.X, ALU.add).then_inc(r_chain, 1)
                            dve.wait_ge(r_chain, NR * b + 3)
                            dve.reciprocal(lrec[:], lsum[:]).then_inc(r_chain, 1)
                            dve.wait_ge(r_chain, NR * b + 4)
                            dve.tensor_tensor(pr, pr, lrec[:].unsqueeze(2).to_broadcast([P, QT, E]), ALU.mult
                                              ).then_inc(r_chain, 1)
                            dve.wait_ge(r_chain, NR * b + 5).then_inc(dve_passed, 1)
                            for q in range(QT):
                                last = dve.max(top[:, q, :], prob[:, q, 0:E])
                            last.then_inc(r_chain, 1)
                            dve.wait_ge(r_chain, NR * b + 6)
                            dve.tensor_reduce(gsum[:], top[:, :, 0:TOPK], AX.X, ALU.add)
                            dve.memset(top[:, :, TOPK:8], -1.0).then_inc(r_chain, 1)
                            dve.wait_ge(r_chain, NR * b + 7).then_inc(dve_passed, 1)
                            for q in range(QT):
                                last = dve.match_replace(repl[:, q, :], top[:, q, :], prob[:, q, :], -2.0)
                            last.then_inc(r_chain, 1)
                            dve.wait_ge(r_chain, NR * b + 8)
                            dve.tensor_tensor(M[:], repl[:, :, 0:E], pr, ALU.not_equal).then_inc(mask_ready, 1)
                        if (g, u) == (1, 1):
                            dve.tensor_scalar(gsum[:], gsum[:], 1e-9, None, ALU.add).then_inc(r_chain, 1)
                            dve.wait_ge(r_chain, NR * b + 9)
                            dve.reciprocal(grec[:], gsum[:]).then_inc(r_chain, 1)
                            dve.wait_ge(r_chain, NR * b + 10)
                            if not (isinstance(b, int) and b == 0):
                                dve.wait_ge(picks_kept, b)
                            dve.tensor_tensor(gate[:], prob[:, :, 0:E],
                                              grec[:].unsqueeze(2).to_broadcast([P, QT, E]), ALU.mult
                                              ).then_inc(r_chain, 1)
                            dve.wait_ge(r_chain, NR * b + 11)
                        if (g, u) == (1, 6):
                            dve.wait_ge(rank_done, b + 1)
                            rank = psC[:, 0:QT * E].rearrange("p (q e) -> p q e", q=QT)
                            dve.scalar_tensor_tensor(out=Mv[:], in0=rank, scalar=float(CAP), in1=M[:],
                                                     op0=ALU.is_lt, op1=ALU.mult)
                            dve.tensor_tensor(slot1[:], rank, base1[:].unsqueeze(1).to_broadcast([P, QT, E]),
                                              ALU.add).then_inc(rows_out, 1)
                            dve.wait_ge(rows_out, b + 1)
                            dve.tensor_tensor(slot1[:], slot1[:], Mv[:], ALU.mult).then_inc(r_chain, 1)
                            dve.wait_ge(r_chain, NR * b + 12).then_inc(dve_passed, 1)
                            for q in range(QT):
                                last = dve.max(v8[:, q, :], slot1[:, q, :])
                            last.then_inc(r_chain, 1)
                            dve.wait_ge(r_chain, NR * b + 13)
                            dve.tensor_scalar(none[:], v8[:], 0.0, FAR, ALU.is_equal, ALU.mult).then_inc(r_chain, 1)
                            dve.wait_ge(r_chain, NR * b + 14)
                            dve.wait_ge(rows_free, b + 2)
                            dve.scalar_tensor_tensor(out=sidx[:], in0=v8[:], scalar=-1.0, in1=none[:],
                                                     op0=ALU.add, op1=ALU.add).then_inc(slots_ready, 1)

            run(dve, step, first)

            def shared_hidden(b):
                dve.wait_ge(sh_gated, b + 1)
                if b >= 2:
                    dve.wait_ge(sh_down, b - 1)
                dve.tensor_tensor(hid[:, b % 2, :], (ps_m, ps_e)[b % 2][1][:], act_g[:, b % 2, :], ALU.mult
                                  ).then_inc(sh_hid, 1)

            def shared_add(b):
                dve.wait_ge(sh_down, b + 1)
                dve.scalar_tensor_tensor(out=H2[:, b].rearrange("p q d -> p (q d)"), in0=(psC, psB)[b % 2][:],
                                         scalar=1.0 / 2, in1=H2[:, b].rearrange("p q d -> p (q d)"),
                                         op0=ALU.mult, op1=ALU.add).then_inc(sh_added, 1)

            shared_hidden(0)
            dve.wait_ge(h2_kept, B)
            for b in range(1, B):
                shared_hidden(b)
                shared_add(b - 1)
            shared_add(B - 1)
PAIRS = E // 2
TILES = CAP // P
HALF = TILES // 2
COLS = HALF * P
AHEAD = 4


def experts(nc, io, H2, picks, picked, dram, ident, out, passed):
    with ExitStack() as ctx:
        def sb(name, shape, dt=F32):
            return ctx.enter_context(nc.sbuf_tensor(name, shape, dt))

        def sem(name):
            return ctx.enter_context(nc.semaphore(name))

        rows = [sb(f"rows{i}", [P, 2, TILES, D]) for i in range(AHEAD)]
        wgu = [sb(f"wgu{i}", [P, 2, 2, FF]) for i in range(AHEAD)]
        wdn = [sb(f"wdn{i}", [P, D]) for i in range(AHEAD)]
        xT = sb("xT3", [P, 2, 2, COLS])
        act_g = sb("act_g", [P, 2, S])
        hid = sb("hid", [P, 2, S])
        yt = [sb(f"yt{i}", [P, 2, TILES, D]) for i in range(AHEAD)]
        zero = sb("zero3", [1, D])
        NG = 4
        got = [sb(f"got{i}", [P, TOPK, D]) for i in range(NG)]
        idx = [sb(f"idx{i}", [P, 8], I32) for i in range(NG)]
        same = sb("same", [P, TOPK, E])
        taken = sb("taken", [P, TOPK, E])
        share = sb("share", [P, B * QT, TOPK])
        gated_rows = sb("gated_rows", [P, TOPK, D])
        total = [sb(f"total{i}", [P, D]) for i in range(NG)]
        res = [sb(f"res{i}", [P, D]) for i in range(NG)]

        ps_x = [ctx.enter_context(nc.psum_tensor(f"px{i}", [P, S], F32)) for i in range(2)]
        ps_g = [ctx.enter_context(nc.psum_tensor(f"pg{i}", [P, S], F32)) for i in range(2)]
        ps_u = [ctx.enter_context(nc.psum_tensor(f"pu{i}", [P, S], F32)) for i in range(2)]
        ps_y = [ctx.enter_context(nc.psum_tensor(f"py{i}", [P, S], F32)) for i in range(2)]

        (zero3_ready, zero3_written, x_turned, x_out,
         gu_done, gated, hid_ready, down_done, y_ready) = [sem(n) for n in (
             "zero3_ready", "zero3_written", "x_turned", "x_out", "gu_done", "gated", "hid_ready", "down_done", "y_ready")]
        rows_in = [sem(f"rows_in{i}") for i in range(AHEAD)]
        y_written = [sem(f"y_written{i}") for i in range(AHEAD)]
        share_chain = sem("share_chain")
        weighed = sem("weighed")
        idx_ready = sem("idx_ready")
        gathered = [sem(f"gathered{i}") for i in range(NG)]
        summed = sem("summed")
        res_ready = sem("res_ready")
        stored = [sem(f"res_stored{i}") for i in range(NG)]

        LOADS = 16 * 3
        UB = 2 * AHEAD
        sp_passed, pool_passed, _, dve_passed = passed
        block = ctx.enter_context(nc.Block())

        @block.sync
        def _(sp):
            def load_rows(p, par):
                sp.dma_start(rows[par][:], dram["rows_x"].rearrange("(e p n) c -> p e n c", e=E, n=TILES)[
                    :, bass.ds(p * 2, 2)]).then_inc(rows_in[par], 16)

            def load_weights(p, par):
                sp.dma_start(wgu[par][:].rearrange("p a b f -> p (a b f)"), io["experts_gu"][p]).then_inc(rows_in[par], 16)
                sp.dma_start(wdn[par][:], io["experts_down"][p]).then_inc(rows_in[par], 16)

            for p in range(AHEAD):
                load_rows(p, p)
                load_weights(p, p)
            sp.wait_ge(zero3_ready, 1)
            sp.dma_start(dram["rows_y"][0:1, :], zero[:]).then_inc(zero3_written, 16)

            def following(p, par, more):
                if more:
                    sp.wait_ge(x_out, 4 * p + 4).then_inc(sp_passed, 1)
                    load_rows(p + AHEAD, par)
                    sp.wait_ge(down_done, 2 * p + 2).then_inc(sp_passed, 1)
                    load_weights(p + AHEAD, par)
                sp.wait_ge(y_ready, 4 * p + 4).then_inc(sp_passed, 1)
                sp.dma_start(dram["rows_y"][1:1 + E * CAP, :].rearrange("(e p n) c -> p e n c", e=E, n=TILES)[
                    :, bass.ds(p * 2, 2)], yt[par][:]).then_inc(y_written[par], 16)

            with sp.Fori(0, PAIRS // AHEAD - 1) as i:
                for n in range(AHEAD):
                    following(i * AHEAD + n, n, True)
            for n in range(AHEAD):
                following(PAIRS - AHEAD + n, n, False)

        @block.tensor
        def _(pe):
            def up(v, half, par):
                pe.wait_ge(x_out, 2 * v + 2)
                if not (isinstance(v, int) and v < 2):
                    pe.wait_ge(hid_ready, v - 1)
                for w, ps in enumerate((ps_g, ps_u)):
                    for j in range(2):
                        last = pe.matmul(ps[half][FF * j:FF * j + FF, 0:COLS], wgu[par][:, w, j, :],
                                         xT[:, half, j, :], start=True, stop=True)
                last.then_inc(gu_done, 1)

            def down(v, half, par):
                pe.wait_ge(hid_ready, v + 1)
                if not (isinstance(v, int) and v == 0):
                    pe.wait_ge(y_ready, 2 * v)
                for k in range(HALF):
                    for j in range(2):
                        last = pe.matmul(ps_y[j][:, k * P:(k + 1) * P],
                                         hid[FF * j:FF * j + FF, half, k * P:(k + 1) * P],
                                         wdn[par][FF * j:FF * j + FF, :], start=True, stop=True)
                last.then_inc(down_done, 1)

            def turn(i, n):
                v, half, par = UB * i + n, n % 2, (n // 2) % AHEAD
                if half == 0:
                    pe.wait_ge(rows_in[par], LOADS * (i + n // UB) + LOADS)
                for j in range(2):
                    m = 2 * v + j
                    if not (isinstance(m, int) and m < 2):
                        pe.wait_ge(x_out, m - 1)
                    for k in range(HALF):
                        last = pe.transpose(ps_x[j][:, k * P:(k + 1) * P],
                                            rows[par][:, j, half * HALF + k, :], ident[:])
                    last.then_inc(x_turned, 1)

            turn(0, 0)
            turn(0, 1)
            up(0, 0, 0)

            def body(i, last):
                for n in range(UB):
                    if n + 2 < UB or not last:
                        turn(i, n + 2)
                    if n + 1 < UB or not last:
                        up(UB * i + n + 1, (n + 1) % 2, ((n + 1) // 2) % AHEAD)
                    down(UB * i + n, n % 2, n // 2)

            with pe.Fori(0, PAIRS // AHEAD - 1) as i:
                body(i, False)
            body(PAIRS // AHEAD - 1, True)

        @block.scalar
        def _(act):
            def take(v, half):
                for j in range(2):
                    act.wait_ge(x_turned, 2 * v + j + 1)
                    if j == 0 and not (isinstance(v, int) and v < 2):
                        act.wait_ge(gu_done, v - 1)
                    act.activation(xT[:, half, j, :], ps_x[j][:, 0:COLS], ACT.Copy).then_inc(x_out, 1)

            def gate(v, half):
                act.wait_ge(gu_done, v + 1)
                if not (isinstance(v, int) and v < 2):
                    act.wait_ge(hid_ready, v - 1)
                act.activation(act_g[:, half, 0:COLS], ps_g[half][:, 0:COLS], ACT.Silu).then_inc(gated, 1)

            take(0, 0)
            take(1, 1)
            gate(0, 0)

            def body(i, last):
                for n in range(UB):
                    if n + 2 < UB or not last:
                        take(UB * i + n + 2, n % 2)
                    if n + 1 < UB or not last:
                        gate(UB * i + n + 1, (n + 1) % 2)

            with act.Fori(0, PAIRS // AHEAD - 1) as i:
                body(i, False)
            body(PAIRS // AHEAD - 1, True)

            def keep(i, n):
                act.wait_ge(res_ready, NG * i + n + 1)
                act.dma_start(out[i, n * P:(n + 1) * P, :], res[n][:]).then_inc(stored[n], 16)

            with act.Fori(0, B) as i:
                for n in range(NG):
                    keep(i, n)
            for n in range(NG):
                act.wait_ge(stored[n], 16 * B)

        @block.vector
        def _(dve):
            dve.memset(zero[:], 0.0).then_inc(zero3_ready, 1)

            def hidden(v, half):
                dve.wait_ge(gated, v + 1)
                if not (isinstance(v, int) and v < 2):
                    dve.wait_ge(down_done, v - 1)
                dve.tensor_tensor(hid[:, half, 0:COLS], ps_u[half][:, 0:COLS], act_g[:, half, 0:COLS],
                                  ALU.mult).then_inc(hid_ready, 1)

            def leave(i, n):
                v, half, par = UB * i + n, n % 2, n // 2
                dve.wait_ge(down_done, v + 1)
                if half == 0 and not (isinstance(i, int) and i == 0):
                    dve.wait_ge(y_written[par], 16 * i)
                for j in range(2):
                    dve.tensor_copy(yt[par][:, j, half * HALF:(half + 1) * HALF, :],
                                    ps_y[j][:, 0:COLS].rearrange("p (n d) -> p n d", n=HALF)).then_inc(y_ready, 1)

            flat = picks[:].rearrange("p b q a e -> p (b q) a e")
            largest = picked[:].rearrange("p b q k -> p (b q) k")

            def shares(tile):
                if not (isinstance(tile, int) and tile == 0):
                    dve.wait_ge(share_chain, 3 * tile).then_inc(dve_passed, 1)
                dve.tensor_tensor(same[:], flat[:, tile, 0, :].unsqueeze(1).to_broadcast([P, TOPK, E]),
                                  largest[:, tile, 0:TOPK].unsqueeze(2).to_broadcast([P, TOPK, E]), ALU.is_equal
                                  ).then_inc(share_chain, 1)
                dve.wait_ge(share_chain, 3 * tile + 1)
                dve.tensor_tensor(taken[:], same[:], flat[:, tile, 1, :].unsqueeze(1).to_broadcast([P, TOPK, E]),
                                  ALU.mult).then_inc(share_chain, 1)
                dve.wait_ge(share_chain, 3 * tile + 2)
                dve.tensor_reduce(share[:, tile, :], taken[:], AX.X, ALU.add).then_inc(share_chain, 1)

            hidden(0, 0)

            def body(i, last):
                for n in range(UB):
                    if n + 1 < UB or not last:
                        hidden(UB * i + n + 1, (n + 1) % 2)
                    leave(i, n)
                    if n % 2:
                        shares(AHEAD * i + n // 2)

            body(0, False)
            with dve.Fori(1, PAIRS // AHEAD - 1) as i:
                body(i, False)
            body(PAIRS // AHEAD - 1, True)
            dve.wait_ge(share_chain, 3 * B * QT)

            def indices(i, n):
                if not (isinstance(i, int) and i == 0):
                    dve.wait_ge(gathered[n], 16 * TOPK * i)
                dve.tensor_copy(idx[n][:], picked[:, i, n]).then_inc(idx_ready, 1)

            def combine(i, n):
                m = NG * i + n
                dve.wait_ge(gathered[n], 16 * TOPK * (i + 1))
                if not (isinstance(m, int) and m == 0):
                    dve.wait_ge(summed, m).then_inc(dve_passed, 1)
                dve.tensor_tensor(gated_rows[:], got[n][:],
                                  share[:, m, :].unsqueeze(2).to_broadcast([P, TOPK, D]), ALU.mult).then_inc(weighed, 1)
                dve.wait_ge(weighed, m + 1)
                dve.tensor_reduce(total[n][:], gated_rows[:].rearrange("p k d -> p d k"), AX.X, ALU.add
                                  ).then_inc(summed, 1)
                dve.wait_ge(summed, m + 1)
                if not (isinstance(i, int) and i == 0):
                    dve.wait_ge(stored[n], 16 * i)
                dve.tensor_tensor(res[n][:], total[n][:], H2[:, i, n, :], ALU.add).then_inc(res_ready, 1)

            for n in range(NG):
                indices(0, n)
            for n in range(NG):
                combine(0, n)
                indices(1, n)
            with dve.Fori(1, B - 1) as i:
                for n in range(NG):
                    combine(i, n)
                    indices(i + 1, n)
            for n in range(NG):
                combine(B - 1, n)

        @block.gpsimd
        def _(pool):
            pool.wait_ge(zero3_written, 16)
            for par in range(AHEAD):
                pool.wait_ge(y_written[par], 16 * (PAIRS // AHEAD))

            def gather(i, n):
                pool.wait_ge(idx_ready, NG * i + n + 1).then_inc(pool_passed, 1)
                if not (isinstance(i, int) and i == 0):
                    pool.wait_ge(weighed, NG * (i - 1) + n + 1).then_inc(pool_passed, 1)
                for k in range(TOPK):
                    pool.indirect_dma_start(got[n][:, k, :], None, dram["rows_y"],
                                            bass.IndirectOffsetOnAxis(ap=idx[n][:, k:k + 1], axis=0)
                                            ).then_inc(gathered[n], 16)

            for n in range(NG):
                gather(0, n)
            with pool.Fori(1, B) as i:
                for n in range(NG):
                    gather(i, n)


def build(nc, io, out):
    dram = {
        "parts": nc.dram_tensor("parts_scratch", [4, 3, P, S], BF16, kind="Internal").ap(),
        "rows": nc.dram_tensor("maxima_scratch", [3, UNITS, P], BF16, kind="Internal").ap(),
        "rows_x": nc.dram_tensor("dispatched", [E * CAP, D], F32, kind="Internal").ap(),
        "rows_y": nc.dram_tensor("expert_out", [1 + E * CAP, D], F32, kind="Internal").ap(),
    }
    with ExitStack() as ctx:
        H2 = ctx.enter_context(nc.sbuf_tensor("H2", [P, B, QT, D], F32))
        Z2 = ctx.enter_context(nc.sbuf_tensor("Z2", [P, B, S], F32))
        picks = ctx.enter_context(nc.sbuf_tensor("picks", [P, B, QT, 2, E], F32))
        picked = ctx.enter_context(nc.sbuf_tensor("picked", [P, B, QT, 8], F32))
        passed = [ctx.enter_context(nc.semaphore(n + "_passed")) for n in ("sp", "pool", "act", "dve")]
        consts = attention_constants(nc, ctx)
        consts_in = ctx.enter_context(nc.semaphore("attention_consts_in"))
        with nc.sbuf_tensor("X", [P, B, S + 2], F32) as X:
            tower(nc, io, X, dram["rows_x"], constant_loads(consts, io), consts_in, passed)
            attention(nc, io, X, H2, Z2, picks, picked, dram, consts, consts_in, passed)
        experts(nc, io, H2, picks, picked, dram, consts[0], out, passed)


def host_constants():
    f = np.float32
    place = np.arange(S - 1, -1, -1, dtype=f)
    freq = (f(1) / f(10000.0) ** (np.arange(0, D, 2, dtype=f) / f(D))).astype(f)
    angle = place[:, None] * freq[None, :]
    i = np.arange(P)
    return {
        "pe": np.concatenate([np.sin(angle), np.cos(angle)], -1).astype(f),
        "ident": np.eye(P, dtype=f),
        "iota": np.arange(P, dtype=f).reshape(P, 1),
        "grp": (i[:, None] // 32 == i[None] // 32).astype(f) / f(32),
        "tri": (i[:, None] < i[None]).astype(f),
        "base1": (np.arange(E) * CAP + 1).astype(f),
    }


def laid_out(inputs):
    a = {k: np.asarray(v) for k, v in inputs.items()}
    out = {k: a[k] for k in ("x", "L0_tok_emb", "L0_tok_ln0_g", "L0_tok_ln0_b", "L0_tok_W1", "L0_tok_W2",
                             "L0_attn_lambda_q1", "L0_attn_lambda_k1", "L0_attn_lambda_q2", "L0_attn_lambda_k2",
                             "L0_attn_gn_w", "L0_attn_gn_b", "L0_attn_out_b", "L0_ffn_bias")}
    for k in ("L0_tok_g1", "L0_tok_b1", "L0_tok_g2", "L0_tok_b2", "L0_attn_V_w", "L0_attn_out_w",
              "L0_ffn_router_w"):
        out[k] = a[k].T
    order = np.arange(D).reshape(HEADS, HD).T.reshape(-1)
    for k in ("Q1", "K1", "Q2", "K2"):
        out[f"L0_attn_{k}_w"] = a[f"L0_attn_{k}_w"][order].T
    for k in ("K1", "K2"):
        out[f"L0_attn_{k}_b"] = a[f"L0_attn_{k}_b"][order]
    gu = np.stack([a["L0_ffn_w_gate"], a["L0_ffn_w_up"]], 0).reshape(2, PAIRS, 2, FF, D)
    out["experts_gu"] = gu.transpose(1, 4, 0, 2, 3).reshape(PAIRS, D, 4 * FF)
    out["experts_down"] = a["L0_ffn_w_down"].transpose(0, 2, 1).reshape(PAIRS, 2 * FF, D)
    sh = np.stack([a["L0_ffn_shared_w_gate"], a["L0_ffn_shared_w_up"]], 0).reshape(2, 2 * FF, D)
    out["shared_gu"] = sh.transpose(2, 0, 1)
    out["shared_down"] = a["L0_ffn_shared_w_down"].transpose(0, 2, 1).reshape(2 * FF, D)
    out.update(host_constants())
    return {k: np.ascontiguousarray(v) for k, v in out.items()}


def kernel(**inputs):
    from concourse import bacc
    from concourse.bass_utils import run_bass_kernel_spmd

    nc = bacc.Bacc("TRN2", target_bir_lowering=False, num_devices=1)
    arrays, io = {}, {}
    for name, a in laid_out(inputs).items():
        arrays["in_" + name] = a
        io[name] = nc.dram_tensor("in_" + name, a.shape, mybir.dt.from_np(a.dtype), kind="ExternalInput").ap()
    out = nc.dram_tensor("out_0", [B, S, D], F32, kind="ExternalOutput").ap()
    build(nc, io, out)
    r = run_bass_kernel_spmd(nc, [arrays], core_ids=[0])
    return r.results[0]["out_0"]
```
